# Optimizing a Trainium2 kernel written in Bass

```python
import numpy as np
import jax
import jax.numpy as jnp

def _softmax(x, axis=-1):
    return jax.nn.softmax(x, axis=axis)

def _gelu(x):
    return jax.nn.gelu(x, approximate=True)

def _silu(x):
    return jax.nn.silu(x)

def _sigmoid(x):
    return jax.nn.sigmoid(x)

def _layernorm(x, axis=-1, eps=1e-05):
    m = jnp.mean(x, axis=axis, keepdims=True)
    v = jnp.var(x, axis=axis, keepdims=True)
    return (x - m) / jnp.sqrt(v + eps)

def _scatter_add(tgt, idx, src, axis=0):
    return tgt.at[idx].add(src)

def _segment_sum(src, seg, n):
    return jax.ops.segment_sum(src, seg, n)
kernel_name = 'mk_decoder_preln_d1_seqx_r4_9a8624'

def setup_inputs(seed: int=0):
    np.random.seed(seed)
    _w = jnp.asarray

    def _rec_inputs():
        import jax
        import jax.numpy as jnp
        _rk = jax.random.key(seed)
        x = -0.0002928 + 1 * jax.random.normal(jax.random.fold_in(_rk, 1), (8, 512, 256), jnp.float32)
        _lenS = 512 - jax.random.randint(jax.random.fold_in(_rk, 7), (8,), 0, max(1, 512 // 4) + 1, jnp.int32)
        _lenS2 = 64 - jax.random.randint(jax.random.fold_in(_rk, 8), (8,), 0, max(1, 64 // 4) + 1, jnp.int32)
        _ctx_1024P = jax.random.normal(jax.random.fold_in(_rk, 11), (8, 16, 256), jnp.float32)
        _ctx_1024c = jax.random.dirichlet(jax.random.fold_in(_rk, 511), 0.3 * jnp.ones((16,), jnp.float32), (8, 64))
        _ctx_1024t = jnp.einsum('bsk,bkd->bsd', _ctx_1024c, _ctx_1024P)
        _ctx_1024t = _ctx_1024t * jax.lax.rsqrt(jnp.mean(jnp.square(_ctx_1024t)) + 1e-12) * 0.953939
        ctx_1024 = 4.13588e-05 + 0.999923 * (_ctx_1024t + 0.3 * jax.random.normal(jax.random.fold_in(_rk, 611), (8, 64, 256), jnp.float32))
        itok_BxS_8_8191 = jax.random.randint(jax.random.fold_in(_rk, 12), (8, 512), 8, 2048, jnp.int32)
        itok_BxS2_1_8191 = jax.random.randint(jax.random.fold_in(_rk, 13), (8, 64), 1, 2048, jnp.int32)
        _validS = jnp.arange(512)[None, :] < _lenS[:, None]
        _validS2 = jnp.arange(64)[None, :] < _lenS2[:, None]
        _causal = jnp.tril(jnp.ones((512, 512), dtype=bool))
        mask_BxSxS2_if1 = jnp.where(jnp.ones((8, 512, 64), dtype=bool), 1, 0).astype(jnp.int32)
        return (x, ctx_1024, itok_BxS_8_8191, itok_BxS2_1_8191, mask_BxSxS2_if1)
    x, ctx_1024, itok_BxS_8_8191, itok_BxS2_1_8191, mask_BxSxS2_if1 = _rec_inputs()

    def _L0_attn_setup():
        import jax, jax.numpy as jnp
        import numpy as np
        B, T, D = (4, 512, 256)
        H = 4
        K = D // H
        V = D // H
        M = 64
        GATE_LOGIT_NORMALIZER = 8.0
        NORM_EPS = 1e-05

        def _swish(x):
            return x * jax.nn.sigmoid(x)

        def _gsa_recurrence(q, k, v, s, g, scale):
            b, t, h, dk = q.shape
            dv = v.shape[-1]
            m = s.shape[-1]

            def step(carry, inp):
                hk, hv = carry
                q_t, k_t, v_t, s_t, g_t = inp
                ge = jnp.exp(g_t)
                hk = hk * ge[:, :, None, :] + k_t[..., :, None] * s_t[..., None, :]
                logits = jnp.einsum('bhk,bhkm->bhm', q_t * scale, hk)
                p = jax.nn.softmax(logits, axis=-1)
                hv = hv * ge[..., :, None] + s_t[..., :, None] * v_t[..., None, :]
                o_t = jnp.einsum('bhm,bhmv->bhv', p, hv)
                return ((hk, hv), o_t)
            init = (jnp.zeros((b, h, dk, m), q.dtype), jnp.zeros((b, h, m, dv), q.dtype))
            xs = tuple((jnp.moveaxis(a, 1, 0) for a in (q, k, v, s, g)))
            _, o = jax.lax.scan(step, init, xs)
            return jnp.moveaxis(o, 0, 1)
        key = jax.random.key(seed)
        ks = jax.random.split(key, 6)
        sc = lambda n: 1.0 / np.sqrt(n)
        return {'x': jax.random.normal(ks[0], (B, T, D), jnp.float32), 'Wq': jax.random.normal(ks[1], (D, H * K), jnp.float32) * sc(D), 'Wk': jax.random.normal(ks[2], (D, H * K), jnp.float32) * sc(D), 'Wv': jax.random.normal(ks[3], (D, H * V), jnp.float32) * sc(D), 'Wf': jax.random.normal(ks[4], (D, H * M), jnp.float32) * sc(D), 'g_norm_w': jnp.ones((V,), jnp.float32), 'Wo': jax.random.normal(ks[5], (H * V, D), jnp.float32) * sc(H * V)}
    _L0_attn_all = _L0_attn_setup()
    _L0_attn_in = {k: v for k, v in _L0_attn_all.items() if k in ('Wq', 'Wk', 'Wv', 'Wf', 'g_norm_w', 'Wo')}
    del _L0_attn_all

    def _L0_xattn_setup():
        import jax, jax.numpy as jnp
        import numpy as np
        DIM = 256
        NUM_HEADS = 16
        HEAD_DIM = DIM // NUM_HEADS

        def _slopes(num_heads):
            ratio = 2.0 ** (-8.0 / num_heads)
            return jnp.asarray([ratio ** i for i in range(1, num_heads + 1)], dtype=jnp.float32)
        key = jax.random.key(seed)
        ks = jax.random.split(key, 10)
        b, q_len, k_len = (2, 512, 1024)
        query = jax.random.normal(ks[0], (b, q_len, DIM), dtype=jnp.float32)
        keys = jax.random.normal(ks[1], (b, k_len, DIM), dtype=jnp.float32)
        values = jax.random.normal(ks[2], (b, k_len, DIM), dtype=jnp.float32)
        query_pos = jnp.sort(jax.random.randint(ks[3], (b, q_len), 0, 2048), axis=-1)
        key_pos = jnp.sort(jax.random.randint(ks[4], (b, k_len), 0, 2048), axis=-1)
        mask = jnp.ones((b, q_len, k_len), dtype=jnp.int32)
        lim = float(np.sqrt(6.0 / (DIM + DIM)))
        W_q = jax.random.uniform(ks[5], (DIM, DIM), minval=-lim, maxval=lim, dtype=jnp.float32)
        W_k = jax.random.uniform(ks[6], (DIM, DIM), minval=-lim, maxval=lim, dtype=jnp.float32)
        W_v = jax.random.uniform(ks[7], (DIM, DIM), minval=-lim, maxval=lim, dtype=jnp.float32)
        W_o = jax.random.uniform(ks[8], (DIM, DIM), minval=-lim, maxval=lim, dtype=jnp.float32)
        return {'query': query, 'keys': keys, 'values': values, 'W_q': W_q, 'W_k': W_k, 'W_v': W_v, 'W_o': W_o, 'query_pos': query_pos, 'key_pos': key_pos, 'mask': mask}
    _L0_xattn_all = _L0_xattn_setup()
    _L0_xattn_in = {k: v for k, v in _L0_xattn_all.items() if k in ('W_q', 'W_k', 'W_v', 'W_o')}
    del _L0_xattn_all

    def _L0_ffn_setup():
        import math
        import jax, jax.numpy as jnp
        import numpy as np
        TOP_K = 2
        CAP_FACTOR = 1.25
        CLAMP = 10000.0
        key = jax.random.key(seed)
        k1, k2, k3, k4, k5 = jax.random.split(key, 5)
        B, S, D, F, E = (4, 512, 256, 1024, 8)
        std = 0.02
        return {'x': jax.random.normal(k1, (B, S, D), dtype=jnp.float32), 'Wr': jax.random.normal(k2, (D, E), dtype=jnp.float32) * std, 'W1': jax.random.normal(k3, (E, D, F), dtype=jnp.float32) * std, 'W3': jax.random.normal(k4, (E, D, F), dtype=jnp.float32) * std, 'W2': jax.random.normal(k5, (E, F, D), dtype=jnp.float32) * std}
    _L0_ffn_all = _L0_ffn_setup()
    _L0_ffn_in = {k: v for k, v in _L0_ffn_all.items() if k in ('Wr', 'W1', 'W3', 'W2')}
    del _L0_ffn_all
    return {'x': x, 'ctx_1024': ctx_1024, 'itok_BxS_8_8191': itok_BxS_8_8191, 'itok_BxS2_1_8191': itok_BxS2_1_8191, 'mask_BxSxS2_if1': mask_BxSxS2_if1, 'L0_attn_Wq': _L0_attn_in['Wq'], 'L0_attn_Wk': _L0_attn_in['Wk'], 'L0_attn_Wv': _L0_attn_in['Wv'], 'L0_attn_Wf': _L0_attn_in['Wf'], 'L0_attn_g_norm_w': _L0_attn_in['g_norm_w'], 'L0_attn_Wo': _L0_attn_in['Wo'], 'L0_xattn_W_q': _L0_xattn_in['W_q'], 'L0_xattn_W_k': _L0_xattn_in['W_k'], 'L0_xattn_W_v': _L0_xattn_in['W_v'], 'L0_xattn_W_o': _L0_xattn_in['W_o'], 'L0_ffn_Wr': _L0_ffn_in['Wr'], 'L0_ffn_W1': _L0_ffn_in['W1'], 'L0_ffn_W3': _L0_ffn_in['W3'], 'L0_ffn_W2': _L0_ffn_in['W2']}

def reference(x, ctx_1024, itok_BxS_8_8191, itok_BxS2_1_8191, mask_BxSxS2_if1, L0_attn_Wq, L0_attn_Wk, L0_attn_Wv, L0_attn_Wf, L0_attn_g_norm_w, L0_attn_Wo, L0_xattn_W_q, L0_xattn_W_k, L0_xattn_W_v, L0_xattn_W_o, L0_ffn_Wr, L0_ffn_W1, L0_ffn_W3, L0_ffn_W2):
    import jax
    import jax.numpy as jnp

    def _L0_attn_ref(x, Wq, Wk, Wv, Wf, g_norm_w, Wo):
        import jax, jax.numpy as jnp
        import numpy as np
        B, T, D = (4, 512, 256)
        H = 4
        K = D // H
        V = D // H
        M = 64
        GATE_LOGIT_NORMALIZER = 8.0
        NORM_EPS = 1e-05

        def _swish(x):
            return x * jax.nn.sigmoid(x)

        def _gsa_recurrence(q, k, v, s, g, scale):
            b, t, h, dk = q.shape
            dv = v.shape[-1]
            m = s.shape[-1]

            def step(carry, inp):
                hk, hv = carry
                q_t, k_t, v_t, s_t, g_t = inp
                ge = jnp.exp(g_t)
                hk = hk * ge[:, :, None, :] + k_t[..., :, None] * s_t[..., None, :]
                logits = jnp.einsum('bhk,bhkm->bhm', q_t * scale, hk)
                p = jax.nn.softmax(logits, axis=-1)
                hv = hv * ge[..., :, None] + s_t[..., :, None] * v_t[..., None, :]
                o_t = jnp.einsum('bhm,bhmv->bhv', p, hv)
                return ((hk, hv), o_t)
            init = (jnp.zeros((b, h, dk, m), q.dtype), jnp.zeros((b, h, m, dv), q.dtype))
            xs = tuple((jnp.moveaxis(a, 1, 0) for a in (q, k, v, s, g)))
            _, o = jax.lax.scan(step, init, xs)
            return jnp.moveaxis(o, 0, 1)
        b, t, d = x.shape
        q = _swish((x @ Wq).reshape(b, t, H, K))
        k = _swish((x @ Wk).reshape(b, t, H, K))
        v = (x @ Wv).reshape(b, t, H, V)
        f = jax.nn.log_sigmoid((x @ Wf).reshape(b, t, H, M)) / GATE_LOGIT_NORMALIZER
        s = 1.0 - jnp.exp(f)
        o = _gsa_recurrence(q, k, v, s, f, scale=K ** (-0.5))
        o = o * jax.lax.rsqrt(jnp.mean(o * o, axis=-1, keepdims=True) + NORM_EPS) * g_norm_w
        return o.reshape(b, t, H * V) @ Wo

    def _L0_xattn_ref(query, keys, values, W_q, W_k, W_v, W_o, query_pos, key_pos, mask):
        import jax, jax.numpy as jnp
        import numpy as np
        DIM = 256
        NUM_HEADS = 16
        HEAD_DIM = DIM // NUM_HEADS

        def _slopes(num_heads):
            ratio = 2.0 ** (-8.0 / num_heads)
            return jnp.asarray([ratio ** i for i in range(1, num_heads + 1)], dtype=jnp.float32)
        b, q_len, _ = query.shape
        k_len = keys.shape[1]
        scale = 1.0 / np.sqrt(HEAD_DIM)
        Q = (query @ W_q.T).reshape(b, q_len, NUM_HEADS, HEAD_DIM).transpose(0, 2, 1, 3)
        K = (keys @ W_k.T).reshape(b, k_len, NUM_HEADS, HEAD_DIM).transpose(0, 2, 1, 3)
        V = (values @ W_v.T).reshape(b, k_len, NUM_HEADS, HEAD_DIM).transpose(0, 2, 1, 3)
        scores = jnp.einsum('bhqd,bhkd->bhqk', Q, K) * scale
        dist = (query_pos[:, :, None] - key_pos[:, None, :]).astype(scores.dtype)
        bias = -_slopes(NUM_HEADS)[None, :, None, None] * dist[:, None, :, :]
        scores = scores + bias
        scores = jnp.where(mask[:, None, :, :] == 0, -jnp.inf, scores)
        m = jnp.max(scores, axis=-1, keepdims=True)
        e = jnp.exp(scores - m)
        attn = e / (1.0 + jnp.sum(e, axis=-1, keepdims=True))
        out = jnp.einsum('bhqk,bhkd->bhqd', attn, V)
        out = out.transpose(0, 2, 1, 3).reshape(b, q_len, DIM)
        return out @ W_o.T

    def _L0_ffn_ref(x, Wr, W1, W3, W2):
        import math
        import jax, jax.numpy as jnp
        import numpy as np
        TOP_K = 2
        CAP_FACTOR = 1.25
        CLAMP = 10000.0
        B, S, D = x.shape
        E = Wr.shape[1]
        K = TOP_K
        T = B * S
        cap = max(1, math.ceil(T * K * CAP_FACTOR / E))
        xf = x.reshape(T, D)
        logits = jnp.clip(xf @ Wr, -CLAMP, CLAMP)
        top_v, top_i = jax.lax.top_k(logits, K)
        m = jnp.max(top_v, axis=-1, keepdims=True)
        expv = jnp.exp(top_v - m)
        top_p = expv / (jnp.sum(expv, axis=-1, keepdims=True) + 1e-12)
        Sp = T * K
        experts = top_i.reshape(Sp)
        weights = top_p.reshape(Sp)
        tokens = jnp.repeat(jnp.arange(T), K)
        oh = experts[:, None] == jnp.arange(E)[None, :]
        pos = jnp.sum(jnp.cumsum(oh.astype(jnp.int32), axis=0) * oh, axis=-1) - 1
        kept = pos < cap
        pos_safe = jnp.where(kept, pos, cap)
        xe = jnp.zeros((E, cap + 1, D), x.dtype).at[experts, pos_safe].set(xf[tokens])[:, :cap]
        h = jax.nn.silu(jnp.einsum('ecd,edf->ecf', xe, W1)) * jnp.einsum('ecd,edf->ecf', xe, W3)
        ye = jnp.einsum('ecf,efd->ecd', h, W2)
        yp = ye[experts, jnp.minimum(pos_safe, cap - 1)]
        wk = weights * kept.astype(weights.dtype)
        out = jnp.zeros((T, D), x.dtype).at[tokens].add(wk[:, None] * yp)
        return out.reshape(B, S, D)
    x = x + _L0_attn_ref(_layernorm(x, axis=-1), L0_attn_Wq, L0_attn_Wk, L0_attn_Wv, L0_attn_Wf, L0_attn_g_norm_w, L0_attn_Wo)
    x = x + _L0_xattn_ref(_layernorm(x, axis=-1), ctx_1024, ctx_1024, L0_xattn_W_q, L0_xattn_W_k, L0_xattn_W_v, L0_xattn_W_o, itok_BxS_8_8191, itok_BxS2_1_8191, mask_BxSxS2_if1)
    x = x + _L0_ffn_ref(_layernorm(x, axis=-1), L0_ffn_Wr, L0_ffn_W1, L0_ffn_W3, L0_ffn_W2)
    return x

_drawn_inputs = setup_inputs


def setup_inputs(seed=0):
    import zlib

    import numpy as np

    out = dict(_drawn_inputs(seed))
    spreads = {'L0_attn_g_norm_w': (1.0, 0.2)}
    factors = {'L0_attn_Wq': 8.0,
     'L0_attn_Wk': 7.676,
     'L0_ffn_Wr': 4.044,
     'L0_ffn_W1': 3.576,
     'L0_ffn_W3': 3.535,
     'L0_ffn_W2': 3.534}
    for name, (base, spread) in spreads.items():
        noise = np.random.default_rng([zlib.crc32(name.encode()), seed]).standard_normal(out[name].shape)
        drawn = base * np.exp(spread * noise) if base else spread * noise
        out[name] = jnp.asarray(drawn.astype(out[name].dtype))
    for name, factor in factors.items():
        out[name] = (out[name] * factor).astype(out[name].dtype)
    return out
```

```python
from contextlib import ExitStack

import concourse.bass as bass
import numpy as np
from concourse import mybir

ALU = mybir.AluOpType
ACT = mybir.ActivationFunctionType
AX = mybir.AxisListType
F32 = mybir.dt.float32
I32 = mybir.dt.int32
U32 = mybir.dt.uint32

P = 128
B, T, D = 8, 512, 256
NCH = B * T // P
CPB = T // P
KT = D // P
H, M = 4, 64
GATE_NORM = 8.0
EPS = 1e-5
XH, XD, KL = 16, 16, 64
HPT = P // XD
PAIRS = XH // 2
XSCALE = 1.0 / 4.0
HIDDEN = 1.0e38
E, F, TOPK = 8, 1024, 2
CAP = -(-B * T * TOPK * 5 // (4 * E))
SLOTS = E * CAP
GS = 256
GPE = CAP // GS
NG = E * GPE
GPL = 2 * GPE
FT = F // P
CLAMP = 10000.0
ROUTE_STEPS = 12
SPACE = 21754
SLOPE = [float(v) for v in np.float32(2.0 ** (-8.0 / XH)) ** np.arange(1, XH + 1, dtype=np.float32)]
SKIPPED = float(4 * SLOTS)


def decoder_layer(nc, x, qpos, kpos, mask, ctx_t, wq, wk, wv, wf, gnorm, wo,
                  xwq_t, xwk_t, xwv_t, xwo_t, wr, w1, w3, w2, out):
    xe_dram = nc.dram_tensor("expert_rows", (SLOTS, D), F32, kind="Internal").ap()
    y_dram = nc.dram_tensor("expert_out", (SLOTS, D), F32, kind="Internal").ap()
    ctx = ExitStack()
    with ctx:
        def sb(name, shape, dt=F32):
            return ctx.enter_context(nc.sbuf_tensor(name, shape, dt))

        def sem(name):
            return ctx.enter_context(nc.semaphore(name))

        ident = sb("ident", [P, P])
        causal = sb("causal", [P, P])
        tri_half = sb("tri_half", [P, P])
        half = sb("half", [P, P])
        ones = sb("ones", [P, P])
        before = sb("before", [P, P])
        diag16 = sb("diag16", [P, HPT])
        pair_of = sb("pair_of", [P, 2])
        slopes = sb("slopes", [P, XH])
        expert_no = sb("expert_no", [P, E])
        neg_half = sb("neg_half", [P, 4])
        w_in = sb("w_in", [P, KT, 4 * D])
        wo_raw = sb("wo_raw", [P, KT, D])
        gn = sb("gn", [P, 1])
        wo_s = sb("wo_s", [P, KT, D])
        xw = sb("xw", [P, 4, KT, D])
        wr_s = sb("wr_s", [P, KT, E])
        ctx_s = sb("ctx_s", [P, KT, B * KL])
        ctx2 = sb("ctx2", [P, KT, 2, KL])
        kp_i = sb("kp_i", [P, B * KL], I32)
        kp = sb("kp", [P, B, KL])
        qp_i = sb("qp_i", [P, NCH], I32)
        qp = sb("qp", [P, NCH])
        zeros = sb("zeros", [P, D])
        k_all = sb("k_all", [P, KT, B * KL])
        v_all = sb("v_all", [P, B, PAIRS, 2, XD])
        idle_v, idle_g = sb("idle_v", [P, 1]), sb("idle_g", [P, 2])
        x2_all = sb("x2_all", [P, NCH, D])
        wgt_all = sb("wgt_all", [P, NCH, 2])
        slot_all = sb("slot_all", [P, NCH, 2], U32)
        space = sb("space", [P, SPACE])
        used = [0, 0]

        def carve(which, shape):
            n = int(np.prod(shape[1:]))
            at = used[which]
            used[which] += n
            flat = space[:, at:at + n]
            if len(shape) == 2:
                return flat
            names = " ".join("abce"[:len(shape) - 1])
            return flat.rearrange(f"p ({names}) -> p {names}", **dict(zip("abce", shape[1:])))

        def lane(name, shape):
            return carve(0, shape)

        def later_use(name, shape):
            return carve(1, shape)

        xin = lane("xin", [P, 4, D])
        f_st, f_mv, f_var, f_rstd = lane("f_st", [P, 6]), lane("f_mv", [P, 2]), lane("f_var", [P, 1]), lane("f_rstd", [P, 1])
        f_xn = lane("f_xn", [P, D])
        f_xnt = lane("f_xnt", [P, KT, P])
        qk_e, qk_l, qk_s = lane("qk_e", [P, 2 * D]), lane("qk_l", [P, 2 * D]), lane("qk_s", [P, 2 * D])
        q_z = lane("q_z", [P, 2, H, P])
        k_s = lane("k_s", [P, D])
        v_s = lane("v_s", [P, 2, D])
        f_abs, f_e, f_l = lane("f_abs", [P, D]), lane("f_e", [P, D]), lane("f_l", [P, D])
        g_s = lane("g_s", [P, 2, D])
        one_less = lane("one_less", [P, D])
        up = lane("up", [P, 2, D])
        down = lane("down", [P, D])
        dec_row = lane("dec_row", [P, D])
        dec_col = lane("dec_col", [P, 2])
        s_s = lane("s_s", [P, 2, D])
        ks_t = lane("ks_t", [P, 2, 4, P])
        a_s = lane("a_s", [P, 2, H, P])
        zk, zv = lane("zk", [P, 2, P]), lane("zv", [P, 2, P])
        hk, hv = lane("hk", [P, 2, 2, P]), lane("hv", [P, 2, 2, P])
        lg, lg_m, lg_d, b_e = lane("lg", [P, H, M]), lane("lg_m", [P, H]), lane("lg_d", [P, H, M]), lane("b_e", [P, H, M])
        b_sum, b_rec = lane("b_sum", [P, H]), lane("b_rec", [P, H])
        b_p = lane("b_p", [P, D])
        p_z = lane("p_z", [P, H, P])
        bt_s = lane("bt_s", [P, H, P])
        b_sq, b_ss, b_t1, b_t2, b_ms = (lane("b_sq", [P, H, M]), lane("b_ss", [P, H]), lane("b_t1", [P, H]),
                                        lane("b_t2", [P, H]), lane("b_ms", [P, H]))
        b_rms, b_w = lane("b_rms", [P, H]), lane("b_w", [P, H])
        b_o = lane("b_o", [P, H, M])
        o_t = lane("o_t", [P, 2, P])
        x1 = lane("x1", [P, 2, D])
        x_st, x_mv, x_var, x_rstd = lane("x_st", [P, 6]), lane("x_mv", [P, 2]), lane("x_var", [P, 1]), lane("x_rstd", [P, 1])
        x_xn = lane("x_xn", [P, D])
        x_xnt = lane("x_xnt", [P, KT, P])
        xq_t = lane("xq_t", [P, KT, P])
        k_bd = lane("k_bd", [P, KT, HPT, KL])
        v_bd = lane("v_bd", [P, PAIRS, 2 * XD])
        mask_i = sb("mask_i", [P, 2, KL], I32)
        hid, dist = lane("hid", [P, KL]), lane("dist", [P, KL])
        bias = lane("bias", [P, XH, KL])
        sc = lane("sc", [P, XH, KL])
        sc_m = lane("sc_m", [P, XH])
        ex = lane("ex", [P, XH, KL])
        x_sum, x_den, x_rec = lane("x_sum", [P, XH]), lane("x_den", [P, XH]), lane("x_rec", [P, XH])
        e_t = lane("e_t", [P, PAIRS, P])
        x_o = lane("x_o", [P, XH, XD])
        xo_t = lane("xo_t", [P, KT, P])
        r_x = sb("r_x", [P, 2, D])
        r_st, r_mv, r_var, r_rstd = sb("r_st", [P, 6]), sb("r_mv", [P, 2]), sb("r_var", [P, 1]), sb("r_rstd", [P, 1])
        r_xn = sb("r_xn", [P, 2, D])
        r_xnt = sb("r_xnt", [P, KT, P])
        r_lg, top, top_i = sb("r_lg", [P, E]), sb("top", [P, 8]), sb("top_i", [P, 8], U32)
        top_f = sb("top_f", [P, 2])
        hot = sb("hot", [P, 2, E])
        both = sb("both", [P, E])
        taken = sb("taken", [P, E])
        place = sb("place", [P, E])
        place_h = sb("place_h", [P, 2, E])
        pos = sb("pos", [P, 2])
        kept, base = sb("kept", [P, 1]), sb("base", [P, 2])
        slot_f, off_f = sb("slot_f", [P, 2]), sb("off_f", [P, 2])
        send = sb("send", [P, 2, 2], U32)
        gap, r_e, r_den, r_p = sb("gap", [P, 1]), sb("r_e", [P, 1]), sb("r_den", [P, 1]), sb("r_p", [P, 1])
        w1_s = [sb("w1_even", [P, KT, F]), later_use("w1_odd", [P, KT, F])]
        w3_s = [sb("w3_even", [P, KT, F]), later_use("w3_odd", [P, KT, F])]
        w2_s = [sb("w2_even", [P, FT, D]), later_use("w2_odd", [P, FT, D])]
        xe = later_use("xe", [P, 2, 2, D])
        xe_t = later_use("xe_t", [P, 2, KT, 2, P])
        h_a = later_use("h_a", [P, 2, GS])
        h_t = later_use("h_t", [P, 2, FT, GS])
        y_s = later_use("y_s", [P, 2, 2, D])
        c_i = sb("c_i", [P, 2, 2], U32)
        c_y = later_use("c_y", [P, 2, 2, D])
        c_1, c_o = later_use("c_1", [P, 2, D]), later_use("c_o", [P, 2, D])

        assert max(used) == SPACE, used
        bank = [ctx.enter_context(nc.psum_tensor(f"bank{i}", [P, 512], F32)) for i in range(8)]
        F0, F1, F2, B0, B1, X0, X1, X2 = (b[:, :] for b in bank)

        consts_made, w_landed, ctx_landed, zeros_sent = sem("consts_made"), sem("w_landed"), sem("ctx_landed"), sem("zeros_sent")
        consts_step = sem("consts_step")
        small_made, ctx_doubled, ctx_mm, v_made = sem("small_made"), sem("ctx_doubled"), sem("ctx_mm"), sem("v_made")
        k_made = sem("k_made")
        x_landed = [sem(f"x_landed{i}") for i in range(4)]
        mask_landed = [sem(f"mask_landed{i}") for i in range(2)]
        f_stats, f_vared, f_rstded, f_normed, f_xnt_mm, f_xnt_ok = map(sem, (
            "f_stats", "f_vared", "f_rstded", "f_normed", "f_xnt_mm", "f_xnt_ok"))
        proj_mm, e_done, l_done, sig_done, v_ok, abs_done, fe_done, fl_done = map(sem, (
            "proj_mm", "e_done", "l_done", "sig_done", "v_ok", "abs_done", "fe_done", "fl_done"))
        g_ok, qk_ok, gsum_mm, less_done, up_ok, down_ok, decr_ok, decc_ok, s_ok = map(sem, (
            "g_ok", "qk_ok", "gsum_mm", "less_done", "up_ok", "down_ok", "decr_ok", "decc_ok", "s_ok"))
        kst_mm, kst_ok, a_mm, a_ok, st_mm, hk_ok, hv_ok, zk_ok, zv_ok = map(sem, (
            "kst_mm", "kst_ok", "a_mm", "a_ok", "st_mm", "hk_ok", "hv_ok", "zk_ok", "zv_ok"))
        l_mm, lg_ok, lgm_ok, lgd_ok, be_ok, bsum_ok, brec_ok, bp_ok, pt_mm, pt_ok = map(sem, (
            "l_mm", "lg_ok", "lgm_ok", "lgd_ok", "be_ok", "bsum_ok", "brec_ok", "bp_ok", "pt_mm", "pt_ok"))
        bt_mm, bt_ok, o_mm, sq_ok, ss_ok, rms_step, ms_ok, rms_ok, bw_ok, bo_ok, ot_mm, ot_ok, y_mm, x1_ok = map(sem, (
            "bt_mm", "bt_ok", "o_mm", "sq_ok", "ss_ok", "rms_step", "ms_ok", "rms_ok", "bw_ok", "bo_ok",
            "ot_mm", "ot_ok", "y_mm", "x1_ok"))
        x_stats, x_vared, x_rstded, x_normed, x_xnt_mm, x_xnt_ok, xq_mm, xq_ok = map(sem, (
            "x_stats", "x_vared", "x_rstded", "x_normed", "x_xnt_mm", "x_xnt_ok", "xq_mm", "xq_ok"))
        kbd_ok, vbd_ok, hid_ok, dist_ok, bias_ok, sc_mm, sc_ok, scm_ok, scd_ok, ex_ok = map(sem, (
            "kbd_ok", "vbd_ok", "hid_ok", "dist_ok", "bias_ok", "sc_mm", "sc_ok", "scm_ok", "scd_ok", "ex_ok"))
        xsum_ok, xden_ok, xrec_ok, et_mm, et_ok_a, et_ok_v, av_mm, xo_ok, xot_mm, xot_ok, xy_mm, x2_made = map(sem, (
            "xsum_ok", "xden_ok", "xrec_ok", "et_mm", "et_ok_a", "et_ok_v", "av_mm", "xo_ok", "xot_mm", "xot_ok",
            "xy_mm", "x2_made"))
        x2_kept = sem("x2_kept")
        r_stats, r_vared, r_rstded, r_normed, r_xnt_mm, r_xnt_ok, rlg_mm, rlg_ok = map(sem, (
            "r_stats", "r_vared", "r_rstded", "r_normed", "r_xnt_mm", "r_xnt_ok", "rlg_mm", "rlg_ok"))
        topi_ok, both_ok, gap_ok, re_ok, cnt_mm, place_ok, taken_ok = map(sem, (
            "topi_ok", "both_ok", "gap_ok", "re_ok", "cnt_mm", "place_ok", "taken_ok"))
        slots_ok, halves_zeroed, route_step = sem("slots_ok"), sem("halves_zeroed"), sem("route_step")
        sent = [sem(f"sent{i}") for i in range(4)]
        wup_landed = [sem(f"wup_landed{i}") for i in range(2)]
        wdn_landed = [sem(f"wdn_landed{i}") for i in range(2)]
        xe_landed = [sem(f"xe_landed{i}") for i in range(2)]
        xet_mm, xet_ok, up_mm, silu_ok, h_ok, dn_mm, y_ok = map(sem, (
            "xet_mm", "xet_ok", "up_mm", "silu_ok", "h_ok", "dn_mm", "y_ok"))
        y_stored = [sem(f"y_stored{i}") for i in range(2)]
        ci_ok, c1_ok, co_ok = sem("ci_ok"), sem("c1_ok"), sem("co_ok")
        gathered = [sem(f"gathered{i}") for i in range(2)]
        held = sem("held")
        stored = [sem(f"stored{i}") for i in range(2)]

        def over_chunks(eng, step, lags=3):
            for c in range(CPB):
                step(0, c, [g <= c for g in range(lags + 1)])
            with eng.Fori(1, B) as b:
                for c in range(CPB):
                    step(b, c, [True] * (lags + 1))
            for c in range(lags):
                step(B, c, [g > c for g in range(lags + 1)])

        def over_groups(eng, step):
            for j in range(GPL):
                step(0, j)
            with eng.Fori(1, E // 2 - 1) as d:
                for j in range(GPL):
                    step(d, j)
            for j in range(GPL):
                step(E // 2 - 1, j)

        def later(n, k):
            return not isinstance(n, int) or n >= k

        def is_last(n, last):
            return isinstance(n, int) and n == last

        CONSTS = 14 + XH
        x_rows = x.rearrange("b (c p) d -> (b c p) d", p=P)
        out_rows = out.rearrange("b t d -> (b t) d")
        mask_rows = mask.rearrange("b t k -> (b t) k")

        block = ctx.enter_context(nc.Block())

        @block.sync
        def _(sp):
            def feat(w):
                return w.rearrange("(k p) n -> p k n", p=P)

            def load_x(n, c):
                sp.dma_start(xin[:, c, :], x_rows[bass.ds(n * P, P), :]).then_inc(x_landed[c], 16)

            load_x(0, 0)
            for j, w in enumerate((wq, wk, wv, wf)):
                sp.dma_start(w_in[:, :, j * D:(j + 1) * D], feat(w)).then_inc(w_landed, 16)
            sp.dma_start(wo_raw[:, :, :], feat(wo)).then_inc(w_landed, 16)
            gcol = gnorm.rearrange("(m a) -> m a", a=1)
            sp.dma_start(gn[0:M, :], gcol).then_inc(w_landed, 16)
            sp.dma_start(gn[M:2 * M, :], gcol).then_inc(w_landed, 16)
            for j, w in enumerate((xwq_t, xwk_t, xwv_t, xwo_t)):
                sp.dma_start(xw[:, j, :, :], feat(w)).then_inc(w_landed, 16)
            sp.dma_start(wr_s[:, :, :], feat(wr)).then_inc(w_landed, 16)
            sp.dma_start(ctx_s[:, :, :], feat(ctx_t)).then_inc(ctx_landed, 16)
            sp.dma_start(kp_i[:, :], kpos.rearrange("(a b) k -> a (b k)", a=1).to_broadcast([P, B * KL]))\
              .then_inc(ctx_landed, 16)
            sp.dma_start(qp_i[:, :], qpos).then_inc(ctx_landed, 16)
            sp.wait_ge(consts_made, 1)
            per = SLOTS // P
            for j in range(4):
                rows = xe_dram[j * SLOTS // 4:(j + 1) * SLOTS // 4, :].rearrange("(p r) d -> p r d", p=P)
                sp.dma_start(rows, zeros[:, :].rearrange("p (r d) -> p r d", r=1).to_broadcast([P, per // 4, D]))\
                  .then_inc(zeros_sent, 16)

            def step(b, c, x_on, mask_on):
                s = b * CPB + c
                if x_on:
                    nxt = (c + 1) % 4
                    if later(s, 3):
                        sp.wait_ge(x1_ok, s - 2)
                    sp.dma_start(xin[:, nxt, :], x_rows[bass.ds((s + 1) * P, P), :]).then_inc(x_landed[nxt], 16)
                if mask_on:
                    par = (c - 2) % 2
                    if later(s, 4):
                        sp.wait_ge(hid_ok, s - 3)
                    sp.dma_start(mask_i[:, par, :], mask_rows[bass.ds((s - 2) * P, P), :])\
                      .then_inc(mask_landed[par], 16)

            for c in range(CPB):
                step(0, c, True, c >= 2)
            with sp.Fori(1, B - 1) as b:
                for c in range(CPB):
                    step(b, c, True, True)
            for s in range(NCH - CPB, NCH + 2):
                step(s // CPB, s % CPB, s < NCH - 1, True)

            def load_expert(e, par):
                sp.dma_start(w1_s[par][:, :, :], w1[bass.ds(e, 1), :, :].rearrange("a (k p) f -> p (a k) f", p=P))\
                  .then_inc(wup_landed[par], 16)
                sp.dma_start(w3_s[par][:, :, :], w3[bass.ds(e, 1), :, :].rearrange("a (k p) f -> p (a k) f", p=P))\
                  .then_inc(wup_landed[par], 16)
                sp.dma_start(w2_s[par][:, :, :], w2[bass.ds(e, 1), :, :].rearrange("a (k p) n -> p (a k) n", p=P))\
                  .then_inc(wdn_landed[par], 16)

            def load_group(g, par):
                sp.dma_start(xe[:, par, :, :], xe_dram[bass.ds(g * GS, GS), :].rearrange("(a p) d -> p a d", p=P))\
                  .then_inc(xe_landed[par], 16)

            load_expert(0, 0)
            for i in range(4):
                sp.wait_ge(sent[i], 16 * NCH // 2)
            load_group(0, 0)

            def store(g, par):
                sp.wait_ge(y_ok, g + 1)
                sp.dma_start(y_dram[bass.ds(g * GS, GS), :].rearrange("(a p) d -> p a d", p=P), y_s[:, par, :, :])\
                  .then_inc(y_stored[par], 16)

            def group(d, j):
                g, par = d * GPL + j, j % 2
                if not is_last(g, NG - 1):
                    if later(g, 1):
                        sp.wait_ge(xet_mm, g)
                    load_group(g + 1, 1 - par)
                if j % GPE == 1 and not (isinstance(d, int) and 2 * d + j // GPE == E - 1):
                    if later(g, GPE):
                        sp.wait_ge(dn_mm, g - 1)
                    load_expert(2 * d + j // GPE + 1, 1 - j // GPE)
                if later(g, 1):
                    store(g - 1, 1 - par)

            over_groups(sp, group)
            store(NG - 1, 1)

            with sp.Fori(0, NCH // 2) as d:
                for par in range(2):
                    n = d * 2 + par
                    sp.wait_ge(co_ok, n + 1)
                    sp.dma_start(out_rows[bass.ds(n * P, P), :], c_o[:, par, :]).then_inc(stored[par], 16)
            for par in range(2):
                sp.wait_ge(stored[par], 16 * NCH // 2)

        @block.gpsimd
        def _(pool):
            pool.memset(zeros[:, :], 0.0).then_inc(consts_made, 1)
            pool.memset(ident[:, :], 0.0).then_inc(consts_step, 1)
            pool.memset(ones[:, :], 1.0).then_inc(consts_step, 1)
            pool.memset(half[:, :], 0.5).then_inc(consts_step, 1)
            pool.memset(neg_half[:, :], -0.5).then_inc(consts_step, 1)
            pool.memset(taken[:, :], 0.0).then_inc(consts_step, 1)
            for h in range(XH):
                pool.memset(slopes[:, h:h + 1], SLOPE[h]).then_inc(consts_step, 1)
            pool.iota(expert_no[:, :], [[1, E]], base=0, channel_multiplier=0,
                      allow_small_or_imprecise_dtypes=True).then_inc(consts_step, 1)
            pool.wait_ge(consts_step, 6 + XH)
            pool.affine_select(out=ident[:, :], in_=ident[:, :], compare_op=ALU.not_equal, fill=1.0,
                               base=0, pattern=[[-1, P]], channel_multiplier=1).then_inc(consts_step, 1)
            pool.affine_select(out=causal[:, :], in_=ones[:, :], compare_op=ALU.is_ge, fill=0.0,
                               base=0, pattern=[[1, P]], channel_multiplier=-1).then_inc(consts_step, 1)
            pool.affine_select(out=tri_half[:, :], in_=half[:, :], compare_op=ALU.is_ge, fill=-0.5,
                               base=0, pattern=[[1, P]], channel_multiplier=-1).then_inc(consts_step, 1)
            pool.affine_select(out=before[:, :], in_=ones[:, :], compare_op=ALU.is_gt, fill=0.0,
                               base=0, pattern=[[1, P]], channel_multiplier=-1).then_inc(consts_step, 1)
            for tile, n, w in ((diag16, HPT, XD), (pair_of, 2, KL)):
                pool.affine_select(out=tile[:, :], in_=ones[:, 0:n], compare_op=ALU.is_ge, fill=0.0,
                                   base=0, pattern=[[-w, n]], channel_multiplier=1).then_inc(consts_step, 1)
            pool.wait_ge(consts_step, 12 + XH)
            for tile, n, w in ((diag16, HPT, XD), (pair_of, 2, KL)):
                pool.affine_select(out=tile[:, :], in_=tile[:, :], compare_op=ALU.is_ge, fill=0.0,
                                   base=w - 1, pattern=[[w, n]], channel_multiplier=-1).then_inc(consts_step, 1)

            pool.wait_ge(consts_step, CONSTS)

            def hold(i):
                return pool.tensor_tensor(idle_g[:, i:i + 1], half[:, 0:1], half[:, 0:1], ALU.add)

            def power(n, var, rstd, ready, done):
                pool.wait_ge(ready, n + 1)
                w = var.shape[1]
                pool.tensor_tensor(rstd[:, :], var[:, :], neg_half[:, 0:w], ALU.pow).then_inc(done, 1)

            def step(b, c, on):
                s = b * CPB + c
                f, bb, xx, rr = (s - g for g in range(4))
                if on[0]:
                    power(f, f_var, f_rstd, f_vared, f_rstded)
                if on[2]:
                    power(xx, x_var, x_rstd, x_vared, x_rstded)
                    if (c - 2) % CPB == 0:
                        if later(s, 3):
                            pool.wait_ge(sc_mm, xx)
                        else:
                            pool.wait_ge(k_made, 1)
                            pool.wait_ge(v_made, B)
                        for h in range(KT):
                            pool.tensor_tensor(
                                k_bd[:, h, :, :],
                                k_all[:, h, bass.ds(b * KL, KL)].rearrange("p (a k) -> p a k", a=1)
                                .to_broadcast([P, HPT, KL]),
                                diag16[:, :].rearrange("p (h a) -> p h a", a=1).to_broadcast([P, HPT, KL]),
                                ALU.mult).then_inc(kbd_ok, 1)
                        if later(s, 3):
                            pool.wait_ge(av_mm, xx)
                        pool.tensor_copy(v_bd[:, :, :].rearrange("p j n -> p (j n)"),
                                         v_all[:, bass.ds(b, 1), :, :, :].rearrange("p a j i d -> p (a j i d)"))\
                            .then_inc(vbd_ok, 1)
                if on[3]:
                    power(rr, r_var, r_rstd, r_vared, r_rstded)
                    pool.wait_ge(x2_made, rr + 1)
                    pool.tensor_copy(x2_all[:, bass.ds(rr, 1), :].rearrange("p a d -> p (a d)"),
                                     r_x[:, (c - 3) % 2, :]).then_inc(x2_kept, 1)
                if on[2]:
                    pool.wait_ge(dist_ok, xx + 1)
                    if later(s, 3):
                        pool.wait_ge(sc_ok, 2 * xx)
                    pool.tensor_tensor(
                        bias[:, :, :],
                        dist[:, :].rearrange("p (a k) -> p a k", a=1).to_broadcast([P, XH, KL]),
                        slopes[:, :].rearrange("p (h a) -> p h a", a=1).to_broadcast([P, XH, KL]),
                        ALU.mult).then_inc(bias_ok, 1)
                if on[1]:
                    pool.wait_ge(be_ok, bb + 1)
                    if later(s, 2):
                        pool.wait_ge(pt_mm, bb)
                    pool.tensor_tensor(b_p[:, :], b_e[:, :, :].rearrange("p h m -> p (h m)"),
                                       up[:, (c - 1) % 2, :], ALU.mult).then_inc(bp_ok, 1)
                if on[2]:
                    pool.wait_ge(scm_ok, xx + 1)
                    pool.tensor_tensor(
                        sc[:, :, :], sc[:, :, :],
                        sc_m[:, :].rearrange("p (h a) -> p h a", a=1).to_broadcast([P, XH, KL]),
                        ALU.subtract).then_inc(scd_ok, 1)
                if on[1]:
                    power(bb, b_ms, b_rms, ms_ok, rms_ok)
                if on[3]:
                    par = (c - 3) % 2
                    if not later(s, 4):
                        pool.wait_ge(zeros_sent, 64)
                    pool.wait_ge(slots_ok, rr + 1)
                    hold(0)
                    for k in range(2):
                        pool.indirect_dma_start(
                            out=xe_dram, out_offset=bass.IndirectOffsetOnAxis(ap=send[:, par, k:k + 1], axis=0),
                            in_=r_xn[:, par, :], in_offset=None, bounds_check=SLOTS - 1, oob_is_err=False)\
                            .then_inc(sent[2 * par + k], 16)

            over_chunks(pool, step)

            for i in range(2):
                pool.wait_ge(y_stored[i], 16 * NG // 2)

            def gather(n, par):
                if later(n, 1):
                    pool.wait_ge(held, n)
                if later(n, 2):
                    pool.wait_ge(co_ok, n - 1)
                pool.wait_ge(ci_ok, n + 1)
                hold(1).then_inc(held, 1)
                for k in range(2):
                    pool.indirect_dma_start(
                        out=c_y[:, par, k, :], out_offset=None, in_=y_dram,
                        in_offset=bass.IndirectOffsetOnAxis(ap=c_i[:, par, k:k + 1], axis=0),
                        bounds_check=SLOTS - 1, oob_is_err=False).then_inc(gathered[par], 16)

            for par in range(2):
                gather(par, par)
            with pool.Fori(1, NCH // 2) as d:
                for par in range(2):
                    gather(d * 2 + par, par)

        @block.scalar
        def _(act):
            def copy(dst, src, ready, done, n, amount=1.0):
                act.wait_ge(ready, n + 1)
                act.activation(dst, src, ACT.Copy, scale=amount).then_inc(done, 1)

            def step(b, c, on):
                s = b * CPB + c
                f, bb, xx, rr = (s - g for g in range(4))
                fp, bp = c % 2, (c - 1) % 2
                first = isinstance(s, int)
                if on[0]:
                    if later(s, 1):
                        act.wait_ge(proj_mm, f)
                    copy(f_xnt[:, :, :], F2[:, 0:D].rearrange("p (k t) -> p k t", k=KT), f_xnt_mm, f_xnt_ok, f)
                if on[2]:
                    if later(s, 3):
                        act.wait_ge(xq_mm, xx)
                    copy(x_xnt[:, :, :], X2[:, 0:D].rearrange("p (k t) -> p k t", k=KT), x_xnt_mm, x_xnt_ok, xx)
                if on[3]:
                    if later(s, 4):
                        act.wait_ge(rlg_mm, rr)
                    copy(r_xnt[:, :, :], B1[:, D:2 * D].rearrange("p (k t) -> p k t", k=KT), r_xnt_mm, r_xnt_ok, rr)
                if on[1]:
                    act.wait_ge(lgd_ok, bb + 1)
                    if later(s, 2):
                        act.wait_ge(bp_ok, bb)
                    act.activation(b_e[:, :, :], lg_d[:, :, :], ACT.Exp, scale=float(M) ** -0.5).then_inc(be_ok, 1)
                if on[0]:
                    act.wait_ge(proj_mm, f + 1)
                    act.activation(qk_e[:, :], F0, ACT.Exp, scale=-1.0).then_inc(e_done, 1)
                    act.activation(f_abs[:, :], F1[:, D:2 * D], ACT.Abs).then_inc(abs_done, 1)
                    if later(s, 2):
                        act.wait_ge(o_mm, f - 1)
                    act.activation(v_s[:, fp, :], F1[:, 0:D], ACT.Copy).then_inc(v_ok, 1)
                    act.wait_ge(abs_done, f + 1)
                    act.activation(f_e[:, :], f_abs[:, :], ACT.Exp, scale=-1.0).then_inc(fe_done, 1)
                    act.wait_ge(fe_done, f + 1)
                    if later(s, 1):
                        act.wait_ge(g_ok, f)
                    act.activation(f_l[:, :], f_e[:, :], ACT.Ln, bias=1.0).then_inc(fl_done, 1)
                    act.wait_ge(e_done, f + 1)
                    act.activation(qk_l[:, :], qk_e[:, :], ACT.Ln, bias=1.0).then_inc(l_done, 1)
                    act.wait_ge(l_done, f + 1)
                    if later(s, 1):
                        act.wait_ge(qk_ok, 3 * f)
                    act.activation(qk_s[:, :], qk_l[:, :], ACT.Exp, scale=-1.0).then_inc(sig_done, 1)
                if on[2]:
                    act.wait_ge(xq_mm, xx + 1)
                    if later(s, 3):
                        act.wait_ge(sc_mm, xx)
                    act.activation(xq_t[:, :, :], X2[:, D:2 * D].rearrange("p (k t) -> p k t", k=KT), ACT.Copy,
                                   scale=XSCALE).then_inc(xq_ok, 1)
                if on[1]:
                    if later(s, 2):
                        act.wait_ge(o_mm, bb)
                    else:
                        act.wait_ge(halves_zeroed, 2)
                    act.wait_ge(pt_mm, bb + 1)
                    for i in range(2):
                        rows = slice(M * i, M * i + M)
                        act.activation(p_z[rows, i::2, :], B0[rows, D:2 * D].rearrange("p (k t) -> p k t", k=2),
                                       ACT.Copy).then_inc(pt_ok, 1)
                if on[0]:
                    act.wait_ge(g_ok, f + 1)
                    if later(s, 1):
                        act.wait_ge(s_ok, f)
                    act.activation(one_less[:, :], g_s[:, fp, :], ACT.Exp, scale=1 / GATE_NORM).then_inc(less_done, 1)
                    act.wait_ge(gsum_mm, f + 1)
                    act.activation(down[:, :], F2[:, 0:D], ACT.Exp, scale=-1 / GATE_NORM).then_inc(down_ok, 1)
                    if later(s, 2):
                        act.wait_ge(bp_ok, f - 1)
                    act.activation(up[:, fp, :], F2[:, 0:D], ACT.Exp, scale=1 / GATE_NORM).then_inc(up_ok, 1)
                    if later(s, 1):
                        act.wait_ge(hk_ok, f)
                        act.wait_ge(hv_ok, f)
                    act.activation(dec_row[:, :], F2[:, D:2 * D], ACT.Exp, scale=1 / GATE_NORM).then_inc(decr_ok, 1)
                    act.activation(dec_col[:, :], F0[:, 0:2], ACT.Exp, scale=1 / GATE_NORM).then_inc(decc_ok, 1)
                if on[2]:
                    act.wait_ge(scd_ok, xx + 1)
                    if later(s, 3):
                        act.wait_ge(et_mm, 2 * xx)
                        act.wait_ge(xsum_ok, xx)
                    act.activation(ex[:, :, :], sc[:, :, :], ACT.Exp).then_inc(ex_ok, 1)
                if on[1]:
                    act.wait_ge(o_mm, bb + 1)
                    if later(s, 2):
                        act.wait_ge(ss_ok, bb)
                    act.activation(b_sq[:, :, :], B0[:, 0:D].rearrange("p (h m) -> p h m", h=H), ACT.Square)\
                        .then_inc(sq_ok, 1)
                if on[0]:
                    if later(s, 2):
                        act.wait_ge(o_mm, f - 1)
                    copy(ks_t[:, fp, :, :], F0.rearrange("p (k t) -> p k t", k=4), kst_mm, kst_ok, f)
                if on[3]:
                    act.wait_ge(gap_ok, rr + 1)
                    if later(s, 4):
                        act.wait_ge(slots_ok, rr)
                    act.activation(r_e[:, :], gap[:, :], ACT.Exp).then_inc(re_ok, 1)
                if on[2]:
                    if later(s, 3):
                        act.wait_ge(av_mm, xx)
                    act.wait_ge(et_mm, 2 * xx + 1)
                    act.activation(e_t[:, 0:4, :], X0.rearrange("p (k t) -> p k t", k=4), ACT.Copy).then_inc(et_ok_a, 1)
                if on[1]:
                    if later(s, 2):
                        act.wait_ge(y_mm, bb)
                    copy(o_t[:, :, :], B0[:, D:2 * D].rearrange("p (k t) -> p k t", k=2), ot_mm, ot_ok, bb)
                if on[2]:
                    if later(s, 3):
                        act.wait_ge(xy_mm, xx)
                    copy(xo_t[:, :, :], X2[:, D:2 * D].rearrange("p (k t) -> p k t", k=KT), xot_mm, xot_ok, xx)

            over_chunks(act, step)

            def group(d, j):
                g = d * GPL + j
                for f in range(FT):
                    n = g * FT + f
                    act.wait_ge(up_mm, n + 1)
                    if later(n, 2):
                        act.wait_ge(h_ok, n - 1)
                    act.activation(h_a[:, f % 2, :], bank[2 + f % 4][:, 0:GS], ACT.Silu).then_inc(silu_ok, 1)

            over_groups(act, group)

        @block.vector
        def _(dve):
            dve.memset(q_z[:, :, :, :], 0.0).then_inc(halves_zeroed, 1)
            dve.memset(p_z[:, :, :], 0.0).then_inc(halves_zeroed, 1)
            dve.wait_ge(ctx_landed, 48)
            dve.tensor_copy(kp[:, :, :], kp_i[:, :].rearrange("p (b k) -> p b k", b=B)).then_inc(small_made, 1)
            dve.tensor_copy(qp[:, :], qp_i[:, :]).then_inc(small_made, 1)
            dve.wait_ge(w_landed, 16 * 12)
            for k in range(KT):
                dve.tensor_scalar(wo_s[:, k, :], wo_raw[:, k, :], gn[:, 0:1], None, ALU.mult).then_inc(small_made, 1)
            dve.wait_ge(consts_step, CONSTS)
            dve.wait_ge(ctx_mm, 1)
            dve.tensor_copy(k_all[:, :, :].rearrange("p k n -> p (k n)")[:, 0:512], F0).then_inc(small_made, 1)
            dve.tensor_copy(k_all[:, :, :].rearrange("p k n -> p (k n)")[:, 512:1024], F1).then_inc(k_made, 1)
            for b in range(B):
                if b:
                    dve.wait_ge(ctx_mm, 1 + b)
                for k in range(KT):
                    dve.tensor_copy(ctx2[:, k, :, :],
                                    ctx_s[:, k, b * KL:(b + 1) * KL].rearrange("p (a k) -> p a k", a=1)
                                    .to_broadcast([P, 2, KL])).then_inc(ctx_doubled, 1)
                dve.wait_ge(ctx_mm, 2 + b)
                dve.tensor_tensor(
                    v_all[:, b, :, :, :], F2[:, 0:D].rearrange("p (j i d) -> p j i d", j=PAIRS, i=2),
                    pair_of[:, :].rearrange("p (a i b) -> p a i b", a=1, b=1).to_broadcast([P, PAIRS, 2, XD]),
                    ALU.mult).then_inc(v_made, 1)

            def hold():
                dve.memset(idle_v[:, :], 0.0)

            def stats(n, src, st, mv, var, stats_s, vared_s, normed_s, first):
                if not first:
                    dve.wait_ge(normed_s, n)
                dve.bn_stats(st[:, :], src).then_inc(stats_s, 1)
                dve.wait_ge(stats_s, 2 * n + 1)
                hold()
                dve.bn_aggr(mv[:, :], st[:, :]).then_inc(stats_s, 1)
                dve.wait_ge(stats_s, 2 * n + 2)
                dve.tensor_scalar(var[:, :], mv[:, 1:2], EPS, None, ALU.add).then_inc(vared_s, 1)

            def normed(n, src, dst, mv, rstd, rstded_s, normed_s):
                dve.wait_ge(rstded_s, n + 1)
                dve.tensor_scalar(dst, src, mv[:, 0:1], rstd[:, 0:1], ALU.subtract, ALU.mult).then_inc(normed_s, 1)

            def wide(t, n):
                return t.rearrange("p (h a) -> p h a", a=1).to_broadcast([P, t.shape[1], n])

            def step(b, c, on):
                s = b * CPB + c
                f, bb, xx, rr = (s - g for g in range(4))
                fp, bp, xp, rp = (c % 2, (c - 1) % 2, (c - 2) % 2, (c - 3) % 2)
                if on[0]:
                    dve.wait_ge(x_landed[c], b * 16 + 16)
                    stats(f, xin[:, c, :], f_st, f_mv, f_var, f_stats, f_vared, f_normed,
                          not later(s, 1))
                if on[2]:
                    dve.wait_ge(x1_ok, xx + 1)
                    stats(xx, x1[:, xp, :], x_st, x_mv, x_var, x_stats, x_vared, x_normed,
                          not later(s, 3))
                if on[3]:
                    dve.wait_ge(x2_made, rr + 1)
                    stats(rr, r_x[:, rp, :], r_st, r_mv, r_var, r_stats, r_vared, r_normed,
                          not later(s, 4))
                if on[1]:
                    dve.wait_ge(l_mm, bb + 1)
                    if later(s, 2):
                        dve.wait_ge(lgd_ok, bb)
                    dve.tensor_tensor(lg[:, :, :], B0[:, 0:D].rearrange("p (h m) -> p h m", h=H),
                                      up[:, bp, :].rearrange("p (h m) -> p h m", h=H), ALU.mult).then_inc(lg_ok, 1)
                    dve.wait_ge(lg_ok, bb + 1)
                    dve.tensor_reduce(lg_m[:, :], lg[:, :, :], AX.X, ALU.max).then_inc(lgm_ok, 1)
                    dve.wait_ge(lgm_ok, bb + 1)
                    if later(s, 2):
                        dve.wait_ge(be_ok, bb)
                    dve.tensor_tensor(lg_d[:, :, :], lg[:, :, :], wide(lg_m[:, :], M), ALU.subtract)\
                       .then_inc(lgd_ok, 1)
                if on[0]:
                    if later(s, 1):
                        dve.wait_ge(f_xnt_mm, f)
                    normed(f, xin[:, c, :], f_xn[:, :], f_mv, f_rstd, f_rstded, f_normed)
                if on[2]:
                    if later(s, 3):
                        dve.wait_ge(x_xnt_mm, xx)
                    normed(xx, x1[:, xp, :], x_xn[:, :], x_mv, x_rstd, x_rstded, x_normed)
                if on[3]:
                    if later(s, 5):
                        for k in range(2):
                            dve.wait_ge(sent[2 * rp + k], (rr - 2 - rp) * 8 + 16)
                        dve.wait_ge(r_xnt_mm, rr - 1)
                    normed(rr, r_x[:, rp, :], r_xn[:, rp, :], r_mv, r_rstd, r_rstded, r_normed)
                if on[2]:
                    dve.wait_ge(mask_landed[xp], (s - 2 - xp) * 8 + 16)
                    if later(s, 3):
                        dve.wait_ge(dist_ok, xx)
                    dve.tensor_scalar(hid[:, :], mask_i[:, xp, :], 0.0, -HIDDEN, ALU.is_equal, ALU.mult)\
                       .then_inc(hid_ok, 1)
                    dve.wait_ge(hid_ok, xx + 1)
                    if later(s, 3):
                        dve.wait_ge(bias_ok, xx)
                    dve.scalar_tensor_tensor(
                        out=dist[:, :], in0=kp[:, bass.ds(b + (c - 2) // CPB, 1), :].rearrange("p a k -> p (a k)"),
                        scalar=qp[:, bass.ds(xx, 1)], in1=hid[:, :], op0=ALU.subtract, op1=ALU.add)\
                       .then_inc(dist_ok, 1)
                if on[1]:
                    dve.wait_ge(be_ok, bb + 1)
                    if later(s, 2):
                        dve.wait_ge(brec_ok, bb)
                    dve.tensor_reduce(b_sum[:, :], b_e[:, :, :], AX.X, ALU.add).then_inc(bsum_ok, 1)
                    dve.wait_ge(bsum_ok, bb + 1)
                    if later(s, 2):
                        dve.wait_ge(bw_ok, bb)
                    dve.reciprocal(b_rec[:, :], b_sum[:, :]).then_inc(brec_ok, 1)
                if on[0]:
                    dve.wait_ge(fl_done, f + 1)
                    dve.wait_ge(v_ok, f + 1)
                    if later(s, 2):
                        dve.wait_ge(gsum_mm, f)
                    dve.scalar_tensor_tensor(out=g_s[:, fp, :], in0=F1[:, D:2 * D], scalar=0.0, in1=f_l[:, :],
                                             op0=ALU.min, op1=ALU.subtract).then_inc(g_ok, 1)
                if on[3]:
                    dve.wait_ge(rlg_mm, rr + 1)
                    if later(s, 4):
                        dve.wait_ge(topi_ok, rr)
                    dve.tensor_scalar(r_lg[:, :], B1[:, D:D + E], -CLAMP, CLAMP, ALU.max, ALU.min)\
                       .then_inc(rlg_ok, 1)
                    dve.wait_ge(rlg_ok, rr + 1)
                    hold()
                    dve.max(top[:, :], r_lg[:, :]).then_inc(route_step, 1)
                    dve.wait_ge(route_step, rr * ROUTE_STEPS + 1)
                    hold()
                    dve.max_index(top_i[:, :], top[:, :], r_lg[:, :]).then_inc(topi_ok, 1)
                    dve.tensor_scalar(gap[:, :], top[:, 1:2], top[:, 0:1], None, ALU.subtract).then_inc(gap_ok, 1)
                    dve.wait_ge(topi_ok, rr + 1)
                    if later(s, 4):
                        dve.wait_ge(slots_ok, rr)
                    dve.tensor_copy(top_f[:, :], top_i[:, 0:2]).then_inc(route_step, 1)
                    dve.wait_ge(route_step, rr * ROUTE_STEPS + 2)
                    for k in range(2):
                        dve.tensor_scalar(hot[:, k, :], expert_no[:, :], top_f[:, k:k + 1], None, ALU.is_equal)\
                           .then_inc(route_step, 1)
                    dve.wait_ge(route_step, rr * ROUTE_STEPS + 4)
                    dve.tensor_tensor(both[:, :], hot[:, 0, :], hot[:, 1, :], ALU.add).then_inc(both_ok, 1)
                if on[0]:
                    dve.wait_ge(sig_done, f + 1)
                    if later(s, 2):
                        dve.wait_ge(l_mm, f - 1)
                    for i in range(2):
                        rows = slice(M * i, M * i + M)
                        dve.tensor_tensor(q_z[rows, fp, i::2, :], F0[rows, 0:D].rearrange("p (k t) -> p k t", k=2),
                                          qk_s[rows, 0:D].rearrange("p (k t) -> p k t", k=2), ALU.mult)\
                           .then_inc(qk_ok, 1)
                    if later(s, 1):
                        dve.wait_ge(st_mm, f)
                    dve.tensor_tensor(k_s[:, :], F0[:, D:2 * D], qk_s[:, D:2 * D], ALU.mult).then_inc(qk_ok, 1)
                if on[2]:
                    dve.wait_ge(bias_ok, xx + 1)
                    dve.wait_ge(sc_mm, xx + 1)
                    if later(s, 3):
                        dve.wait_ge(ex_ok, xx)
                    for h, xb in enumerate((X0, X1)):
                        dve.tensor_tensor(sc[:, 8 * h:8 * h + 8, :], xb.rearrange("p (h k) -> p h k", h=HPT),
                                          bias[:, 8 * h:8 * h + 8, :], ALU.add).then_inc(sc_ok, 1)
                    dve.wait_ge(sc_ok, 2 * xx + 2)
                    if later(s, 3):
                        dve.wait_ge(scd_ok, xx)
                    dve.tensor_reduce(sc_m[:, :], sc[:, :, :], AX.X, ALU.max).then_inc(scm_ok, 1)
                if on[1]:
                    dve.wait_ge(bt_mm, bb + 1)
                    if later(s, 2):
                        dve.wait_ge(o_mm, bb)
                    dve.tensor_tensor(bt_s[:, :, :], B1.rearrange("p (h t) -> p h t", h=H),
                                      causal[:, :].rearrange("p (a t) -> p a t", a=1).to_broadcast([P, H, P]),
                                      ALU.mult).then_inc(bt_ok, 1)
                if on[0]:
                    dve.wait_ge(less_done, f + 1)
                    dve.wait_ge(down_ok, f + 1)
                    if later(s, 1):
                        dve.wait_ge(st_mm, f)
                    if later(s, 2):
                        dve.wait_ge(l_mm, f - 1)
                    dve.scalar_tensor_tensor(out=s_s[:, fp, :], in0=one_less[:, :], scalar=1.0, in1=down[:, :],
                                             op0=ALU.subtract, op1=ALU.mult, reverse0=True).then_inc(s_ok, 1)
                if on[0]:
                    if later(s, 2):
                        dve.wait_ge(o_mm, f - 1)
                    if later(s, 1):
                        dve.wait_ge(zk_ok, f)
                        dve.wait_ge(zv_ok, f)
                    if c == 0:
                        dve.memset(hk[:, fp, :, :], 0.0).then_inc(hk_ok, 1)
                        dve.memset(hv[:, fp, :, :], 0.0).then_inc(hv_ok, 1)
                    else:
                        dve.wait_ge(decr_ok, f + 1)
                        dve.tensor_tensor(hk[:, fp, :, :], zk[:, :, :],
                                          dec_row[:, :].rearrange("p (k m) -> p k m", k=2), ALU.mult)\
                           .then_inc(hk_ok, 1)
                        dve.wait_ge(decc_ok, f + 1)
                        dve.tensor_tensor(hv[:, fp, :, :], zv[:, :, :], wide(dec_col[:, :], P), ALU.mult)\
                           .then_inc(hv_ok, 1)
                if on[1]:
                    dve.wait_ge(sq_ok, bb + 1)
                    if later(s, 2):
                        dve.wait_ge(rms_step, 2 * bb)
                    dve.tensor_reduce(b_ss[:, :], b_sq[:, :, :], AX.X, ALU.add).then_inc(ss_ok, 1)
                    dve.wait_ge(ss_ok, bb + 1)
                    dve.wait_ge(brec_ok, bb + 1)
                    dve.tensor_tensor(b_t1[:, :], b_ss[:, :], b_rec[:, :], ALU.mult).then_inc(rms_step, 1)
                    dve.wait_ge(rms_step, 2 * bb + 1)
                    dve.tensor_tensor(b_t2[:, :], b_t1[:, :], b_rec[:, :], ALU.mult).then_inc(rms_step, 1)
                    dve.wait_ge(rms_step, 2 * bb + 2)
                    dve.tensor_scalar(b_ms[:, :], b_t2[:, :], 1.0 / M, EPS, ALU.mult, ALU.add).then_inc(ms_ok, 1)
                if on[1]:
                    dve.wait_ge(rms_ok, bb + 1)
                    dve.tensor_tensor(b_w[:, :], b_rms[:, :], b_rec[:, :], ALU.mult).then_inc(bw_ok, 1)
                    dve.wait_ge(bw_ok, bb + 1)
                    if later(s, 2):
                        dve.wait_ge(ot_mm, bb)
                    dve.tensor_tensor(b_o[:, :, :], B0[:, 0:D].rearrange("p (h m) -> p h m", h=H), wide(b_w[:, :], M),
                                      ALU.mult).then_inc(bo_ok, 1)
                if on[0]:
                    dve.wait_ge(st_mm, f + 1)
                    dve.wait_ge(hk_ok, f + 1)
                    dve.tensor_tensor(zk[:, :, :], F2[:, 0:D].rearrange("p (k m) -> p k m", k=2), hk[:, fp, :, :],
                                      ALU.add).then_inc(zk_ok, 1)
                    dve.wait_ge(hv_ok, f + 1)
                    dve.tensor_tensor(zv[:, :, :], F2[:, D:2 * D].rearrange("p (k m) -> p k m", k=2), hv[:, fp, :, :],
                                      ALU.add).then_inc(zv_ok, 1)
                    dve.wait_ge(a_mm, f + 1)
                    if later(s, 2):
                        dve.wait_ge(l_mm, f - 1)
                    dve.tensor_tensor(a_s[:, fp, :, :], F1.rearrange("p (h t) -> p h t", h=H),
                                      causal[:, :].rearrange("p (a t) -> p a t", a=1).to_broadcast([P, H, P]),
                                      ALU.mult).then_inc(a_ok, 1)
                if on[2]:
                    dve.wait_ge(ex_ok, xx + 1)
                    if later(s, 3):
                        dve.wait_ge(xden_ok, xx)
                    dve.tensor_reduce(x_sum[:, :], ex[:, :, :], AX.X, ALU.add).then_inc(xsum_ok, 1)
                    dve.wait_ge(et_mm, 2 * xx + 2)
                    if later(s, 3):
                        dve.wait_ge(av_mm, xx)
                    dve.tensor_copy(e_t[:, 4:8, :], X1.rearrange("p (k t) -> p k t", k=4)).then_inc(et_ok_v, 1)
                    dve.wait_ge(xsum_ok, xx + 1)
                    if later(s, 3):
                        dve.wait_ge(xrec_ok, xx)
                    dve.tensor_scalar(x_den[:, :], x_sum[:, :], 1.0, None, ALU.add).then_inc(xden_ok, 1)
                    dve.wait_ge(xden_ok, xx + 1)
                    if later(s, 3):
                        dve.wait_ge(xo_ok, xx)
                    dve.reciprocal(x_rec[:, :], x_den[:, :]).then_inc(xrec_ok, 1)
                if on[3]:
                    dve.wait_ge(cnt_mm, rr + 1)
                    if later(s, 4):
                        dve.wait_ge(taken_ok, rr)
                    dve.tensor_tensor(place[:, :], B1[:, D:D + E], taken[:, :], ALU.add).then_inc(place_ok, 1)
                    dve.wait_ge(place_ok, rr + 1)
                    dve.tensor_tensor(taken[:, :], B1[:, D + E:D + 2 * E], taken[:, :], ALU.add).then_inc(taken_ok, 1)
                    dve.tensor_tensor(place_h[:, :, :], hot[:, :, :],
                                      place[:, :].rearrange("p (a e) -> p a e", a=1).to_broadcast([P, 2, E]),
                                      ALU.mult).then_inc(route_step, 1)
                    dve.tensor_scalar(base[:, :], top_f[:, :], float(CAP), None, ALU.mult).then_inc(route_step, 1)
                    dve.wait_ge(re_ok, rr + 1)
                    dve.tensor_scalar(r_den[:, :], r_e[:, :], 1.0, 1e-12, ALU.add, ALU.add).then_inc(route_step, 1)
                    dve.wait_ge(route_step, rr * ROUTE_STEPS + 5)
                    dve.tensor_reduce(pos[:, :], place_h[:, :, :], AX.X, ALU.add).then_inc(route_step, 1)
                    dve.wait_ge(route_step, rr * ROUTE_STEPS + 7)
                    dve.reciprocal(r_p[:, :], r_den[:, :]).then_inc(route_step, 1)
                    dve.wait_ge(route_step, rr * ROUTE_STEPS + 8)
                    dve.tensor_scalar(off_f[:, :], pos[:, :], float(CAP), SKIPPED, ALU.is_ge, ALU.mult)\
                       .then_inc(route_step, 1)
                    dve.wait_ge(route_step, rr * ROUTE_STEPS + 6)
                    dve.scalar_tensor_tensor(out=slot_f[:, :], in0=pos[:, :], scalar=float(CAP - 1), in1=base[:, :],
                                             op0=ALU.min, op1=ALU.add).then_inc(route_step, 1)
                    dve.wait_ge(route_step, rr * ROUTE_STEPS + 9)
                    dve.tensor_scalar(wgt_all[:, bass.ds(rr, 1), 0:1].rearrange("p a k -> p (a k)"), pos[:, 0:1],
                                      float(CAP), r_p[:, 0:1], ALU.is_lt, ALU.mult)
                    dve.tensor_scalar(kept[:, :], pos[:, 1:2], float(CAP), r_p[:, 0:1], ALU.is_lt, ALU.mult)\
                       .then_inc(route_step, 1)
                    dve.wait_ge(route_step, rr * ROUTE_STEPS + 11)
                    dve.tensor_copy(slot_all[:, bass.ds(rr, 1), :].rearrange("p a k -> p (a k)"), slot_f[:, :])
                    dve.wait_ge(route_step, rr * ROUTE_STEPS + 12)
                    dve.tensor_scalar(wgt_all[:, bass.ds(rr, 1), 1:2].rearrange("p a k -> p (a k)"), kept[:, :],
                                      r_e[:, :], None, ALU.mult)
                    if later(s, 5):
                        for k in range(2):
                            dve.wait_ge(sent[2 * rp + k], (rr - 2 - rp) * 8 + 16)
                    dve.wait_ge(route_step, rr * ROUTE_STEPS + 10)
                    dve.tensor_tensor(send[:, rp, :], slot_f[:, :], off_f[:, :], ALU.add).then_inc(slots_ok, 1)
                if on[2]:
                    dve.wait_ge(xrec_ok, xx + 1)
                    dve.wait_ge(av_mm, xx + 1)
                    if later(s, 3):
                        dve.wait_ge(xot_mm, xx)
                    dve.tensor_tensor(x_o[:, :, :], X2[:, 0:D].rearrange("p (h d) -> p h d", h=XH),
                                      wide(x_rec[:, :], XD), ALU.mult).then_inc(xo_ok, 1)
                if on[1]:
                    dve.wait_ge(y_mm, bb + 1)
                    if later(s, 3):
                        dve.wait_ge(x2_made, bb - 1)
                    dve.tensor_tensor(x1[:, bp, :], B1[:, 0:D], xin[:, (c - 1) % 4, :], ALU.add).then_inc(x1_ok, 1)
                if on[2]:
                    dve.wait_ge(xy_mm, xx + 1)
                    if later(s, 4):
                        dve.wait_ge(x2_kept, xx - 1)
                    dve.tensor_tensor(r_x[:, xp, :], X2[:, 0:D], x1[:, xp, :], ALU.add).then_inc(x2_made, 1)

            over_chunks(dve, step)

            def columns(g, par):
                dve.wait_ge(xet_mm, g + 1)
                if later(g, 2):
                    dve.wait_ge(up_mm, (g - 1) * FT)
                dve.tensor_copy(xe_t[:, par, :, :, :].rearrange("p k a t -> p (k a t)"), bank[0][:, :]).then_inc(xet_ok, 1)

            def gated(g, par):
                for f in range(FT):
                    n = g * FT + f
                    dve.wait_ge(silu_ok, n + 1)
                    if f == 0 and later(g, 2):
                        dve.wait_ge(dn_mm, g - 1)
                    dve.tensor_tensor(h_t[:, par, f, :], bank[2 + f % 4][:, GS:2 * GS], h_a[:, f % 2, :], ALU.mult)\
                       .then_inc(h_ok, 1)

            def results(g, par):
                dve.wait_ge(dn_mm, g + 1)
                if later(g, 2):
                    dve.wait_ge(y_stored[par], (g - 2 - par) * 8 + 16)
                dve.tensor_copy(y_s[:, par, :, :].rearrange("p a d -> p (a d)"), bank[6 + par][:, :]).then_inc(y_ok, 1)

            columns(0, 0)

            def group(d, j):
                g, par = d * GPL + j, j % 2
                gated(g, par)
                if not is_last(g, NG - 1):
                    columns(g + 1, 1 - par)
                if later(g, 1):
                    results(g - 1, 1 - par)

            over_groups(dve, group)
            results(NG - 1, 1)

            def indices(n, par):
                if not isinstance(n, int):
                    dve.wait_ge(gathered[par], (n - par) * 16)
                dve.tensor_copy(c_i[:, par, :], slot_all[:, bass.ds(n, 1), :].rearrange("p a k -> p (a k)"))\
                   .then_inc(ci_ok, 1)

            def combine(n, par):
                dve.wait_ge(gathered[par], (n - par) * 16 + 32)
                dve.scalar_tensor_tensor(
                    out=c_1[:, par, :], in0=c_y[:, par, 0, :],
                    scalar=wgt_all[:, bass.ds(n, 1), 0:1].rearrange("p a k -> p (a k)"),
                    in1=x2_all[:, bass.ds(n, 1), :].rearrange("p a d -> p (a d)"), op0=ALU.mult, op1=ALU.add)\
                   .then_inc(c1_ok, 1)
                dve.wait_ge(c1_ok, n + 1)
                if not isinstance(n, int):
                    dve.wait_ge(stored[par], (n - par) * 8)
                dve.scalar_tensor_tensor(
                    out=c_o[:, par, :], in0=c_y[:, par, 1, :],
                    scalar=wgt_all[:, bass.ds(n, 1), 1:2].rearrange("p a k -> p (a k)"),
                    in1=c_1[:, par, :], op0=ALU.mult, op1=ALU.add).then_inc(co_ok, 1)

            dve.wait_ge(x2_kept, NCH)
            indices(0, 0)
            indices(1, 1)
            for n in range(2):
                combine(n, n)
            with dve.Fori(1, NCH // 2) as d:
                for par in range(2):
                    indices(d * 2 + par, par)
                for par in range(2):
                    combine(d * 2 + par, par)

        @block.tensor
        def _(pe):
            def flip(dst, tiles, done):
                for i, t in enumerate(tiles):
                    last = pe.transpose(dst[:, i * P:(i + 1) * P], t, ident[:, :])
                last.then_inc(done, 1)

            def product(dst, pairs):
                for i, (lhs, rhs) in enumerate(pairs):
                    last = pe.matmul(dst, lhs, rhs, start=(i == 0), stop=(i == len(pairs) - 1))
                return last

            def halves(t):
                return [t[:, k * P:(k + 1) * P] for k in range(2)]

            pe.wait_ge(consts_step, CONSTS)
            pe.wait_ge(w_landed, 16 * 12)
            pe.wait_ge(ctx_landed, 48)
            for m in range(KT):
                last = product((F0, F1)[m], [(xw[:, 1, k, m * P:(m + 1) * P], ctx_s[:, k, :]) for k in range(KT)])
            last.then_inc(ctx_mm, 1)
            for b in range(B):
                pe.wait_ge(ctx_doubled, 2 * b + 2)
                if b:
                    pe.wait_ge(v_made, b)
                product(F2[:, 0:D], [(ctx2[:, k, :, :].rearrange("p a k -> p (a k)"), xw[:, 2, k, :])
                                     for k in range(KT)]).then_inc(ctx_mm, 1)
            pe.wait_ge(k_made, 1)
            pe.wait_ge(v_made, B)

            def step(b, c, on):
                s = b * CPB + c
                f, bb, xx, rr = (s - g for g in range(4))
                fp, bp, xp, rp = (c % 2, (c - 1) % 2, (c - 2) % 2, (c - 3) % 2)
                if on[1]:
                    pe.wait_ge(a_ok, bb + 1)
                    pe.wait_ge(s_ok, bb + 1)
                    pe.wait_ge(hk_ok, bb + 1)
                    if later(s, 2):
                        pe.wait_ge(ot_ok, bb)
                    for h in range(H):
                        cols = slice(h * M, (h + 1) * M)
                        last = product(B0[:, cols], [
                            (a_s[:, bp, h, :], s_s[:, bp, cols]),
                            (q_z[:, bp, h, :], hk[:, bp, h // 2, (h % 2) * M:(h % 2 + 1) * M])])
                    last.then_inc(l_mm, 1)
                if on[0]:
                    pe.wait_ge(f_normed, f + 1)
                    if later(s, 1):
                        pe.wait_ge(zk_ok, f)
                        pe.wait_ge(zv_ok, f)
                    flip(F2, halves(f_xn), f_xnt_mm)
                if on[2]:
                    pe.wait_ge(x_normed, xx + 1)
                    if later(s, 3):
                        pe.wait_ge(x2_made, xx)
                    flip(X2, halves(x_xn), x_xnt_mm)
                if on[3]:
                    pe.wait_ge(r_normed, rr + 1)
                    pe.wait_ge(x1_ok, min(rr + 2, NCH) if isinstance(rr, int) else rr + 2)
                    if later(s, 4):
                        pe.wait_ge(taken_ok, rr)
                    flip(B1[:, D:2 * D], halves(r_xn[:, rp, :]), r_xnt_mm)
                if on[0]:
                    pe.wait_ge(f_xnt_ok, f + 1)
                    if later(s, 1):
                        pe.wait_ge(kst_ok, f)
                        pe.wait_ge(a_ok, f)
                    for m in range(2):
                        product(F0[:, m * P:(m + 1) * P],
                                [(w_in[:, k, m * P:(m + 1) * P], f_xnt[:, k, :]) for k in range(KT)])
                    product(F0[:, D:2 * D], [(f_xnt[:, k, :], w_in[:, k, D:2 * D]) for k in range(KT)])
                    product(F1, [(f_xnt[:, k, :], w_in[:, k, 2 * D:4 * D]) for k in range(KT)]).then_inc(proj_mm, 1)
                if on[2]:
                    pe.wait_ge(x_xnt_ok, xx + 1)
                    if later(s, 3):
                        pe.wait_ge(xot_ok, xx)
                    for m in range(2):
                        last = product(X2[:, D + m * P:D + (m + 1) * P],
                                       [(xw[:, 0, k, m * P:(m + 1) * P], x_xnt[:, k, :]) for k in range(KT)])
                    last.then_inc(xq_mm, 1)
                if on[3]:
                    pe.wait_ge(r_xnt_ok, rr + 1)
                    product(B1[:, D:D + E], [(r_xnt[:, k, :], wr_s[:, k, :]) for k in range(KT)]).then_inc(rlg_mm, 1)
                if on[2]:
                    pe.wait_ge(xq_ok, xx + 1)
                    pe.wait_ge(kbd_ok, (b + (c - 2) // CPB) * 2 + 2)
                    if later(s, 3):
                        pe.wait_ge(et_ok_a, xx)
                        pe.wait_ge(et_ok_v, xx)
                    for k, xb in enumerate((X0, X1)):
                        last = product(xb, [(xq_t[:, k, :], k_bd[:, k, :, :].rearrange("p h k -> p (h k)"))])
                    last.then_inc(sc_mm, 1)
                if on[1]:
                    pe.wait_ge(bp_ok, bb + 1)
                    flip(B0[:, D:2 * D], halves(b_p), pt_mm)
                if on[0]:
                    pe.wait_ge(g_ok, f + 1)
                    product(F2[:, 0:D], [(tri_half[:, :], g_s[:, fp, :])])
                    now_last = [fp] if c == 0 else [fp, 1 - fp]
                    product(F2[:, D:2 * D], [(half[:, :], g_s[:, i, :]) for i in now_last])
                    pe.wait_ge(qk_ok, 3 * f + 3)
                    for m in range(2):
                        last = product(F0[:, m:m + 1], [(g_s[:, i, m * P:(m + 1) * P], half[:, 0:1]) for i in now_last])
                    last.then_inc(gsum_mm, 1)
                if on[1]:
                    pe.wait_ge(pt_ok, 2 * bb + 2)
                    if on[3]:
                        pe.wait_ge(rlg_ok, rr + 1)
                    if later(s, 2):
                        pe.wait_ge(x1_ok, bb)
                    for h in range(H):
                        last = product(B1[:, h * P:(h + 1) * P], [(ks_t[:, bp, 2 + h // 2, :], p_z[:, h, :])])
                    last.then_inc(bt_mm, 1)
                if on[0]:
                    pe.wait_ge(s_ok, f + 1)
                    pe.wait_ge(decc_ok, f + 1)
                    flip(F0, halves(k_s) + halves(s_s[:, fp, :]), kst_mm)
                if on[2]:
                    pe.wait_ge(ex_ok, xx + 1)
                    for k, xb in enumerate((X0, X1)):
                        flip(xb, [ex[:, 8 * k + 2 * j:8 * k + 2 * j + 2, :].rearrange("p h k -> p (h k)")
                                  for j in range(4)], et_mm)
                if on[1]:
                    pe.wait_ge(bt_ok, bb + 1)
                    pe.wait_ge(lg_ok, bb + 1)
                    pe.wait_ge(hv_ok, bb + 1)
                    pe.wait_ge(v_ok, bb + 1)
                    for h in range(H):
                        cols = slice(h * M, (h + 1) * M)
                        last = product(B0[:, cols], [
                            (bt_s[:, h, :], v_s[:, bp, cols]),
                            (p_z[:, h, :], hv[:, bp, h // 2, (h % 2) * M:(h % 2 + 1) * M])])
                    last.then_inc(o_mm, 1)
                if on[0]:
                    pe.wait_ge(v_ok, f + 1)
                    pe.wait_ge(up_ok, f + 1)
                    pe.wait_ge(down_ok, f + 1)
                    pe.wait_ge(decr_ok, f + 1)
                    for m in range(2):
                        cols = slice(m * P, (m + 1) * P)
                        product(F2[:, m * P:(m + 1) * P], [(k_s[:, cols], s_s[:, fp, cols])])
                        last = product(F2[:, D + m * P:D + (m + 1) * P], [(s_s[:, fp, cols], v_s[:, fp, cols])])
                    last.then_inc(st_mm, 1)
                    pe.wait_ge(kst_ok, f + 1)
                    for h in range(H):
                        last = product(F1[:, h * P:(h + 1) * P], [(ks_t[:, fp, h // 2, :], q_z[:, fp, h, :])])
                    last.then_inc(a_mm, 1)
                if on[3]:
                    pe.wait_ge(both_ok, rr + 1)
                    if on[1]:
                        pe.wait_ge(bt_ok, bb + 1)
                    product(B1[:, D:D + E], [(before[:, :], both[:, :])])
                    product(B1[:, D + E:D + 2 * E], [(ones[:, :], both[:, :])]).then_inc(cnt_mm, 1)
                if on[2]:
                    pe.wait_ge(et_ok_a, xx + 1)
                    pe.wait_ge(et_ok_v, xx + 1)
                    pe.wait_ge(vbd_ok, (b + (c - 2) // CPB) + 1)
                    for j in range(PAIRS):
                        last = product(X2[:, j * 2 * XD:(j + 1) * 2 * XD], [(e_t[:, j, :], v_bd[:, j, :])])
                    last.then_inc(av_mm, 1)
                if on[1]:
                    pe.wait_ge(bo_ok, bb + 1)
                    flip(B0[:, D:2 * D], halves(b_o[:, :, :].rearrange("p h m -> p (h m)")), ot_mm)
                    pe.wait_ge(ot_ok, bb + 1)
                    if on[3]:
                        pe.wait_ge(taken_ok, rr + 1)
                    product(B1[:, 0:D], [(o_t[:, k, :], wo_s[:, k, :]) for k in range(2)]).then_inc(y_mm, 1)
                if on[2]:
                    pe.wait_ge(xo_ok, xx + 1)
                    flip(X2[:, D:2 * D], halves(x_o[:, :, :].rearrange("p h d -> p (h d)")), xot_mm)
                    pe.wait_ge(xot_ok, xx + 1)
                    product(X2[:, 0:D], [(xo_t[:, k, :], xw[:, 3, k, :]) for k in range(KT)]).then_inc(xy_mm, 1)

            over_chunks(pe, step)

            def columns(g, par):
                pe.wait_ge(xe_landed[par], (g - par) * 8 + 16)
                if later(g, 1):
                    pe.wait_ge(xet_ok, g)
                flip(bank[0], [xe[:, par, a, k * P:(k + 1) * P] for k in range(KT) for a in range(2)], xet_mm)

            def hidden(g, j):
                par, w = j % 2, j // GPE
                pe.wait_ge(xet_ok, g + 1)
                for f in range(FT):
                    n = g * FT + f
                    if later(n, 4):
                        pe.wait_ge(h_ok, n - 3)
                    to = bank[2 + f % 4]
                    for i, wt in enumerate((w1_s, w3_s)):
                        last = product(to[:, i * GS:(i + 1) * GS], [
                            (wt[w][:, k, f * P:(f + 1) * P], xe_t[:, par, k, :, :].rearrange("p a t -> p (a t)"))
                            for k in range(KT)])
                    last.then_inc(up_mm, 1)

            def results(d, j):
                g, par, w = d * GPL + j, j % 2, (j // GPE) % 2
                pe.wait_ge(h_ok, g * FT + FT)
                pe.wait_ge(wdn_landed[w], (d + j // GPL) * 16 + 16)
                if later(g, 2):
                    pe.wait_ge(y_ok, g - 1)
                for a in range(2):
                    last = product(bank[6 + par][:, a * D:(a + 1) * D],
                                   [(h_t[:, par, f, a * P:(a + 1) * P], w2_s[w][:, f, :]) for f in range(FT)])
                last.then_inc(dn_mm, 1)

            def group(d, j):
                g = d * GPL + j
                if not is_last(g, NG - 1):
                    columns(g + 1, 1 - j % 2)
                if j % GPE == 0:
                    pe.wait_ge(wup_landed[j // GPE], d * 32 + 32)
                hidden(g, j)
                if later(g, 1):
                    results(d, j - 1)

            columns(0, 0)
            over_groups(pe, group)
            results(E // 2 - 1, GPL - 1)


def kernel(x, ctx_1024, itok_BxS_8_8191, itok_BxS2_1_8191, mask_BxSxS2_if1, L0_attn_Wq, L0_attn_Wk, L0_attn_Wv,
           L0_attn_Wf, L0_attn_g_norm_w, L0_attn_Wo, L0_xattn_W_q, L0_xattn_W_k, L0_xattn_W_v, L0_xattn_W_o,
           L0_ffn_Wr, L0_ffn_W1, L0_ffn_W3, L0_ffn_W2):
    import concourse.bacc as bacc
    from concourse.bass_utils import run_bass_kernel_spmd

    laid_out = {
        "x": x, "qpos": itok_BxS_8_8191.reshape(NCH, P).T, "kpos": itok_BxS2_1_8191, "mask": mask_BxSxS2_if1,
        "ctx_t": ctx_1024.reshape(B * KL, D).T, "wq": L0_attn_Wq, "wk": L0_attn_Wk, "wv": L0_attn_Wv,
        "wf": L0_attn_Wf, "gnorm": L0_attn_g_norm_w, "wo": L0_attn_Wo, "xwq_t": L0_xattn_W_q.T,
        "xwk_t": L0_xattn_W_k.T, "xwv_t": L0_xattn_W_v.T, "xwo_t": L0_xattn_W_o.T, "wr": L0_ffn_Wr,
        "w1": L0_ffn_W1, "w3": L0_ffn_W3, "w2": L0_ffn_W2,
    }
    nc = bacc.Bacc("TRN2", target_bir_lowering=False, num_devices=1)
    arrays, args = {}, []
    for name, a in laid_out.items():
        a = np.ascontiguousarray(a)
        arrays[f"in_{name}"] = a
        args.append(nc.dram_tensor(f"in_{name}", a.shape, mybir.dt.from_np(a.dtype), kind="ExternalInput").ap())
    args.append(nc.dram_tensor("out_dram", (B, T, D), F32, kind="ExternalOutput").ap())
    decoder_layer(nc, *args)
    return run_bass_kernel_spmd(nc, [arrays], core_ids=[0]).results[0]["out_dram"]
```

```python
from contextlib import ExitStack

import concourse.bass as bass
import numpy as np
from concourse import mybir

ALU = mybir.AluOpType
ACT = mybir.ActivationFunctionType
AX = mybir.AxisListType
F32 = mybir.dt.float32
I32 = mybir.dt.int32
U32 = mybir.dt.uint32
BF16 = mybir.dt.bfloat16

P = 128
B, T, D = 8, 512, 256
NCH = B * T // P
CPB = T // P
KT = D // P
H, M = 4, 64
GATE_NORM = 8.0
EPS = 1e-5
XH, XD, KL = 16, 16, 64
HPT = P // XD
PAIRS = XH // 2
VW = 2 * XD + 2
XSCALE = 1.0 / 4.0
HIDDEN = 1.0e38
E, F, TOPK = 8, 1024, 2
CAP = -(-B * T * TOPK * 5 // (4 * E))
SLOTS = E * CAP
GS = 256
GPE = CAP // GS
NG = E * GPE
GPL = 2 * GPE
FT = F // P
CLAMP = 10000.0
X2_LAG = 3
LAGS = 4
ROW = D + 2
SPARE = B * T
ROUTE_STEPS = 11
SPACE = 18936
SLOPE = [float(v) for v in np.float32(2.0 ** (-8.0 / XH)) ** np.arange(1, XH + 1, dtype=np.float32)]
SKIPPED = float(4 * SLOTS)


def decoder_layer(nc, x, qpos, kpos, mask, ctx_t, wq, wk, wv, wf, gnorm, wo,
                  xwq_t, xwk_t, xwv_t, xwo_t, wr, w1, w3, w2, out):
    xe_dram = nc.dram_tensor("expert_rows", (SLOTS, ROW), F32, kind="Internal").ap()
    ctx = ExitStack()
    with ctx:
        def sb(name, shape, dt=F32):
            return ctx.enter_context(nc.sbuf_tensor(name, shape, dt))

        def sem(name):
            return ctx.enter_context(nc.semaphore(name))

        ident = sb("ident", [P, P])
        causal = sb("causal", [P, P])
        tri_half = sb("tri_half", [P, P])
        half = sb("half", [P, P])
        ones = sb("ones", [P, P])
        before = sb("before", [P, P], BF16)
        all_b = sb("all_b", [P, P], BF16)
        diag16 = sb("diag16", [P, HPT])
        pair_of = sb("pair_of", [P, 2])
        slopes = sb("slopes", [P, XH])
        expert_no = sb("expert_no", [P, E])
        neg_half = sb("neg_half", [P, 4])
        w_in = sb("w_in", [P, KT, 4 * D])
        wo_raw = sb("wo_raw", [P, KT, D])
        gn = sb("gn", [P, 1])
        wo_s = sb("wo_s", [P, KT, D])
        xw = sb("xw", [P, 4, KT, D])
        wr_s = sb("wr_s", [P, KT, E])
        ctx_s = sb("ctx_s", [P, KT, B * KL])
        ctx2 = sb("ctx2", [P, KT, 2, KL])
        kp_i = sb("kp_i", [P, B * KL], I32)
        kp = sb("kp", [P, B, KL])
        qp_i = sb("qp_i", [P, NCH], I32)
        qp = sb("qp", [P, NCH])
        token_no = sb("token_no", [P, NCH])
        empty = sb("empty", [P, ROW])
        k_all = sb("k_all", [P, KT, B * KL])
        v_all = sb("v_all", [P, B, PAIRS, VW])
        idle_v, idle_g = sb("idle_v", [P, 1]), sb("idle_g", [P, 2])
        space = sb("space", [P, SPACE])
        used = [0, 0]

        def carve(which, shape):
            n = int(np.prod(shape[1:]))
            at = used[which]
            used[which] += n
            flat = space[:, at:at + n]
            if len(shape) == 2:
                return flat
            names = " ".join("abce"[:len(shape) - 1])
            return flat.rearrange(f"p ({names}) -> p {names}", **dict(zip("abce", shape[1:])))

        def lane(name, shape):
            return carve(0, shape)

        def later_use(name, shape):
            return carve(1, shape)

        xin = lane("xin", [P, 4, D])
        f_st, f_mv, f_var, f_rstd = (lane(t, [P, w]) for t, w in (("f_st", 6), ("f_mv", 2), ("f_var", 1), ("f_rstd", 1)))
        f_xn = lane("f_xn", [P, D])
        f_xnt = lane("f_xnt", [P, KT, P])
        qk_e, qk_l, qk_s = (lane(t, [P, 2 * D]) for t in ("qk_e", "qk_l", "qk_s"))
        q_z = lane("q_z", [P, H, P])
        k_s, v_s = lane("k_s", [P, D]), lane("v_s", [P, D])
        f_abs, f_e, f_l = (lane(t, [P, D]) for t in ("f_abs", "f_e", "f_l"))
        g_s = lane("g_s", [P, 2, D])
        one_less = lane("one_less", [P, D])
        up, down = lane("up", [P, D]), lane("down", [P, D])
        decay = lane("decay", [P, D])
        s_s = lane("s_s", [P, D])
        ks_t = lane("ks_t", [P, 4, P])
        a_s = lane("a_s", [P, H, P])
        zk, zv = lane("zk", [P, 2, P]), lane("zv", [P, 2, P])
        hk, hv = lane("hk", [P, 2, P]), lane("hv", [P, 2, P])
        lg, lg_d, b_e = (lane(t, [P, H, M]) for t in ("lg", "lg_d", "b_e"))
        lg_m, b_sum, b_rec, b_ss, b_t1, b_t2, b_ms, b_rms, b_w = (
            lane(t, [P, H]) for t in ("lg_m", "b_sum", "b_rec", "b_ss", "b_t1", "b_t2", "b_ms", "b_rms", "b_w"))
        b_p = lane("b_p", [P, D])
        p_z = lane("p_z", [P, H, P])
        bt_s = lane("bt_s", [P, H, P])
        b_sq, b_o = lane("b_sq", [P, H, M]), lane("b_o", [P, H, M])
        o_t = lane("o_t", [P, 2, P])
        x1 = lane("x1", [P, 2, D])
        x_st, x_mv, x_var, x_rstd = (lane(t, [P, w]) for t, w in (("x_st", 6), ("x_mv", 2), ("x_var", 1), ("x_rstd", 1)))
        x_xn = lane("x_xn", [P, D])
        x_xnt, xq_t = lane("x_xnt", [P, KT, P]), lane("xq_t", [P, KT, P])
        k_bd = lane("k_bd", [P, KT, HPT, KL])
        v_bd = lane("v_bd", [P, PAIRS, VW])
        mask_i = sb("mask_i", [P, 2, KL], I32)
        hid, dist = lane("hid", [P, KL]), lane("dist", [P, KL])
        bias, sc, ex = (lane(t, [P, XH, KL]) for t in ("bias", "sc", "ex"))
        sc_m, x_den, x_rec = (lane(t, [P, XH]) for t in ("sc_m", "x_den", "x_rec"))
        e_t = lane("e_t", [P, PAIRS, P])
        x_o = lane("x_o", [P, PAIRS, 2 * XD])
        xo_t = lane("xo_t", [P, KT, P])
        r_st, r_mv, r_var, r_rstd = sb("r_st", [P, 6]), sb("r_mv", [P, 2]), sb("r_var", [P, 1]), sb("r_rstd", [P, 1])
        x2 = sb("x2", [P, 2, D])
        r_xn = sb("r_xn", [P, 2, 2, ROW])
        r_xnt = sb("r_xnt", [P, KT, P])
        r_lg, top, top_i = sb("r_lg", [P, E]), sb("top", [P, 8]), sb("top_i", [P, 8], U32)
        top_f = sb("top_f", [P, 2])
        hot = sb("hot", [P, 2, E])
        both = sb("both", [P, E], BF16)
        taken = sb("taken", [P, E])
        place = sb("place", [P, E])
        place_h = sb("place_h", [P, 2, E])
        pos = sb("pos", [P, 2])
        base = sb("base", [P, 2])
        slot_f, off_f = sb("slot_f", [P, 2]), sb("off_f", [P, 2])
        send = sb("send", [P, 2, 2], U32)
        gap, r_e, r_den, r_p = sb("gap", [P, 1]), sb("r_e", [P, 1]), sb("r_den", [P, 1]), sb("r_p", [P, 1])
        w1_s = [sb("w1_even", [P, KT, F]), later_use("w1_odd", [P, KT, F])]
        w3_s = [sb("w3_even", [P, KT, F]), later_use("w3_odd", [P, KT, F])]
        w2_s = [sb("w2_even", [P, FT, D]), later_use("w2_odd", [P, FT, D])]
        xe = later_use("xe", [P, 2, 2, ROW])
        about = sb("about", [P, 2, 2, 2])
        token = [[sb(f"token{i}{a}", [P, 1], U32) for a in range(2)] for i in range(2)]
        xe_t = later_use("xe_t", [P, 2, KT, 2, P])
        h_a = later_use("h_a", [P, 2, GS])
        h_t = later_use("h_t", [P, 2, FT, GS])
        y_s = later_use("y_s", [P, 2, 2, D])

        assert max(used) == SPACE, used
        bank = [ctx.enter_context(nc.psum_tensor(f"bank{i}", [P, 512], F32)) for i in range(8)]
        turns = [
            [("counts", 4), ("read", 0)],
            [("xo_cols", 3), ("qk", 0), ("scores", 0)],
            [("vf", 0), ("r_cols", 3), ("mix", 0)],
            [("r_logits", 4), ("o_cols", 1), ("ks_cols", 0), ("sums", 0)],
            [("f_cols", 0), ("decay_cols", 0), ("e_cols0", 2), ("values", 2)],
            [("x_scores1", 2), ("gates", 0), ("p_cols", 0)],
            [("x_scores0", 2), ("y", 1), ("e_cols1", 2)],
            [("xy", 3), ("logits", 0), ("x_cols", 1), ("xq", 1)],
        ]
        tile = {t: bank[i][:, :] for i, turn in enumerate(turns) for t, _ in turn}

        consts_made, w_landed, ctx_landed, zeros_sent = sem("consts_made"), sem("w_landed"), sem("ctx_landed"), sem("zeros_sent")
        consts_step = sem("consts_step")
        small_made, ctx_doubled, ctx_mm, v_made = sem("small_made"), sem("ctx_doubled"), sem("ctx_mm"), sem("v_made")
        k_made = sem("k_made")
        x_landed = [sem(f"x_landed{i}") for i in range(4)]
        mask_landed = [sem(f"mask_landed{i}") for i in range(2)]
        def sems(names):
            return [sem(t) for t in names.split()]

        f_stats, f_vared, f_rstded, f_normed, f_cols_mm, f_cols_ok, qk_mm, vf_mm = sems(
            "f_stats f_vared f_rstded f_normed f_cols_mm f_cols_ok qk_mm vf_mm")
        e_ok, l_ok, sig_ok, v_ok, abs_ok, fe_ok, fl_ok, g_ok, qk_ok = sems(
            "e_ok l_ok sig_ok v_ok abs_ok fe_ok fl_ok g_ok qk_ok")
        gates_mm, less_ok, gates_ok, s_ok, decay_mm, h_ok, ks_mm, ks_ok, sums_mm, z_ok, scores_mm, a_ok = sems(
            "gates_mm less_ok gates_ok s_ok decay_mm h_ok ks_mm ks_ok sums_mm z_ok scores_mm a_ok")
        logits_mm, lg_ok, lgm_ok, lgd_ok, be_ok, bsum_ok, brec_ok, bp_ok, p_mm, p_ok, mix_mm, mix_ok = sems(
            "logits_mm lg_ok lgm_ok lgd_ok be_ok bsum_ok brec_ok bp_ok p_mm p_ok mix_mm mix_ok")
        read_mm, sq_ok, rms_step, ms_ok, rms_ok, bw_ok, bo_ok, o_mm, o_ok, y_mm, x1_ok = sems(
            "read_mm sq_ok rms_step ms_ok rms_ok bw_ok bo_ok o_mm o_ok y_mm x1_ok")
        x_stats, x_vared, x_rstded, x_normed, x_cols_mm, x_cols_ok, xq_mm, xq_ok = sems(
            "x_stats x_vared x_rstded x_normed x_cols_mm x_cols_ok xq_mm xq_ok")
        kbd_ok, vbd_ok, hid_ok, dist_ok, bias_ok, xs_mm, sc_ok, scm_ok, scd_ok, ex_ok = sems(
            "kbd_ok vbd_ok hid_ok dist_ok bias_ok xs_mm sc_ok scm_ok scd_ok ex_ok")
        et_mm, et_ok, av_mm, xden_ok, xrec_ok, xo_ok, xot_mm, xot_ok, xy_mm, x2_ok = sems(
            "et_mm et_ok av_mm xden_ok xrec_ok xo_ok xot_mm xot_ok xy_mm x2_ok")
        r_stats, r_vared, r_rstded, r_normed, r_cols_mm, r_cols_ok, rlg_mm, rlg_ok = sems(
            "r_stats r_vared r_rstded r_normed r_cols_mm r_cols_ok rlg_mm rlg_ok")
        topi_ok, both_ok, gap_ok, re_ok, cnt_mm, place_ok, taken_ok, slots_ok, route_step, halves_zeroed = sems(
            "topi_ok both_ok gap_ok re_ok cnt_mm place_ok taken_ok slots_ok route_step halves_zeroed")
        left = dict(f_cols=f_cols_ok, qk=qk_ok, vf=g_ok, gates=gates_ok, decay_cols=h_ok, ks_cols=ks_ok, sums=z_ok,
                    scores=a_ok, logits=lg_ok, p_cols=p_ok, mix=mix_ok, read=bo_ok, o_cols=o_ok, y=x1_ok,
                    x_cols=x_cols_ok, xq=xq_ok, x_scores0=sc_ok, x_scores1=sc_ok, e_cols0=et_ok, e_cols1=et_ok,
                    values=xo_ok, xo_cols=xot_ok, xy=x2_ok, r_cols=r_cols_ok, r_logits=rlg_ok, counts=taken_ok)
        number_ok = sem("number_ok")
        sent = [sem(f"sent{i}") for i in range(4)]
        wup_landed = [sem(f"wup_landed{i}") for i in range(2)]
        wdn_landed = [sem(f"wdn_landed{i}") for i in range(2)]
        xe_landed = [sem(f"xe_landed{i}") for i in range(2)]
        xet_mm, xet_ok, up_mm, silu_ok, gated_ok, dn_mm, y_ok = sems("xet_mm xet_ok up_mm silu_ok gated_ok dn_mm y_ok")
        about_ok, added, held = sem("about_ok"), sem("added"), sem("held")
        x2_stored = [sem(f"x2_stored{i}") for i in range(2)]
        spare_stored = sem("spare_stored")

        def over_chunks(eng, step):
            def at(b, c):
                def run(lag, work):
                    n = b * CPB + c - lag
                    if not isinstance(n, int) or 0 <= n < NCH:
                        work(n, (c - lag) % CPB, b + (c - lag) // CPB)
                return run

            for c in range(2 * CPB):
                step(at(c // CPB, c % CPB))
            with eng.Fori(2, B) as b:
                for c in range(CPB):
                    step(at(b, c))
            for c in range(LAGS):
                step(at(B, c))

        def bank_left(pe, name, n):
            turn = next(t for t in turns if name in [x for x, _ in t])
            i = [x for x, _ in turn].index(name)
            lag = turn[i][1]
            for j, (other, other_lag) in enumerate(turn):
                m = n + lag - other_lag - (1 if j >= i else 0)
                if isinstance(n, int):
                    m = min(m, NCH - 1)
                    if m >= 0:
                        pe.wait_ge(left[other], m + 1)
                elif j == (i - 1) % len(turn):
                    pe.wait_ge(left[other], m + 1)

        def over_groups(eng, step):
            for j in range(GPL):
                step(0, j)
            with eng.Fori(1, E // 2 - 1) as d:
                for j in range(GPL):
                    step(d, j)
            for j in range(GPL):
                step(E // 2 - 1, j)

        def later(n, k):
            return not isinstance(n, int) or n >= k

        def is_last(n, last):
            return isinstance(n, int) and n == last

        CONSTS = 15 + XH
        x_rows = x.rearrange("b (c p) d -> (b c p) d", p=P)
        mask_rows = mask.rearrange("b t k -> (b t) k")

        block = ctx.enter_context(nc.Block())

        @block.sync
        def _(sp):
            def feat(w):
                return w.rearrange("(k p) n -> p k n", p=P)

            def load_x(n, c):
                sp.dma_start(xin[:, c, :], x_rows[bass.ds(n * P, P), :]).then_inc(x_landed[c], 16)

            load_x(0, 0)
            for j, w in enumerate((wq, wk, wv, wf)):
                sp.dma_start(w_in[:, :, j * D:(j + 1) * D], feat(w)).then_inc(w_landed, 16)
            sp.dma_start(wo_raw[:, :, :], feat(wo)).then_inc(w_landed, 16)
            gcol = gnorm.rearrange("(m a) -> m a", a=1)
            sp.dma_start(gn[0:M, :], gcol).then_inc(w_landed, 16)
            sp.dma_start(gn[M:2 * M, :], gcol).then_inc(w_landed, 16)
            for j, w in enumerate((xwq_t, xwk_t, xwv_t, xwo_t)):
                sp.dma_start(xw[:, j, :, :], feat(w)).then_inc(w_landed, 16)
            sp.dma_start(wr_s[:, :, :], feat(wr)).then_inc(w_landed, 16)
            sp.dma_start(ctx_s[:, :, :], feat(ctx_t)).then_inc(ctx_landed, 16)
            sp.dma_start(kp_i[:, :], kpos.rearrange("(a b) k -> a (b k)", a=1).to_broadcast([P, B * KL]))\
              .then_inc(ctx_landed, 16)
            sp.dma_start(qp_i[:, :], qpos).then_inc(ctx_landed, 16)
            sp.wait_ge(consts_made, 3)
            per = SLOTS // P
            for j in range(4):
                rows = xe_dram[j * SLOTS // 4:(j + 1) * SLOTS // 4, :].rearrange("(r p) d -> p r d", p=P)
                sp.dma_start(rows, empty[:, :].rearrange("p (r d) -> p r d", r=1).to_broadcast([P, per // 4, ROW]))\
                  .then_inc(zeros_sent, 16)
            sp.dma_start(out[SPARE:SPARE + P, :], empty[:, 0:D]).then_inc(spare_stored, 16)

            def store_x2(n, par):
                sp.wait_ge(x2_ok, n + 1)
                sp.dma_start(out[bass.ds(n * P, P), :], x2[:, par, :]).then_inc(x2_stored[par], 16)

            def step(b, c, x_on=True):
                s = b * CPB + c
                if x_on:
                    nxt = (c + 1) % 4
                    if later(s, 3):
                        sp.wait_ge(x1_ok, s - 2)
                    sp.dma_start(xin[:, nxt, :], x_rows[bass.ds((s + 1) * P, P), :]).then_inc(x_landed[nxt], 16)
                if later(s, 2):
                    sp.wait_ge(hid_ok, s - 1)
                sp.dma_start(mask_i[:, c % 2, :], mask_rows[bass.ds(s * P, P), :]).then_inc(mask_landed[c % 2], 16)
                if later(s, X2_LAG):
                    store_x2(s - X2_LAG, (c - X2_LAG) % 2)

            for c in range(2 * CPB):
                step(c // CPB, c % CPB)
            with sp.Fori(2, B - 1) as b:
                for c in range(CPB):
                    step(b, c)
            for c in range(CPB):
                step(B - 1, c, c < CPB - 1)
            for n in range(NCH - X2_LAG, NCH):
                store_x2(n, n % 2)

            def load_expert(e, par):
                sp.dma_start(w1_s[par][:, :, :], w1[bass.ds(e, 1), :, :].rearrange("a (k p) f -> p (a k) f", p=P))\
                  .then_inc(wup_landed[par], 16)
                sp.dma_start(w3_s[par][:, :, :], w3[bass.ds(e, 1), :, :].rearrange("a (k p) f -> p (a k) f", p=P))\
                  .then_inc(wup_landed[par], 16)
                sp.dma_start(w2_s[par][:, :, :], w2[bass.ds(e, 1), :, :].rearrange("a (k p) n -> p (a k) n", p=P))\
                  .then_inc(wdn_landed[par], 16)

            def load_group(g, par):
                sp.dma_start(xe[:, par, :, :], xe_dram[bass.ds(g * GS, GS), :].rearrange("(a p) d -> p a d", p=P))\
                  .then_inc(xe_landed[par], 16)

            load_expert(0, 0)
            for i in range(4):
                sp.wait_ge(sent[i], 16 * NCH // 2)
            for g in range(2):
                load_group(g, g)

            def group(d, j):
                g, par = d * GPL + j, j % 2
                if not isinstance(g, int) or g + 2 < NG:
                    sp.wait_ge(xet_mm, g + 1)
                    sp.wait_ge(about_ok, g + 1)
                    load_group(g + 2, par)
                if j % GPE == 1 and not (isinstance(d, int) and 2 * d + j // GPE == E - 1):
                    if later(g, GPE):
                        sp.wait_ge(dn_mm, g - 1)
                    load_expert(2 * d + j // GPE + 1, 1 - j // GPE)

            over_groups(sp, group)

        @block.gpsimd
        def _(pool):
            pool.memset(empty[:, :], 0.0).then_inc(consts_made, 1)
            pool.wait_ge(consts_made, 1)
            pool.iota(empty[:, D:D + 1], [[0, 1]], base=SPARE, channel_multiplier=1,
                      allow_small_or_imprecise_dtypes=True).then_inc(consts_made, 1)
            pool.iota(token_no[:, :], [[P, NCH]], base=0, channel_multiplier=1,
                      allow_small_or_imprecise_dtypes=True).then_inc(consts_made, 1)
            pool.memset(ident[:, :], 0.0).then_inc(consts_step, 1)
            pool.memset(ones[:, :], 1.0).then_inc(consts_step, 1)
            pool.memset(all_b[:, :], 1.0).then_inc(consts_step, 1)
            pool.memset(half[:, :], 0.5).then_inc(consts_step, 1)
            pool.memset(neg_half[:, :], -0.5).then_inc(consts_step, 1)
            pool.memset(taken[:, :], 0.0).then_inc(consts_step, 1)
            for h in range(XH):
                pool.memset(slopes[:, h:h + 1], SLOPE[h]).then_inc(consts_step, 1)
            pool.iota(expert_no[:, :], [[1, E]], base=0, channel_multiplier=0,
                      allow_small_or_imprecise_dtypes=True).then_inc(consts_step, 1)
            pool.wait_ge(consts_step, 7 + XH)
            pool.affine_select(out=ident[:, :], in_=ident[:, :], compare_op=ALU.not_equal, fill=1.0,
                               base=0, pattern=[[-1, P]], channel_multiplier=1).then_inc(consts_step, 1)
            pool.affine_select(out=causal[:, :], in_=ones[:, :], compare_op=ALU.is_ge, fill=0.0,
                               base=0, pattern=[[1, P]], channel_multiplier=-1).then_inc(consts_step, 1)
            pool.affine_select(out=tri_half[:, :], in_=half[:, :], compare_op=ALU.is_ge, fill=-0.5,
                               base=0, pattern=[[1, P]], channel_multiplier=-1).then_inc(consts_step, 1)
            pool.affine_select(out=before[:, :], in_=all_b[:, :], compare_op=ALU.is_gt, fill=0.0,
                               base=0, pattern=[[1, P]], channel_multiplier=-1).then_inc(consts_step, 1)
            for tile, n, w in ((diag16, HPT, XD), (pair_of, 2, KL)):
                pool.affine_select(out=tile[:, :], in_=ones[:, 0:n], compare_op=ALU.is_ge, fill=0.0,
                                   base=0, pattern=[[-w, n]], channel_multiplier=1).then_inc(consts_step, 1)
            pool.wait_ge(consts_step, 13 + XH)
            for tile, n, w in ((diag16, HPT, XD), (pair_of, 2, KL)):
                pool.affine_select(out=tile[:, :], in_=tile[:, :], compare_op=ALU.is_ge, fill=0.0,
                                   base=w - 1, pattern=[[w, n]], channel_multiplier=-1).then_inc(consts_step, 1)

            pool.wait_ge(consts_step, CONSTS)

            def hold(i):
                return pool.tensor_tensor(idle_g[:, i:i + 1], half[:, 0:1], half[:, 0:1], ALU.add)

            def power(n, var, rstd, ready, done, used):
                if later(n, 1):
                    pool.wait_ge(used, n)
                pool.wait_ge(ready, n + 1)
                pool.tensor_tensor(rstd[:, :], var[:, :], neg_half[:, 0:var.shape[1]], ALU.pow).then_inc(done, 1)

            def f_power(n, c, b):
                power(n, f_var, f_rstd, f_vared, f_rstded, f_normed)

            def x_power(n, c, b):
                power(n, x_var, x_rstd, x_vared, x_rstded, x_normed)

            def r_power(n, c, b):
                power(n, r_var, r_rstd, r_vared, r_rstded, r_normed)

            def head_power(n, c, b):
                power(n, b_ms, b_rms, ms_ok, rms_ok, bw_ok)

            def keys(n, c, b):
                if c == 0:
                    if later(n, 1):
                        pool.wait_ge(xs_mm, n)
                    else:
                        pool.wait_ge(k_made, 1)
                    for h in range(KT):
                        pool.tensor_tensor(
                            k_bd[:, h, :, :],
                            k_all[:, h, bass.ds(b * KL, KL)].rearrange("p (a k) -> p a k", a=1)
                            .to_broadcast([P, HPT, KL]),
                            diag16[:, :].rearrange("p (h a) -> p h a", a=1).to_broadcast([P, HPT, KL]),
                            ALU.mult).then_inc(kbd_ok, 1)

            def values(n, c, b):
                if c == 0:
                    if later(n, 1):
                        pool.wait_ge(av_mm, n)
                    else:
                        pool.wait_ge(v_made, 2 * B)
                    pool.tensor_copy(v_bd[:, :, :].rearrange("p j n -> p (j n)"),
                                     v_all[:, bass.ds(b, 1), :, :].rearrange("p a j n -> p (a j n)"))\
                        .then_inc(vbd_ok, 1)

            def biases(n, c, b):
                pool.wait_ge(dist_ok, n + 1)
                if later(n, 1):
                    pool.wait_ge(sc_ok, n)
                pool.tensor_tensor(
                    bias[:, :, :],
                    dist[:, :].rearrange("p (a k) -> p a k", a=1).to_broadcast([P, XH, KL]),
                    slopes[:, :].rearrange("p (h a) -> p h a", a=1).to_broadcast([P, XH, KL]),
                    ALU.mult).then_inc(bias_ok, 1)

            def gate_probs(n, c, b):
                if later(n, 1):
                    pool.wait_ge(p_mm, n)
                pool.wait_ge(be_ok, n + 1)
                pool.tensor_tensor(b_p[:, :], b_e[:, :, :].rearrange("p h m -> p (h m)"), up[:, :], ALU.mult)\
                    .then_inc(bp_ok, 1)

            def less_max(n, c, b):
                pool.wait_ge(scm_ok, n + 1)
                pool.tensor_tensor(
                    sc[:, :, :], sc[:, :, :],
                    sc_m[:, :].rearrange("p (h a) -> p h a", a=1).to_broadcast([P, XH, KL]),
                    ALU.subtract).then_inc(scd_ok, 1)

            def send_rows(n, c, b):
                par = c % 2
                if not later(n, 1):
                    pool.wait_ge(zeros_sent, 64)
                pool.wait_ge(slots_ok, n + 1)
                hold(0)
                for k in range(2):
                    pool.indirect_dma_start(
                        out=xe_dram, out_offset=bass.IndirectOffsetOnAxis(ap=send[:, par, k:k + 1], axis=0),
                        in_=r_xn[:, par, k, :], in_offset=None, bounds_check=SLOTS - 1, oob_is_err=False)\
                        .then_inc(sent[2 * par + k], 16)

            def step(run):
                run(0, f_power)
                run(1, head_power)
                run(2, values)
                run(2, less_max)
                run(4, send_rows)
                run(1, keys)
                run(3, r_power)
                run(1, biases)
                run(1, x_power)
                run(0, gate_probs)

            over_chunks(pool, step)

            for i in range(2):
                pool.wait_ge(x2_stored[i], 16 * NCH // 2)
            pool.wait_ge(spare_stored, 16)

            def add_rows(g, par):
                pool.wait_ge(y_ok, g + 1)
                for a in range(2):
                    if a or later(g, 1):
                        pool.wait_ge(added, g * 32 + a * 16)
                        pool.wait_ge(held, g * 2 + a)
                    hold(1).then_inc(held, 1)
                    pool.indirect_dma_start(
                        out=out, out_offset=bass.IndirectOffsetOnAxis(ap=token[par][a][:, :], axis=0),
                        in_=y_s[:, par, a, :], in_offset=None, compute_op=ALU.add).then_inc(added, 16)

            def group(d, j):
                add_rows(d * GPL + j, j % 2)

            over_groups(pool, group)
            pool.wait_ge(added, NG * 32)

        @block.scalar
        def _(act):
            act.preload_act_table_set("natural_log_exp_and_others")

            def evacuate(n, dst, src, ready, used, done, amount=1.0):
                if later(n, 1):
                    act.wait_ge(used, n)
                act.wait_ge(ready, n + 1)
                act.activation(dst, src, ACT.Copy, scale=amount).then_inc(done, 1)

            def two(t):
                return t.rearrange("p (k t) -> p k t", k=2)

            def f_columns(n, c, b):
                evacuate(n, f_xnt[:, :, :], two(tile["f_cols"][:, 0:D]), f_cols_mm, qk_mm, f_cols_ok)

            def x_columns(n, c, b):
                evacuate(n, x_xnt[:, :, :], two(tile["x_cols"][:, 0:D]), x_cols_mm, xq_mm, x_cols_ok)

            def r_columns(n, c, b):
                evacuate(n, r_xnt[:, :, :], two(tile["r_cols"][:, 0:D]), r_cols_mm, rlg_mm, r_cols_ok)

            def x_queries(n, c, b):
                evacuate(n, xq_t[:, :, :], two(tile["xq"][:, 0:D]), xq_mm, xs_mm, xq_ok, XSCALE)

            def o_columns(n, c, b):
                evacuate(n, o_t[:, :, :], two(tile["o_cols"][:, 0:D]), o_mm, y_mm, o_ok)

            def xo_columns(n, c, b):
                evacuate(n, xo_t[:, :, :], two(tile["xo_cols"][:, 0:D]), xot_mm, xy_mm, xot_ok)

            def ks_columns(n, c, b):
                evacuate(n, ks_t[:, :, :], tile["ks_cols"].rearrange("p (k t) -> p k t", k=4), ks_mm, mix_mm, ks_ok)

            def e_columns(n, c, b):
                if later(n, 1):
                    act.wait_ge(av_mm, n)
                act.wait_ge(et_mm, n + 1)
                for k in range(2):
                    last = act.activation(e_t[:, 4 * k:4 * k + 4, :],
                                          tile[f"e_cols{k}"].rearrange("p (k t) -> p k t", k=4), ACT.Copy)
                last.then_inc(et_ok, 1)

            def p_columns(n, c, b):
                if later(n, 1):
                    act.wait_ge(read_mm, n)
                else:
                    act.wait_ge(halves_zeroed, 2)
                act.wait_ge(p_mm, n + 1)
                for i in range(2):
                    rows = slice(M * i, M * i + M)
                    last = act.activation(p_z[rows, i::2, :], two(tile["p_cols"][rows, 0:D]), ACT.Copy)
                last.then_inc(p_ok, 1)

            def f_absolute(n, c, b):
                act.wait_ge(vf_mm, n + 1)
                act.activation(f_abs[:, :], tile["vf"][:, D:2 * D], ACT.Abs).then_inc(abs_ok, 1)
                if later(n, 1):
                    act.wait_ge(read_mm, n)
                act.activation(v_s[:, :], tile["vf"][:, 0:D], ACT.Copy).then_inc(v_ok, 1)
                act.wait_ge(abs_ok, n + 1)
                act.activation(f_e[:, :], f_abs[:, :], ACT.Exp, scale=-1.0).then_inc(fe_ok, 1)
                act.wait_ge(fe_ok, n + 1)
                if later(n, 1):
                    act.wait_ge(g_ok, n)
                act.activation(f_l[:, :], f_e[:, :], ACT.Ln, bias=1.0).then_inc(fl_ok, 1)

            def qk_sigmoid(n, c, b):
                act.wait_ge(qk_mm, n + 1)
                act.activation(qk_e[:, :], tile["qk"], ACT.Exp, scale=-1.0).then_inc(e_ok, 1)
                act.wait_ge(e_ok, n + 1)
                act.activation(qk_l[:, :], qk_e[:, :], ACT.Ln, bias=1.0).then_inc(l_ok, 1)
                act.wait_ge(l_ok, n + 1)
                if later(n, 1):
                    act.wait_ge(qk_ok, n)
                act.activation(qk_s[:, :], qk_l[:, :], ACT.Exp, scale=-1.0).then_inc(sig_ok, 1)

            def one_minus(n, c, b):
                act.wait_ge(g_ok, n + 1)
                if later(n, 1):
                    act.wait_ge(s_ok, n)
                act.activation(one_less[:, :], g_s[:, c % 2, :], ACT.Exp, scale=1 / GATE_NORM).then_inc(less_ok, 1)

            def gates(n, c, b):
                act.wait_ge(gates_mm, n + 1)
                if later(n, 1):
                    act.wait_ge(s_ok, n)
                    act.wait_ge(bp_ok, n)
                    act.wait_ge(h_ok, n)
                grow = tile["gates"][:, 0:D]
                act.activation(down[:, :], grow, ACT.Exp, scale=-1 / GATE_NORM)
                act.activation(decay[:, :], tile["gates"][:, D:2 * D], ACT.Exp, scale=1 / GATE_NORM)
                act.activation(up[:, :], grow, ACT.Exp, scale=1 / GATE_NORM).then_inc(gates_ok, 1)

            def softmax_exp(n, c, b):
                act.wait_ge(lgd_ok, n + 1)
                if later(n, 1):
                    act.wait_ge(bp_ok, n)
                    act.wait_ge(bsum_ok, n)
                act.activation(b_e[:, :, :], lg_d[:, :, :], ACT.Exp, scale=float(M) ** -0.5).then_inc(be_ok, 1)

            def squares(n, c, b):
                act.wait_ge(read_mm, n + 1)
                if later(n, 1):
                    act.wait_ge(rms_step, 3 * n)
                act.activation(b_sq[:, :, :], tile["read"][:, 0:D].rearrange("p (h m) -> p h m", h=H), ACT.Square)\
                    .then_inc(sq_ok, 1)

            def x_exp(n, c, b):
                act.wait_ge(scd_ok, n + 1)
                if later(n, 1):
                    act.wait_ge(et_mm, n)
                act.activation(ex[:, :, :], sc[:, :, :], ACT.Exp).then_inc(ex_ok, 1)

            def router_exp(n, c, b):
                act.wait_ge(gap_ok, n + 1)
                if later(n, 1):
                    act.wait_ge(slots_ok, n)
                act.activation(r_e[:, :], gap[:, :], ACT.Exp).then_inc(re_ok, 1)

            def step(run):
                run(1, squares)
                run(0, f_columns)
                run(3, xo_columns)
                run(0, f_absolute)
                run(4, router_exp)
                run(0, qk_sigmoid)
                run(0, gates)
                run(0, one_minus)
                run(1, o_columns)
                run(2, x_exp)
                run(0, ks_columns)
                run(2, e_columns)
                run(0, softmax_exp)
                run(3, r_columns)
                run(1, x_columns)
                run(0, p_columns)
                run(1, x_queries)

            over_chunks(act, step)

            def group(d, j):
                g = d * GPL + j
                for f in range(FT):
                    n = g * FT + f
                    act.wait_ge(up_mm, n + 1)
                    if later(n, 2):
                        act.wait_ge(gated_ok, n - 1)
                    act.activation(h_a[:, f % 2, :], bank[2 + f % 4][:, 0:GS], ACT.Silu).then_inc(silu_ok, 1)

            over_groups(act, group)

        @block.vector
        def _(dve):
            dve.memset(q_z[:, :, :], 0.0).then_inc(halves_zeroed, 1)
            dve.memset(p_z[:, :, :], 0.0).then_inc(halves_zeroed, 1)
            dve.wait_ge(ctx_landed, 48)
            dve.tensor_copy(kp[:, :, :], kp_i[:, :].rearrange("p (b k) -> p b k", b=B)).then_inc(small_made, 1)
            dve.tensor_copy(qp[:, :], qp_i[:, :]).then_inc(small_made, 1)
            dve.wait_ge(w_landed, 16 * 12)
            for k in range(KT):
                dve.tensor_scalar(wo_s[:, k, :], wo_raw[:, k, :], gn[:, 0:1], None, ALU.mult).then_inc(small_made, 1)
            dve.wait_ge(consts_step, CONSTS)
            dve.wait_ge(ctx_mm, 1)
            for k in range(KT):
                last = dve.tensor_copy(k_all[:, k, :], bank[k][:, :])
            last.then_inc(k_made, 1)
            for b in range(B):
                if b:
                    dve.wait_ge(ctx_mm, 1 + b)
                for k in range(KT):
                    dve.tensor_copy(ctx2[:, k, :, :],
                                    ctx_s[:, k, b * KL:(b + 1) * KL].rearrange("p (a k) -> p a k", a=1)
                                    .to_broadcast([P, 2, KL])).then_inc(ctx_doubled, 1)
                dve.wait_ge(ctx_mm, 2 + b)
                dve.tensor_tensor(
                    v_all[:, b, :, 0:2 * XD].rearrange("p j (i d) -> p j i d", i=2),
                    bank[2][:, 0:D].rearrange("p (j i d) -> p j i d", j=PAIRS, i=2),
                    pair_of[:, :].rearrange("p (a i b) -> p a i b", a=1, b=1).to_broadcast([P, PAIRS, 2, XD]),
                    ALU.mult).then_inc(v_made, 1)
                dve.tensor_copy(v_all[:, b, :, 2 * XD:VW],
                                pair_of[:, :].rearrange("p (a i) -> p a i", a=1).to_broadcast([P, PAIRS, 2]))\
                   .then_inc(v_made, 1)

            def hold():
                dve.memset(idle_v[:, :], 0.0)

            def statistics(n, src, st, mv, var, step_s, vared_s, rstded_s):
                dve.bn_stats(st[:, :], src).then_inc(step_s, 1)
                dve.wait_ge(step_s, 2 * n + 1)
                hold()
                dve.bn_aggr(mv[:, :], st[:, :]).then_inc(step_s, 1)
                dve.wait_ge(step_s, 2 * n + 2)
                if later(n, 1):
                    dve.wait_ge(rstded_s, n)
                dve.tensor_scalar(var[:, :], mv[:, 1:2], EPS, None, ALU.add).then_inc(vared_s, 1)

            def norm(n, src, dst, mv, rstd, rstded_s, normed_s):
                dve.wait_ge(rstded_s, n + 1)
                dve.tensor_scalar(dst, src, mv[:, 0:1], rstd[:, 0:1], ALU.subtract, ALU.mult).then_inc(normed_s, 1)

            def wide(t, n):
                return t.rearrange("p (h a) -> p h a", a=1).to_broadcast([P, t.shape[1], n])

            def heads(t):
                return t.rearrange("p (h m) -> p h m", h=H)

            def two(t):
                return t.rearrange("p (k t) -> p k t", k=2)

            causal_h = causal[:, :].rearrange("p (a t) -> p a t", a=1).to_broadcast([P, H, P])

            def f_statistics(n, c, b):
                dve.wait_ge(x_landed[c], (n - c) * 4 + 16)
                statistics(n, xin[:, c, :], f_st, f_mv, f_var, f_stats, f_vared, f_rstded)

            def f_norm(n, c, b):
                if later(n, 1):
                    dve.wait_ge(f_cols_mm, n)
                norm(n, xin[:, c, :], f_xn[:, :], f_mv, f_rstd, f_rstded, f_normed)

            def log_gates(n, c, b):
                dve.wait_ge(fl_ok, n + 1)
                dve.wait_ge(v_ok, n + 1)
                if later(n, 1):
                    dve.wait_ge(gates_mm, n)
                if later(n, 2):
                    dve.wait_ge(less_ok, n - 1)
                dve.scalar_tensor_tensor(out=g_s[:, c % 2, :], in0=tile["vf"][:, D:2 * D], scalar=0.0, in1=f_l[:, :],
                                         op0=ALU.min, op1=ALU.subtract).then_inc(g_ok, 1)

            def queries_keys(n, c, b):
                dve.wait_ge(sig_ok, n + 1)
                if later(n, 1):
                    dve.wait_ge(logits_mm, n)
                    dve.wait_ge(sums_mm, n)
                for i in range(2):
                    rows = slice(M * i, M * i + M)
                    dve.tensor_tensor(q_z[rows, i::2, :], two(tile["qk"][rows, 0:D]), two(qk_s[rows, 0:D]), ALU.mult)
                dve.tensor_tensor(k_s[:, :], tile["qk"][:, D:2 * D], qk_s[:, D:2 * D], ALU.mult).then_inc(qk_ok, 1)

            def slot_values(n, c, b):
                dve.wait_ge(less_ok, n + 1)
                dve.wait_ge(gates_ok, n + 1)
                if later(n, 1):
                    dve.wait_ge(sums_mm, n)
                    dve.wait_ge(logits_mm, n)
                dve.scalar_tensor_tensor(out=s_s[:, :], in0=one_less[:, :], scalar=1.0, in1=down[:, :],
                                         op0=ALU.subtract, op1=ALU.mult, reverse0=True).then_inc(s_ok, 1)

            def start_states(n, c, b):
                if later(n, 1):
                    dve.wait_ge(read_mm, n)
                    dve.wait_ge(z_ok, n)
                dve.wait_ge(decay_mm, n + 1)
                if c == 0:
                    dve.memset(hk[:, :, :], 0.0)
                    dve.memset(hv[:, :, :], 0.0).then_inc(h_ok, 1)
                else:
                    dve.tensor_tensor(hk[:, :, :], zk[:, :, :], two(decay[:, :]), ALU.mult)
                    dve.tensor_tensor(hv[:, :, :], zv[:, :, :],
                                      two(tile["decay_cols"][:, 0:D])[:, :, 0:1].to_broadcast([P, 2, P]), ALU.mult)\
                       .then_inc(h_ok, 1)

            def end_states(n, c, b):
                dve.wait_ge(sums_mm, n + 1)
                dve.wait_ge(h_ok, n + 1)
                dve.tensor_tensor(zk[:, :, :], two(tile["sums"][:, 0:D]), hk[:, :, :], ALU.add)
                dve.tensor_tensor(zv[:, :, :], two(tile["sums"][:, D:2 * D]), hv[:, :, :], ALU.add).then_inc(z_ok, 1)

            def causal_scores(n, c, b):
                if later(n, 1):
                    dve.wait_ge(logits_mm, n)
                dve.wait_ge(scores_mm, n + 1)
                dve.tensor_tensor(a_s[:, :, :], tile["scores"].rearrange("p (h t) -> p h t", h=H), causal_h, ALU.mult)\
                   .then_inc(a_ok, 1)

            def slot_logits(n, c, b):
                dve.wait_ge(logits_mm, n + 1)
                dve.wait_ge(gates_ok, n + 1)
                dve.tensor_tensor(lg[:, :, :], heads(tile["logits"][:, 0:D]), heads(up[:, :]), ALU.mult).then_inc(lg_ok, 1)
                dve.wait_ge(lg_ok, n + 1)
                dve.tensor_reduce(lg_m[:, :], lg[:, :, :], AX.X, ALU.max).then_inc(lgm_ok, 1)
                dve.wait_ge(lgm_ok, n + 1)
                if later(n, 1):
                    dve.wait_ge(be_ok, n)
                dve.tensor_tensor(lg_d[:, :, :], lg[:, :, :], wide(lg_m[:, :], M), ALU.subtract).then_inc(lgd_ok, 1)

            def softmax_sum(n, c, b):
                dve.wait_ge(be_ok, n + 1)
                dve.tensor_reduce(b_sum[:, :], b_e[:, :, :], AX.X, ALU.add).then_inc(bsum_ok, 1)
                dve.wait_ge(bsum_ok, n + 1)
                dve.reciprocal(b_rec[:, :], b_sum[:, :]).then_inc(brec_ok, 1)

            def causal_mix(n, c, b):
                if later(n, 1):
                    dve.wait_ge(read_mm, n)
                dve.wait_ge(mix_mm, n + 1)
                dve.tensor_tensor(bt_s[:, :, :], tile["mix"].rearrange("p (h t) -> p h t", h=H), causal_h, ALU.mult)\
                   .then_inc(mix_ok, 1)

            def head_squares(n, c, b):
                dve.wait_ge(sq_ok, n + 1)
                dve.tensor_reduce(b_ss[:, :], b_sq[:, :, :], AX.X, ALU.add).then_inc(rms_step, 1)
                dve.wait_ge(rms_step, 3 * n + 1)
                dve.wait_ge(brec_ok, n + 1)
                dve.tensor_tensor(b_t1[:, :], b_ss[:, :], b_rec[:, :], ALU.mult).then_inc(rms_step, 1)

            def head_squares2(n, c, b):
                dve.wait_ge(rms_step, 3 * n + 2)
                dve.tensor_tensor(b_t2[:, :], b_t1[:, :], b_rec[:, :], ALU.mult).then_inc(rms_step, 1)
                dve.wait_ge(rms_step, 3 * n + 3)
                if later(n, 1):
                    dve.wait_ge(rms_ok, n)
                dve.tensor_scalar(b_ms[:, :], b_t2[:, :], 1.0 / M, EPS, ALU.mult, ALU.add).then_inc(ms_ok, 1)

            def head_weights(n, c, b):
                dve.wait_ge(rms_ok, n + 1)
                dve.tensor_tensor(b_w[:, :], b_rms[:, :], b_rec[:, :], ALU.mult).then_inc(bw_ok, 1)

            def head_outputs(n, c, b):
                dve.wait_ge(bw_ok, n + 1)
                if later(n, 1):
                    dve.wait_ge(o_mm, n)
                dve.tensor_tensor(b_o[:, :, :], heads(tile["read"][:, 0:D]), wide(b_w[:, :], M), ALU.mult)\
                   .then_inc(bo_ok, 1)

            def residual1(n, c, b):
                dve.wait_ge(y_mm, n + 1)
                dve.tensor_tensor(x1[:, c % 2, :], tile["y"][:, 0:D], xin[:, c, :], ALU.add).then_inc(x1_ok, 1)

            def x_statistics(n, c, b):
                dve.wait_ge(x1_ok, n + 1)
                statistics(n, x1[:, c % 2, :], x_st, x_mv, x_var, x_stats, x_vared, x_rstded)

            def x_norm(n, c, b):
                if later(n, 1):
                    dve.wait_ge(x_cols_mm, n)
                norm(n, x1[:, c % 2, :], x_xn[:, :], x_mv, x_rstd, x_rstded, x_normed)

            def hidden_keys(n, c, b):
                dve.wait_ge(mask_landed[c % 2], (n - c % 2) * 8 + 16)
                dve.tensor_scalar(hid[:, :], mask_i[:, c % 2, :], 0.0, -HIDDEN, ALU.is_equal, ALU.mult)\
                   .then_inc(hid_ok, 1)

            def distances(n, c, b):
                dve.wait_ge(hid_ok, n + 1)
                if later(n, 1):
                    dve.wait_ge(bias_ok, n)
                dve.scalar_tensor_tensor(
                    out=dist[:, :], in0=kp[:, bass.ds(b, 1), :].rearrange("p a k -> p (a k)"),
                    scalar=qp[:, bass.ds(n, 1)], in1=hid[:, :], op0=ALU.subtract, op1=ALU.add).then_inc(dist_ok, 1)

            def x_scores(n, c, b):
                dve.wait_ge(bias_ok, n + 1)
                dve.wait_ge(xs_mm, n + 1)
                if later(n, 1):
                    dve.wait_ge(ex_ok, n)
                for k in range(2):
                    last = dve.tensor_tensor(sc[:, 8 * k:8 * k + 8, :],
                                             tile[f"x_scores{k}"].rearrange("p (h k) -> p h k", h=HPT),
                                             bias[:, 8 * k:8 * k + 8, :], ALU.add)
                last.then_inc(sc_ok, 1)

            def x_maximum(n, c, b):
                dve.wait_ge(sc_ok, n + 1)
                if later(n, 1):
                    dve.wait_ge(scd_ok, n)
                dve.tensor_reduce(sc_m[:, :], sc[:, :, :], AX.X, ALU.max).then_inc(scm_ok, 1)

            def x_denominators(n, c, b):
                dve.wait_ge(av_mm, n + 1)
                dve.tensor_scalar(x_den[:, :].rearrange("p (j i) -> p j i", i=2),
                                  tile["values"][:, 0:PAIRS * VW].rearrange("p (j n) -> p j n", n=VW)[:, :, 2 * XD:VW],
                                  1.0, None, ALU.add).then_inc(xden_ok, 1)
                dve.wait_ge(xden_ok, n + 1)
                dve.reciprocal(x_rec[:, :], x_den[:, :]).then_inc(xrec_ok, 1)

            def x_outputs(n, c, b):
                dve.wait_ge(xrec_ok, n + 1)
                if later(n, 1):
                    dve.wait_ge(xot_mm, n)
                dve.tensor_tensor(
                    x_o[:, :, :].rearrange("p j (i d) -> p j i d", i=2),
                    tile["values"][:, 0:PAIRS * VW].rearrange("p (j n) -> p j n", n=VW)[:, :, 0:2 * XD]
                    .rearrange("p j (i d) -> p j i d", i=2),
                    x_rec[:, :].rearrange("p (j i a) -> p j i a", i=2, a=1).to_broadcast([P, PAIRS, 2, XD]),
                    ALU.mult).then_inc(xo_ok, 1)

            def residual2(n, c, b):
                dve.wait_ge(xy_mm, n + 1)
                if later(n, 2):
                    dve.wait_ge(x2_stored[c % 2], (n - c % 2) * 8)
                dve.tensor_tensor(x2[:, c % 2, :], tile["xy"][:, 0:D], x1[:, c % 2, :], ALU.add).then_inc(x2_ok, 1)

            def r_statistics(n, c, b):
                dve.wait_ge(x2_ok, n + 1)
                statistics(n, x2[:, c % 2, :], r_st, r_mv, r_var, r_stats, r_vared, r_rstded)

            def sent_before(n, c):
                if later(n, 2):
                    for k in range(2):
                        dve.wait_ge(sent[2 * (c % 2) + k], (n - c % 2) * 8)

            def r_norm(n, c, b):
                sent_before(n, c)
                if later(n, 2):
                    dve.wait_ge(r_cols_mm, n - 1)
                norm(n, x2[:, c % 2, :].rearrange("p (a d) -> p a d", a=1).to_broadcast([P, 2, D]),
                     r_xn[:, c % 2, :, 0:D], r_mv, r_rstd, r_rstded, r_normed)
                dve.tensor_copy(r_xn[:, c % 2, :, D:D + 1],
                                token_no[:, bass.ds(n, 1)].rearrange("p (a b) -> p a b", b=1).to_broadcast([P, 2, 1]))\
                   .then_inc(number_ok, 1)

            def top_two(n, c, b):
                dve.wait_ge(rlg_mm, n + 1)
                dve.tensor_scalar(r_lg[:, :], tile["r_logits"][:, 0:E], -CLAMP, CLAMP, ALU.max, ALU.min)\
                   .then_inc(rlg_ok, 1)
                dve.wait_ge(rlg_ok, n + 1)
                hold()
                dve.max(top[:, :], r_lg[:, :]).then_inc(route_step, 1)
                dve.wait_ge(route_step, n * ROUTE_STEPS + 1)
                if later(n, 1):
                    dve.wait_ge(re_ok, n)
                dve.tensor_scalar(gap[:, :], top[:, 1:2], top[:, 0:1], None, ALU.subtract).then_inc(gap_ok, 1)
                dve.max_index(top_i[:, :], top[:, :], r_lg[:, :]).then_inc(topi_ok, 1)
                dve.wait_ge(topi_ok, n + 1)
                dve.tensor_copy(top_f[:, :], top_i[:, 0:2]).then_inc(route_step, 1)
                dve.wait_ge(route_step, n * ROUTE_STEPS + 2)
                for k in range(2):
                    dve.tensor_scalar(hot[:, k, :], expert_no[:, :], top_f[:, k:k + 1], None, ALU.is_equal)\
                       .then_inc(route_step, 1)
                dve.wait_ge(route_step, n * ROUTE_STEPS + 4)
                if later(n, 1):
                    dve.wait_ge(cnt_mm, n)
                dve.tensor_tensor(both[:, :], hot[:, 0, :], hot[:, 1, :], ALU.add).then_inc(both_ok, 1)

            def places(n, c, b):
                dve.wait_ge(cnt_mm, n + 1)
                if later(n, 1):
                    dve.wait_ge(taken_ok, n)
                dve.tensor_tensor(place[:, :], tile["counts"][:, 0:E], taken[:, :], ALU.add).then_inc(place_ok, 1)
                dve.wait_ge(place_ok, n + 1)
                dve.tensor_tensor(taken[:, :], tile["counts"][:, E:2 * E], taken[:, :], ALU.add).then_inc(taken_ok, 1)
                dve.tensor_tensor(place_h[:, :, :], hot[:, :, :],
                                  place[:, :].rearrange("p (a e) -> p a e", a=1).to_broadcast([P, 2, E]),
                                  ALU.mult).then_inc(route_step, 1)
                dve.tensor_scalar(base[:, :], top_f[:, :], float(CAP), None, ALU.mult).then_inc(route_step, 1)
                dve.wait_ge(re_ok, n + 1)
                dve.tensor_scalar(r_den[:, :], r_e[:, :], 1.0, 1e-12, ALU.add, ALU.add).then_inc(route_step, 1)
                dve.wait_ge(route_step, n * ROUTE_STEPS + 5)
                dve.tensor_reduce(pos[:, :], place_h[:, :, :], AX.X, ALU.add).then_inc(route_step, 1)
                dve.wait_ge(route_step, n * ROUTE_STEPS + 7)
                dve.reciprocal(r_p[:, :], r_den[:, :]).then_inc(route_step, 1)
                dve.wait_ge(route_step, n * ROUTE_STEPS + 8)
                dve.tensor_scalar(off_f[:, :], pos[:, :], float(CAP), SKIPPED, ALU.is_ge, ALU.mult)\
                   .then_inc(route_step, 1)
                dve.tensor_tensor(slot_f[:, :], pos[:, :], base[:, :], ALU.add).then_inc(route_step, 1)
                dve.wait_ge(route_step, n * ROUTE_STEPS + 9)
                dve.tensor_copy(r_xn[:, c % 2, 0, D + 1:ROW], r_p[:, :])
                dve.tensor_tensor(r_xn[:, c % 2, 1, D + 1:ROW], r_p[:, :], r_e[:, :], ALU.mult)
                dve.wait_ge(route_step, n * ROUTE_STEPS + ROUTE_STEPS)
                dve.tensor_tensor(send[:, c % 2, :], slot_f[:, :], off_f[:, :], ALU.add).then_inc(slots_ok, 1)

            def step(run):
                run(0, f_statistics)
                run(1, head_squares)
                run(0, f_norm)
                run(1, head_squares2)
                run(2, x_scores)
                run(1, head_weights)
                run(1, head_outputs)
                run(2, x_maximum)
                run(4, top_two)
                run(0, log_gates)
                run(4, places)
                run(0, queries_keys)
                run(0, slot_values)
                run(0, start_states)
                run(3, residual2)
                run(3, r_statistics)
                run(1, residual1)
                run(0, causal_scores)
                run(1, x_statistics)
                run(1, hidden_keys)
                run(1, distances)
                run(3, r_norm)
                run(0, slot_logits)
                run(1, x_norm)
                run(0, softmax_sum)
                run(2, x_denominators)
                run(2, x_outputs)
                run(0, causal_mix)
                run(0, end_states)

            over_chunks(dve, step)

            def columns(g, par):
                dve.wait_ge(xet_mm, g + 1)
                if later(g, 2):
                    dve.wait_ge(up_mm, (g - 1) * FT)
                dve.tensor_copy(xe_t[:, par, :, :, :].rearrange("p k a t -> p (k a t)"), bank[0][:, :]).then_inc(xet_ok, 1)

            def gated(g, par):
                for f in range(FT):
                    n = g * FT + f
                    dve.wait_ge(silu_ok, n + 1)
                    if f == 0 and later(g, 2):
                        dve.wait_ge(dn_mm, g - 1)
                    dve.tensor_tensor(h_t[:, par, f, :], bank[2 + f % 4][:, GS:2 * GS], h_a[:, f % 2, :], ALU.mult)\
                       .then_inc(gated_ok, 1)

            def results(g, par):
                dve.wait_ge(dn_mm, g + 1)
                if later(g, 2):
                    dve.wait_ge(added, (g - 1) * 32)
                dve.wait_ge(about_ok, g + 1)
                for a in range(2):
                    dve.tensor_copy(token[par][a][:, :], about[:, par, a, 0:1])
                for a in range(2):
                    last = dve.tensor_scalar(y_s[:, par, a, :], bank[6 + par][:, a * D:(a + 1) * D],
                                             about[:, par, a, 1:2], None, ALU.mult)
                last.then_inc(y_ok, 1)

            def read_about(g, par):
                if later(g, 2):
                    dve.wait_ge(y_ok, g - 1)
                dve.wait_ge(xe_landed[par], (g - par) * 8 + 16)
                dve.tensor_copy(about[:, par, :, :], xe[:, par, :, D:ROW]).then_inc(about_ok, 1)

            columns(0, 0)
            for g in range(2):
                read_about(g, g)

            def group(d, j):
                g, par = d * GPL + j, j % 2
                gated(g, par)
                if not is_last(g, NG - 1):
                    columns(g + 1, 1 - par)
                if later(g, 1):
                    results(g - 1, 1 - par)
                    if not is_last(g, NG - 1):
                        read_about(g + 1, 1 - par)

            over_groups(dve, group)
            results(NG - 1, 1)

        @block.tensor
        def _(pe):
            def flip(dst, tiles, done):
                for i, t in enumerate(tiles):
                    last = pe.transpose(dst[:, i * P:(i + 1) * P], t, ident[:, :])
                last.then_inc(done, 1)

            def product(dst, pairs):
                for i, (lhs, rhs) in enumerate(pairs):
                    last = pe.matmul(dst, lhs, rhs, start=(i == 0), stop=(i == len(pairs) - 1))
                return last

            def halves(t):
                return [t[:, k * P:(k + 1) * P] for k in range(2)]

            pe.wait_ge(consts_step, CONSTS)
            pe.wait_ge(w_landed, 16 * 12)
            pe.wait_ge(ctx_landed, 48)
            for m in range(KT):
                last = product(bank[m][:, :], [(xw[:, 1, k, m * P:(m + 1) * P], ctx_s[:, k, :]) for k in range(KT)])
            last.then_inc(ctx_mm, 1)
            for b in range(B):
                pe.wait_ge(ctx_doubled, 2 * b + 2)
                if b:
                    pe.wait_ge(v_made, 2 * b)
                product(bank[2][:, 0:D], [(ctx2[:, k, :, :].rearrange("p a k -> p (a k)"), xw[:, 2, k, :])
                                          for k in range(KT)]).then_inc(ctx_mm, 1)
            pe.wait_ge(k_made, 1)
            pe.wait_ge(v_made, 2 * B)

            def f_columns(n, c, b):
                pe.wait_ge(f_normed, n + 1)
                bank_left(pe, "f_cols", n)
                flip(tile["f_cols"], halves(f_xn), f_cols_mm)

            def project_vf(n, c, b):
                pe.wait_ge(f_cols_ok, n + 1)
                bank_left(pe, "vf", n)
                product(tile["vf"], [(f_xnt[:, k, :], w_in[:, k, 2 * D:4 * D]) for k in range(KT)]).then_inc(vf_mm, 1)

            def project_qk(n, c, b):
                bank_left(pe, "qk", n)
                for m in range(2):
                    product(tile["qk"][:, m * P:(m + 1) * P],
                            [(w_in[:, k, m * P:(m + 1) * P], f_xnt[:, k, :]) for k in range(KT)])
                product(tile["qk"][:, D:2 * D], [(f_xnt[:, k, :], w_in[:, k, D:2 * D]) for k in range(KT)])\
                    .then_inc(qk_mm, 1)

            def sum_gates(n, c, b):
                pe.wait_ge(g_ok, n + 1)
                bank_left(pe, "gates", n)
                product(tile["gates"][:, 0:D], [(tri_half[:, :], g_s[:, c % 2, :])])
                now_last = [c % 2] if c == 0 else [c % 2, 1 - c % 2]
                product(tile["gates"][:, D:2 * D], [(half[:, :], g_s[:, i, :]) for i in now_last]).then_inc(gates_mm, 1)

            def decay_columns(n, c, b):
                pe.wait_ge(gates_ok, n + 1)
                bank_left(pe, "decay_cols", n)
                flip(tile["decay_cols"], halves(decay), decay_mm)

            def ks_columns(n, c, b):
                pe.wait_ge(s_ok, n + 1)
                pe.wait_ge(qk_ok, n + 1)
                bank_left(pe, "ks_cols", n)
                flip(tile["ks_cols"], halves(k_s) + halves(s_s), ks_mm)

            def sum_states(n, c, b):
                pe.wait_ge(v_ok, n + 1)
                bank_left(pe, "sums", n)
                for m in range(2):
                    cols = slice(m * P, (m + 1) * P)
                    product(tile["sums"][:, cols], [(k_s[:, cols], s_s[:, cols])])
                    last = product(tile["sums"][:, D + m * P:D + (m + 1) * P], [(s_s[:, cols], v_s[:, cols])])
                last.then_inc(sums_mm, 1)

            def scores(n, c, b):
                pe.wait_ge(ks_ok, n + 1)
                bank_left(pe, "scores", n)
                for m in range(2):
                    last = product(tile["scores"][:, m * D:(m + 1) * D],
                                   [(ks_t[:, m, :], q_z[:, 2 * m:2 * m + 2, :].rearrange("p h t -> p (h t)"))])
                last.then_inc(scores_mm, 1)

            def logits(n, c, b):
                pe.wait_ge(a_ok, n + 1)
                pe.wait_ge(h_ok, n + 1)
                bank_left(pe, "logits", n)
                for h in range(H):
                    cols = slice(h * M, (h + 1) * M)
                    last = product(tile["logits"][:, cols], [
                        (a_s[:, h, :], s_s[:, cols]), (q_z[:, h, :], hk[:, h // 2, (h % 2) * M:(h % 2 + 1) * M])])
                last.then_inc(logits_mm, 1)

            def p_columns(n, c, b):
                pe.wait_ge(bp_ok, n + 1)
                bank_left(pe, "p_cols", n)
                flip(tile["p_cols"], halves(b_p), p_mm)

            def mix(n, c, b):
                pe.wait_ge(p_ok, n + 1)
                bank_left(pe, "mix", n)
                for m in range(2):
                    last = product(tile["mix"][:, m * D:(m + 1) * D],
                                   [(ks_t[:, 2 + m, :], p_z[:, 2 * m:2 * m + 2, :].rearrange("p h t -> p (h t)"))])
                last.then_inc(mix_mm, 1)

            def read_out(n, c, b):
                pe.wait_ge(mix_ok, n + 1)
                bank_left(pe, "read", n)
                for h in range(H):
                    cols = slice(h * M, (h + 1) * M)
                    last = product(tile["read"][:, cols], [
                        (bt_s[:, h, :], v_s[:, cols]), (p_z[:, h, :], hv[:, h // 2, (h % 2) * M:(h % 2 + 1) * M])])
                last.then_inc(read_mm, 1)

            def o_columns(n, c, b):
                pe.wait_ge(bo_ok, n + 1)
                bank_left(pe, "o_cols", n)
                flip(tile["o_cols"], halves(b_o[:, :, :].rearrange("p h m -> p (h m)")), o_mm)

            def project_o(n, c, b):
                pe.wait_ge(o_ok, n + 1)
                bank_left(pe, "y", n)
                product(tile["y"][:, 0:D], [(o_t[:, k, :], wo_s[:, k, :]) for k in range(2)]).then_inc(y_mm, 1)

            def x_columns(n, c, b):
                pe.wait_ge(x_normed, n + 1)
                bank_left(pe, "x_cols", n)
                flip(tile["x_cols"], halves(x_xn), x_cols_mm)

            def x_queries(n, c, b):
                pe.wait_ge(x_cols_ok, n + 1)
                bank_left(pe, "xq", n)
                for m in range(2):
                    last = product(tile["xq"][:, m * P:(m + 1) * P],
                                   [(xw[:, 0, k, m * P:(m + 1) * P], x_xnt[:, k, :]) for k in range(KT)])
                last.then_inc(xq_mm, 1)

            def x_scores(n, c, b):
                pe.wait_ge(xq_ok, n + 1)
                pe.wait_ge(kbd_ok, b * KT + KT)
                for k in range(KT):
                    bank_left(pe, f"x_scores{k}", n)
                    last = product(tile[f"x_scores{k}"], [(xq_t[:, k, :], k_bd[:, k, :, :].rearrange("p h k -> p (h k)"))])
                last.then_inc(xs_mm, 1)

            def e_columns(n, c, b):
                pe.wait_ge(ex_ok, n + 1)
                for k in range(2):
                    bank_left(pe, f"e_cols{k}", n)
                    for j in range(4):
                        pair = ex[:, 8 * k + 2 * j:8 * k + 2 * j + 2, :].rearrange("p h k -> p (h k)")
                        last = pe.transpose(tile[f"e_cols{k}"][:, j * P:(j + 1) * P], pair, ident[:, :])
                last.then_inc(et_mm, 1)

            def values(n, c, b):
                pe.wait_ge(et_ok, n + 1)
                pe.wait_ge(vbd_ok, b + 1)
                bank_left(pe, "values", n)
                for j in range(PAIRS):
                    last = product(tile["values"][:, j * VW:(j + 1) * VW], [(e_t[:, j, :], v_bd[:, j, :])])
                last.then_inc(av_mm, 1)

            def xo_columns(n, c, b):
                pe.wait_ge(xo_ok, n + 1)
                bank_left(pe, "xo_cols", n)
                flip(tile["xo_cols"], halves(x_o[:, :, :].rearrange("p j n -> p (j n)")), xot_mm)

            def x_project_o(n, c, b):
                pe.wait_ge(xot_ok, n + 1)
                bank_left(pe, "xy", n)
                product(tile["xy"][:, 0:D], [(xo_t[:, k, :], xw[:, 3, k, :]) for k in range(KT)]).then_inc(xy_mm, 1)

            def r_columns(n, c, b):
                pe.wait_ge(r_normed, n + 1)
                bank_left(pe, "r_cols", n)
                flip(tile["r_cols"], halves(r_xn[:, c % 2, 0, :]), r_cols_mm)

            def r_logits(n, c, b):
                pe.wait_ge(r_cols_ok, n + 1)
                bank_left(pe, "r_logits", n)
                product(tile["r_logits"][:, 0:E], [(r_xnt[:, k, :], wr_s[:, k, :]) for k in range(KT)]).then_inc(rlg_mm, 1)

            def counts(n, c, b):
                pe.wait_ge(both_ok, n + 1)
                bank_left(pe, "counts", n)
                product(tile["counts"][:, 0:E], [(before[:, :], both[:, :])])
                product(tile["counts"][:, E:2 * E], [(all_b[:, :], both[:, :])]).then_inc(cnt_mm, 1)

            def step(run):
                run(2, x_scores)
                run(0, f_columns)
                run(3, xo_columns)
                run(4, r_logits)
                run(0, project_vf)
                run(0, project_qk)
                run(1, o_columns)
                run(4, counts)
                run(0, sum_gates)
                run(3, x_project_o)
                run(0, decay_columns)
                run(0, ks_columns)
                run(1, project_o)
                run(0, scores)
                run(2, e_columns)
                run(0, logits)
                run(2, values)
                run(3, r_columns)
                run(1, x_columns)
                run(0, p_columns)
                run(1, x_queries)
                run(0, mix)
                run(0, sum_states)
                run(0, read_out)

            over_chunks(pe, step)

            def columns(g, par):
                pe.wait_ge(xe_landed[par], (g - par) * 8 + 16)
                if later(g, 1):
                    pe.wait_ge(xet_ok, g)
                flip(bank[0], [xe[:, par, a, k * P:(k + 1) * P] for k in range(KT) for a in range(2)], xet_mm)

            def hidden(g, j):
                par, w = j % 2, j // GPE
                pe.wait_ge(xet_ok, g + 1)
                for f in range(FT):
                    n = g * FT + f
                    if later(n, 4):
                        pe.wait_ge(gated_ok, n - 3)
                    to = bank[2 + f % 4]
                    for i, wt in enumerate((w1_s, w3_s)):
                        last = product(to[:, i * GS:(i + 1) * GS], [
                            (wt[w][:, k, f * P:(f + 1) * P], xe_t[:, par, k, :, :].rearrange("p a t -> p (a t)"))
                            for k in range(KT)])
                    last.then_inc(up_mm, 1)

            def results(d, j):
                g, par, w = d * GPL + j, j % 2, (j // GPE) % 2
                pe.wait_ge(gated_ok, g * FT + FT)
                pe.wait_ge(wdn_landed[w], (d + j // GPL) * 16 + 16)
                if later(g, 2):
                    pe.wait_ge(y_ok, g - 1)
                for a in range(2):
                    last = product(bank[6 + par][:, a * D:(a + 1) * D],
                                   [(h_t[:, par, f, a * P:(a + 1) * P], w2_s[w][:, f, :]) for f in range(FT)])
                last.then_inc(dn_mm, 1)

            def group(d, j):
                g = d * GPL + j
                if not is_last(g, NG - 1):
                    columns(g + 1, 1 - j % 2)
                if j % GPE == 0:
                    pe.wait_ge(wup_landed[j // GPE], d * 32 + 32)
                hidden(g, j)
                if later(g, 1):
                    results(d, j - 1)

            columns(0, 0)
            over_groups(pe, group)
            results(E // 2 - 1, GPL - 1)


def kernel(x, ctx_1024, itok_BxS_8_8191, itok_BxS2_1_8191, mask_BxSxS2_if1, L0_attn_Wq, L0_attn_Wk, L0_attn_Wv,
           L0_attn_Wf, L0_attn_g_norm_w, L0_attn_Wo, L0_xattn_W_q, L0_xattn_W_k, L0_xattn_W_v, L0_xattn_W_o,
           L0_ffn_Wr, L0_ffn_W1, L0_ffn_W3, L0_ffn_W2):
    import concourse.bacc as bacc
    from concourse.bass_utils import run_bass_kernel_spmd

    laid_out = {
        "x": x, "qpos": itok_BxS_8_8191.reshape(NCH, P).T, "kpos": itok_BxS2_1_8191, "mask": mask_BxSxS2_if1,
        "ctx_t": ctx_1024.reshape(B * KL, D).T, "wq": L0_attn_Wq, "wk": L0_attn_Wk, "wv": L0_attn_Wv,
        "wf": L0_attn_Wf, "gnorm": L0_attn_g_norm_w, "wo": L0_attn_Wo, "xwq_t": L0_xattn_W_q.T,
        "xwk_t": L0_xattn_W_k.T, "xwv_t": L0_xattn_W_v.T, "xwo_t": L0_xattn_W_o.T, "wr": L0_ffn_Wr,
        "w1": L0_ffn_W1, "w3": L0_ffn_W3, "w2": L0_ffn_W2,
    }
    nc = bacc.Bacc("TRN2", target_bir_lowering=False, num_devices=1)
    arrays, args = {}, []
    for name, a in laid_out.items():
        a = np.ascontiguousarray(a)
        arrays[f"in_{name}"] = a
        args.append(nc.dram_tensor(f"in_{name}", a.shape, mybir.dt.from_np(a.dtype), kind="ExternalInput").ap())
    args.append(nc.dram_tensor("out_dram", (B * T + P, D), F32, kind="ExternalOutput").ap())
    decoder_layer(nc, *args)
    return run_bass_kernel_spmd(nc, [arrays], core_ids=[0]).results[0]["out_dram"][:B * T].reshape(B, T, D)
```

```python
from contextlib import ExitStack

import concourse.bass as bass
import numpy as np
from concourse import mybir

ALU = mybir.AluOpType
ACT = mybir.ActivationFunctionType
AX = mybir.AxisListType
F32 = mybir.dt.float32
I32 = mybir.dt.int32
U32 = mybir.dt.uint32
F32R = mybir.dt.float32r
BF16 = mybir.dt.bfloat16

P = 128
B, T, D = 8, 512, 256
NCH = B * T // P
CPB = T // P
KT = D // P
H, M = 4, 64
PAIRS1 = H // 2
GATE_NORM = 8.0
EPS = 1e-5
XH, XD, KL = 16, 16, 64
HPT = P // XD
PAIRS = XH // 2
VW = 2 * XD + 2
XSCALE = 1.0 / 4.0
HIDDEN = 1.0e38
E, F, TOPK = 8, 1024, 2
CAP = -(-B * T * TOPK * 5 // (4 * E))
SLOTS = E * CAP
GS = 256
GPE = CAP // GS
NG = E * GPE
GPL = 2 * GPE
FT = F // P
CLAMP = 10000.0
X2_LAG = 3
LAGS = 4
ROW = D + 2
SPARE = B * T
ROUTE_STEPS = 11
PIECES = 6
SLOPE = [float(v) for v in np.float32(2.0 ** (-8.0 / XH)) ** np.arange(1, XH + 1, dtype=np.float32)]
SKIPPED = float(4 * SLOTS)


def decoder_layer(nc, x, qpos, kpos, mask, ctx_t, wq, wk, wv, wf, gnorm, wo,
                  xwq_t, xwk_t, xwv_t, xwo_t, wr, w1, w3, w2, out):
    xe_dram = nc.dram_tensor("expert_rows", (SLOTS, ROW), F32, kind="Internal").ap()
    ctx = ExitStack()
    with ctx:
        def sb(name, shape, dt=F32):
            return ctx.enter_context(nc.sbuf_tensor(name, shape, dt))

        def sem(name):
            return ctx.enter_context(nc.semaphore(name))

        ident = sb("ident", [P, P])
        half = sb("half", [P, P])
        neg_half = sb("neg_half", [P, 4])
        idle_v, idle_g = sb("idle_v", [P, 1]), sb("idle_g", [P, 2])
        raw = [sb(f"raw{m}", [P, 2, 4 * D]) for m in range(3)]
        w_even = [[sb(f"w{m}_even_{part}", [P, 2, 4 * D], F32R) for part in ("hi", "lo")] for m in range(3)]
        tiles1 = ExitStack()

        def part1(name, shape, dt=F32):
            return tiles1.enter_context(nc.sbuf_tensor(name, shape, dt))

        causal = part1("causal", [P, P])
        tri_half = part1("tri_half", [P, P])
        ones = part1("ones", [P, P])
        before = part1("before", [P, P], BF16)
        all_b = part1("all_b", [P, P], BF16)
        diag16 = part1("diag16", [P, HPT])
        pair_of = part1("pair_of", [P, 2])
        slopes = part1("slopes", [P, XH])
        expert_no = part1("expert_no", [P, E])
        w_in = part1("w_in", [P, KT, 4 * D])
        wo_raw = part1("wo_raw", [P, KT, D])
        gn = part1("gn", [P, 1])
        wo_s = part1("wo_s", [P, KT, D])
        xw = part1("xw", [P, 4, KT, D])
        wr_s = part1("wr_s", [P, KT, E])
        ctx_s = part1("ctx_s", [P, KT, B * KL])
        ctx2 = raw[0][:, :, :].rearrange("p k (b i n) -> p k b i n", b=B, i=2)
        kp_i = part1("kp_i", [P, B * KL], I32)
        kp = part1("kp", [P, B, KL])
        qp_i = part1("qp_i", [P, NCH], I32)
        qp = part1("qp", [P, NCH])
        token_no = part1("token_no", [P, NCH])
        empty = part1("empty", [P, ROW])
        k_all = part1("k_all", [P, KT, B * KL])
        v_all = part1("v_all", [P, B, PAIRS, VW])
        xin = part1("xin", [P, 4, D])
        f_st, f_mv, f_var, f_rstd = (part1(t, [P, w]) for t, w in (("f_st", 6), ("f_mv", 2), ("f_var", 1), ("f_rstd", 1)))
        f_xn = part1("f_xn", [P, D])
        f_xnt = part1("f_xnt", [P, KT, P])
        qk_e, qk_l, qk_s = (part1(t, [P, 2 * D]) for t in ("qk_e", "qk_l", "qk_s"))
        q_t = part1("q_t", [P, 2, PAIRS1, P])
        k_s, v_s = part1("k_s", [P, 2, D]), part1("v_s", [P, 2, D])
        f_abs, f_e, f_l = (part1(t, [P, D]) for t in ("f_abs", "f_e", "f_l"))
        g_s = part1("g_s", [P, 2, D])
        one_less = part1("one_less", [P, D])
        up, down = part1("up", [P, 2, D]), part1("down", [P, D])
        decay = part1("decay", [P, D])
        s_s = part1("s_s", [P, 2, D])
        k_z, s_z = part1("k_z", [P, H, P]), part1("s_z", [P, H, P])
        a_s = part1("a_s", [P, H, P])
        zk, zv = part1("zk", [P, 2, P]), part1("zv", [P, 2, P])
        hk, hv = ([part1(f"{t}{i}", [P, 2, P]) for i in range(2)] for t in ("hk", "hv"))
        lg, lg_d, b_e = (part1(t, [P, H, M]) for t in ("lg", "lg_d", "b_e"))
        lg_m, b_sum, b_rec, b_ss, b_t1, b_t2, b_ms, b_rms, b_w = (
            part1(t, [P, H]) for t in ("lg_m", "b_sum", "b_rec", "b_ss", "b_t1", "b_t2", "b_ms", "b_rms", "b_w"))
        b_p = part1("b_p", [P, D])
        p_t = part1("p_t", [P, PAIRS1, P])
        bt_s = part1("bt_s", [P, H, P])
        b_sq, b_o = part1("b_sq", [P, H, M]), part1("b_o", [P, H, M])
        o_t = part1("o_t", [P, 2, P])
        x1 = part1("x1", [P, 2, D])
        x_st, x_mv, x_var, x_rstd = (part1(t, [P, w]) for t, w in (("x_st", 6), ("x_mv", 2), ("x_var", 1), ("x_rstd", 1)))
        x_xn = part1("x_xn", [P, D])
        x_xnt, xq_t = part1("x_xnt", [P, KT, P]), part1("xq_t", [P, KT, P])
        k_bd = part1("k_bd", [P, KT, HPT, KL])
        v_bd = part1("v_bd", [P, PAIRS, VW])
        mask_i = part1("mask_i", [P, 2, KL], I32)
        hid, dist = part1("hid", [P, KL]), part1("dist", [P, KL])
        bias, sc, ex = (part1(t, [P, XH, KL]) for t in ("bias", "sc", "ex"))
        sc_m, x_den, x_rec = (part1(t, [P, XH]) for t in ("sc_m", "x_den", "x_rec"))
        e_t = part1("e_t", [P, PAIRS, P])
        x_o = part1("x_o", [P, PAIRS, 2 * XD])
        xo_t = part1("xo_t", [P, KT, P])
        r_st, r_mv, r_var, r_rstd = part1("r_st", [P, 6]), part1("r_mv", [P, 2]), part1("r_var", [P, 1]), part1("r_rstd", [P, 1])
        x2 = part1("x2", [P, 2, D])
        r_xn = part1("r_xn", [P, 2, 2, ROW])
        r_xnt = part1("r_xnt", [P, KT, P])
        r_lg, top, top_i = part1("r_lg", [P, E]), part1("top", [P, 8]), part1("top_i", [P, 8], U32)
        top_f = part1("top_f", [P, 2])
        hot = part1("hot", [P, 2, E])
        both = part1("both", [P, E], BF16)
        taken = part1("taken", [P, E])
        place = part1("place", [P, E])
        place_h = part1("place_h", [P, 2, E])
        pos = part1("pos", [P, 2])
        base = part1("base", [P, 2])
        slot_f, off_f = part1("slot_f", [P, 2]), part1("off_f", [P, 2])
        send = part1("send", [P, 2, 2], U32)
        gap, r_e, r_den, r_p = part1("gap", [P, 1]), part1("r_e", [P, 1]), part1("r_den", [P, 1]), part1("r_p", [P, 1])
        tiles1.close()
        w_odd = [[sb(f"w{m}_odd_{part}", [P, 2, 4 * D], F32R) for part in ("hi", "lo")] for m in range(3)]
        w_s = [w_even, w_odd]
        xe = sb("xe", [P, 2, 2, ROW])
        about = sb("about", [P, 2, 2, 2])
        token = [[sb(f"token{i}{a}", [P, 1], U32) for a in range(2)] for i in range(2)]
        xe_t = [sb(f"xe_t_{part}", [P, 2, KT, GS], F32R) for part in ("hi", "lo")]
        h_a, h_f = sb("h_a", [P, 2, GS]), sb("h_f", [P, 2, GS])
        h_t = [sb(f"h_t_{part}", [P, 2, FT, GS], F32R) for part in ("hi", "lo")]
        y_s = sb("y_s", [P, 2, 2, D])

        bank = [ctx.enter_context(nc.psum_tensor(f"bank{i}", [P, 512], F32)) for i in range(8)]
        turns = [
            [("counts", 4), ("e_cols0", 2), ("read", 0)],
            [("xo_cols", 3), ("qk", 0), ("scores", 0)],
            [("vf", 0), ("ks_cols", 0), ("logits", 0), ("r_cols", 3)],
            [("o_cols", 1), ("values", 2), ("sums", 0)],
            [("f_cols", 0), ("decay_cols", 0), ("mix", 0)],
            [("x_scores1", 2), ("p_cols", 0)],
            [("x_scores0", 2), ("gates", 0), ("y", 1), ("e_cols1", 2), ("xq", 1)],
            [("r_logits", 4), ("xy", 3), ("x_cols", 1)],
        ]
        tile = {t: bank[i][:, :] for i, turn in enumerate(turns) for t, _ in turn}

        consts_made, w_landed, ctx_landed, zeros_sent = sem("consts_made"), sem("w_landed"), sem("ctx_landed"), sem("zeros_sent")
        consts_step = sem("consts_step")
        small_made, ctx_doubled, ctx_mm, v_made = sem("small_made"), sem("ctx_doubled"), sem("ctx_mm"), sem("v_made")
        k_made = sem("k_made")
        x_landed = [sem(f"x_landed{i}") for i in range(4)]
        mask_landed = [sem(f"mask_landed{i}") for i in range(2)]
        def sems(names):
            return [sem(t) for t in names.split()]

        f_stats, f_vared, f_rstded, f_normed, f_cols_mm, f_cols_ok, qk_mm, vf_mm = sems(
            "f_stats f_vared f_rstded f_normed f_cols_mm f_cols_ok qk_mm vf_mm")
        e_ok, l_ok, sig_ok, v_ok, abs_ok, fe_ok, fl_ok, g_ok, qk_ok = sems(
            "e_ok l_ok sig_ok v_ok abs_ok fe_ok fl_ok g_ok qk_ok")
        gates_mm, less_ok, gates_ok, s_ok, decay_mm, h_ok, ks_mm, ks_ok, sums_mm, z_ok, scores_mm, a_ok = sems(
            "gates_mm less_ok gates_ok s_ok decay_mm h_ok ks_mm ks_ok sums_mm z_ok scores_mm a_ok")
        logits_mm, lg_ok, lgm_ok, lgd_ok, be_ok, bsum_ok, brec_ok, bp_ok, p_mm, p_ok, mix_mm, mix_ok = sems(
            "logits_mm lg_ok lgm_ok lgd_ok be_ok bsum_ok brec_ok bp_ok p_mm p_ok mix_mm mix_ok")
        read_mm, sq_ok, rms_step, ms_ok, rms_ok, bw_ok, bo_ok, o_mm, o_ok, y_mm, x1_ok = sems(
            "read_mm sq_ok rms_step ms_ok rms_ok bw_ok bo_ok o_mm o_ok y_mm x1_ok")
        x_stats, x_vared, x_rstded, x_normed, x_cols_mm, x_cols_ok, xq_mm, xq_ok = sems(
            "x_stats x_vared x_rstded x_normed x_cols_mm x_cols_ok xq_mm xq_ok")
        kbd_ok, vbd_ok, hid_ok, dist_ok, bias_ok, xs_mm, sc_ok, scm_ok, scd_ok, ex_ok = sems(
            "kbd_ok vbd_ok hid_ok dist_ok bias_ok xs_mm sc_ok scm_ok scd_ok ex_ok")
        et_mm, et_ok, av_mm, xden_ok, xrec_ok, xo_ok, xot_mm, xot_ok, xy_mm, x2_ok = sems(
            "et_mm et_ok av_mm xden_ok xrec_ok xo_ok xot_mm xot_ok xy_mm x2_ok")
        r_stats, r_vared, r_rstded, r_normed, r_cols_mm, r_cols_ok, rlg_mm, rlg_ok = sems(
            "r_stats r_vared r_rstded r_normed r_cols_mm r_cols_ok rlg_mm rlg_ok")
        topi_ok, both_ok, gap_ok, re_ok, cnt_mm, place_ok, taken_ok, slots_ok, route_step, halves_zeroed = sems(
            "topi_ok both_ok gap_ok re_ok cnt_mm place_ok taken_ok slots_ok route_step halves_zeroed")
        down_ok, decay_ok, kz_ok = sems("down_ok decay_ok kz_ok")
        left = dict(f_cols=f_cols_ok, qk=qk_ok, vf=g_ok, gates=gates_ok, decay_cols=h_ok, ks_cols=ks_ok, sums=z_ok,
                    scores=a_ok, logits=lg_ok, p_cols=p_ok, mix=mix_ok, read=bo_ok, o_cols=o_ok, y=x1_ok,
                    x_cols=x_cols_ok, xq=xq_ok, x_scores0=sc_ok, x_scores1=sc_ok, e_cols0=et_ok, e_cols1=et_ok,
                    values=xo_ok, xo_cols=xot_ok, xy=x2_ok, r_cols=r_cols_ok, r_logits=rlg_ok, counts=taken_ok)
        sent = [sem(f"sent{i}") for i in range(4)]
        raw_landed = [sem(f"raw_landed{m}") for m in range(3)]
        w_hi_ok, w_lo_ok, xe_hi_ok, h_hi_ok, h_lo_ok = sems("w_hi_ok w_lo_ok xe_hi_ok h_hi_ok h_lo_ok")
        xe_landed = [sem(f"xe_landed{i}") for i in range(2)]
        xet_mm, xet_ok, up_mm, silu_ok, gated_ok, dn_mm, y_ok = sems("xet_mm xet_ok up_mm silu_ok gated_ok dn_mm y_ok")
        about_ok, added, held = sem("about_ok"), sem("added"), sem("held")
        x2_stored = [sem(f"x2_stored{i}") for i in range(2)]
        spare_stored = sem("spare_stored")

        def over_chunks(eng, step):
            def at(b, c):
                def run(lag, work):
                    n = b * CPB + c - lag
                    if not isinstance(n, int) or 0 <= n < NCH:
                        work(n, (c - lag) % CPB, b + (c - lag) // CPB)
                return run

            for c in range(2 * CPB):
                step(at(c // CPB, c % CPB))
            with eng.Fori(2, B) as b:
                for c in range(CPB):
                    step(at(b, c))
            for c in range(LAGS):
                step(at(B, c))

        def bank_left(pe, name, n):
            turn = next(t for t in turns if name in [x for x, _ in t])
            i = [x for x, _ in turn].index(name)
            lag = turn[i][1]
            for j, (other, other_lag) in enumerate(turn):
                m = n + lag - other_lag - (1 if j >= i else 0)
                if isinstance(n, int):
                    m = min(m, NCH - 1)
                    if m >= 0:
                        pe.wait_ge(left[other], m + 1)
                elif j == (i - 1) % len(turn):
                    pe.wait_ge(left[other], m + 1)

        def over_groups(eng, step):
            for j in range(GPL):
                step(0, j)
            with eng.Fori(1, E // 2 - 1) as d:
                for j in range(GPL):
                    step(d, j)
            for j in range(GPL):
                step(E // 2 - 1, j)

        def splits(d, j, f):
            e, g = 2 * d + j // GPE, j % GPE
            if g in (1, 2, 3) and f in (3, 6) and not is_last(e, E - 1):
                return e + 1, (g - 1) * 2 + (f == 6)
            return None

        def later(n, k):
            return not isinstance(n, int) or n >= k

        def is_last(n, last):
            return isinstance(n, int) and n == last

        CONSTS = 15 + XH
        W_LOADS = 12
        x_rows = x.rearrange("b (c p) d -> (b c p) d", p=P)
        mask_rows = mask.rearrange("b t k -> (b t) k")

        block = ctx.enter_context(nc.Block())

        @block.sync
        def _(sp):
            def feat(w):
                return w.rearrange("(k p) n -> p k n", p=P)

            def load_x(n, c):
                sp.dma_start(xin[:, c, :], x_rows[bass.ds(n * P, P), :]).then_inc(x_landed[c], 16)

            sp.dma_start(ctx_s[:, :, :], feat(ctx_t)).then_inc(ctx_landed, 16)
            for j, w in ((1, xwk_t), (2, xwv_t)):
                sp.dma_start(xw[:, j, :, :], feat(w)).then_inc(ctx_landed, 16)
            load_x(0, 0)
            for j, w in enumerate((wq, wk, wv, wf)):
                sp.dma_start(w_in[:, :, j * D:(j + 1) * D], feat(w)).then_inc(w_landed, 16)
            sp.dma_start(wo_raw[:, :, :], feat(wo)).then_inc(w_landed, 16)
            gcol = gnorm.rearrange("(m a) -> m a", a=1)
            sp.dma_start(gn[0:M, :], gcol).then_inc(w_landed, 16)
            sp.dma_start(gn[M:2 * M, :], gcol).then_inc(w_landed, 16)
            for j, w in ((0, xwq_t), (3, xwo_t)):
                sp.dma_start(xw[:, j, :, :], feat(w)).then_inc(w_landed, 16)
            sp.dma_start(wr_s[:, :, :], feat(wr)).then_inc(w_landed, 16)
            sp.dma_start(kp_i[:, :], kpos.rearrange("(a b) k -> a (b k)", a=1).to_broadcast([P, B * KL]))\
              .then_inc(w_landed, 16)
            sp.dma_start(qp_i[:, :], qpos).then_inc(w_landed, 16)
            sp.wait_ge(consts_made, 3)
            per = SLOTS // P
            for j in range(4):
                rows = xe_dram[j * SLOTS // 4:(j + 1) * SLOTS // 4, :].rearrange("(r p) d -> p r d", p=P)
                sp.dma_start(rows, empty[:, :].rearrange("p (r d) -> p r d", r=1).to_broadcast([P, per // 4, ROW]))\
                  .then_inc(zeros_sent, 16)
            sp.dma_start(out[SPARE:SPARE + P, :], empty[:, 0:D]).then_inc(spare_stored, 16)

            def store_x2(n, par):
                sp.wait_ge(x2_ok, n + 1)
                sp.dma_start(out[bass.ds(n * P, P), :], x2[:, par, :]).then_inc(x2_stored[par], 16)

            def step(b, c, x_on=True):
                s = b * CPB + c
                if x_on:
                    nxt = (c + 1) % 4
                    if later(s, 3):
                        sp.wait_ge(x1_ok, s - 2)
                    sp.dma_start(xin[:, nxt, :], x_rows[bass.ds((s + 1) * P, P), :]).then_inc(x_landed[nxt], 16)
                if later(s, 2):
                    sp.wait_ge(hid_ok, s - 1)
                sp.dma_start(mask_i[:, c % 2, :], mask_rows[bass.ds(s * P, P), :]).then_inc(mask_landed[c % 2], 16)
                if later(s, X2_LAG):
                    store_x2(s - X2_LAG, (c - X2_LAG) % 2)

            for c in range(2 * CPB):
                step(c // CPB, c % CPB)
            with sp.Fori(2, B - 1) as b:
                for c in range(CPB):
                    step(b, c)
            for c in range(CPB):
                step(B - 1, c, c < CPB - 1)
            for n in range(NCH - X2_LAG, NCH):
                store_x2(n, n % 2)

            def load_expert(e):
                for m, (w, tiles) in enumerate(((w1, KT), (w3, KT), (w2, FT))):
                    sp.dma_start(raw[m][:, :, :].rearrange("p i n -> p (i n)").rearrange("p (k n) -> p k n", k=tiles),
                                 w[bass.ds(e, 1), :, :].rearrange("a (k p) n -> p (a k) n", p=P))\
                      .then_inc(raw_landed[m], 16)

            def load_group(g, par):
                sp.dma_start(xe[:, par, :, :], xe_dram[bass.ds(g * GS, GS), :].rearrange("(a p) d -> p a d", p=P))\
                  .then_inc(xe_landed[par], 16)

            load_expert(0)
            for i in range(4):
                sp.wait_ge(sent[i], 16 * NCH // 2)
            for g in range(2):
                load_group(g, g)

            def group(d, j):
                g, par = d * GPL + j, j % 2
                if not isinstance(g, int) or g + 2 < NG:
                    sp.wait_ge(xet_mm, g + 1)
                    sp.wait_ge(about_ok, g + 1)
                    load_group(g + 2, par)
                if j % GPE == 0 and not (isinstance(d, int) and 2 * d + j // GPE == E - 1):
                    e = 2 * d + j // GPE
                    sp.wait_ge(w_lo_ok, (e + 1) * PIECES)
                    load_expert(e + 1)

            over_groups(sp, group)

        @block.gpsimd
        def _(pool):
            pool.memset(empty[:, :], 0.0).then_inc(consts_made, 1)
            pool.wait_ge(consts_made, 1)
            pool.iota(empty[:, D:D + 1], [[0, 1]], base=SPARE, channel_multiplier=1,
                      allow_small_or_imprecise_dtypes=True).then_inc(consts_made, 1)
            pool.iota(token_no[:, :], [[P, NCH]], base=0, channel_multiplier=1,
                      allow_small_or_imprecise_dtypes=True).then_inc(consts_made, 1)
            pool.memset(ident[:, :], 0.0).then_inc(consts_step, 1)
            pool.memset(ones[:, :], 1.0).then_inc(consts_step, 1)
            pool.memset(all_b[:, :], 1.0).then_inc(consts_step, 1)
            pool.memset(half[:, :], 0.5).then_inc(consts_step, 1)
            pool.memset(neg_half[:, :], -0.5).then_inc(consts_step, 1)
            pool.memset(taken[:, :], 0.0).then_inc(consts_step, 1)
            for h in range(XH):
                pool.memset(slopes[:, h:h + 1], SLOPE[h]).then_inc(consts_step, 1)
            pool.iota(expert_no[:, :], [[1, E]], base=0, channel_multiplier=0,
                      allow_small_or_imprecise_dtypes=True).then_inc(consts_step, 1)
            pool.wait_ge(consts_step, 7 + XH)
            pool.affine_select(out=ident[:, :], in_=ident[:, :], compare_op=ALU.not_equal, fill=1.0,
                               base=0, pattern=[[-1, P]], channel_multiplier=1).then_inc(consts_step, 1)
            pool.affine_select(out=causal[:, :], in_=ones[:, :], compare_op=ALU.is_ge, fill=0.0,
                               base=0, pattern=[[1, P]], channel_multiplier=-1).then_inc(consts_step, 1)
            pool.affine_select(out=tri_half[:, :], in_=half[:, :], compare_op=ALU.is_ge, fill=-0.5,
                               base=0, pattern=[[1, P]], channel_multiplier=-1).then_inc(consts_step, 1)
            pool.affine_select(out=before[:, :], in_=all_b[:, :], compare_op=ALU.is_gt, fill=0.0,
                               base=0, pattern=[[1, P]], channel_multiplier=-1).then_inc(consts_step, 1)
            for tile, n, w in ((diag16, HPT, XD), (pair_of, 2, KL)):
                pool.affine_select(out=tile[:, :], in_=ones[:, 0:n], compare_op=ALU.is_ge, fill=0.0,
                                   base=0, pattern=[[-w, n]], channel_multiplier=1).then_inc(consts_step, 1)
            pool.wait_ge(consts_step, 13 + XH)
            for tile, n, w in ((diag16, HPT, XD), (pair_of, 2, KL)):
                pool.affine_select(out=tile[:, :], in_=tile[:, :], compare_op=ALU.is_ge, fill=0.0,
                                   base=w - 1, pattern=[[w, n]], channel_multiplier=-1).then_inc(consts_step, 1)

            pool.wait_ge(consts_step, CONSTS)

            def hold(i):
                return pool.tensor_tensor(idle_g[:, i:i + 1], half[:, 0:1], half[:, 0:1], ALU.add)

            def power(n, var, rstd, ready, done, used):
                if later(n, 1):
                    pool.wait_ge(used, n)
                pool.wait_ge(ready, n + 1)
                pool.tensor_tensor(rstd[:, :], var[:, :], neg_half[:, 0:var.shape[1]], ALU.pow).then_inc(done, 1)

            def f_power(n, c, b):
                power(n, f_var, f_rstd, f_vared, f_rstded, f_normed)

            def x_power(n, c, b):
                power(n, x_var, x_rstd, x_vared, x_rstded, x_normed)

            def r_power(n, c, b):
                power(n, r_var, r_rstd, r_vared, r_rstded, r_normed)

            def head_power(n, c, b):
                power(n, b_ms, b_rms, ms_ok, rms_ok, bw_ok)

            def keys(n, c, b):
                if c == 0:
                    if later(n, 1):
                        pool.wait_ge(xs_mm, n)
                    else:
                        pool.wait_ge(k_made, 1)
                    for h in range(KT):
                        pool.tensor_tensor(
                            k_bd[:, h, :, :],
                            k_all[:, h, bass.ds(b * KL, KL)].rearrange("p (a k) -> p a k", a=1)
                            .to_broadcast([P, HPT, KL]),
                            diag16[:, :].rearrange("p (h a) -> p h a", a=1).to_broadcast([P, HPT, KL]),
                            ALU.mult).then_inc(kbd_ok, 1)

            def values(n, c, b):
                if c == 0:
                    if later(n, 1):
                        pool.wait_ge(av_mm, n)
                    else:
                        pool.wait_ge(v_made, 2 * B)
                    pool.tensor_copy(v_bd[:, :, :].rearrange("p j n -> p (j n)"),
                                     v_all[:, bass.ds(b, 1), :, :].rearrange("p a j n -> p (a j n)"))\
                        .then_inc(vbd_ok, 1)

            def biases(n, c, b):
                pool.wait_ge(dist_ok, n + 1)
                if later(n, 1):
                    pool.wait_ge(sc_ok, n)
                pool.tensor_tensor(
                    bias[:, :, :],
                    dist[:, :].rearrange("p (a k) -> p a k", a=1).to_broadcast([P, XH, KL]),
                    slopes[:, :].rearrange("p (h a) -> p h a", a=1).to_broadcast([P, XH, KL]),
                    ALU.mult).then_inc(bias_ok, 1)

            def less_max(n, c, b):
                pool.wait_ge(scm_ok, n + 1)
                pool.tensor_tensor(
                    sc[:, :, :], sc[:, :, :],
                    sc_m[:, :].rearrange("p (h a) -> p h a", a=1).to_broadcast([P, XH, KL]),
                    ALU.subtract).then_inc(scd_ok, 1)

            def send_rows(n, c, b):
                par = c % 2
                if not later(n, 1):
                    pool.wait_ge(zeros_sent, 64)
                pool.wait_ge(slots_ok, n + 1)
                hold(0)
                for k in range(2):
                    pool.indirect_dma_start(
                        out=xe_dram, out_offset=bass.IndirectOffsetOnAxis(ap=send[:, par, k:k + 1], axis=0),
                        in_=r_xn[:, par, k, :], in_offset=None, bounds_check=SLOTS - 1, oob_is_err=False)\
                        .then_inc(sent[2 * par + k], 16)

            def step(run):
                run(0, f_power)
                run(2, values)
                run(1, head_power)
                run(2, less_max)
                run(4, send_rows)
                run(1, keys)
                run(3, r_power)
                run(1, x_power)
                run(1, biases)

            over_chunks(pool, step)

            for i in range(2):
                pool.wait_ge(x2_stored[i], 16 * NCH // 2)
            pool.wait_ge(spare_stored, 16)

            def add_rows(g, par):
                pool.wait_ge(y_ok, g + 1)
                for a in range(2):
                    if a or later(g, 1):
                        pool.wait_ge(added, g * 32 + a * 16)
                        pool.wait_ge(held, g * 2 + a)
                    hold(1).then_inc(held, 1)
                    pool.indirect_dma_start(
                        out=out, out_offset=bass.IndirectOffsetOnAxis(ap=token[par][a][:, :], axis=0),
                        in_=y_s[:, par, a, :], in_offset=None, compute_op=ALU.add).then_inc(added, 16)

            def group(d, j):
                add_rows(d * GPL + j, j % 2)

            over_groups(pool, group)
            pool.wait_ge(added, NG * 32)

        @block.scalar
        def _(act):
            act.preload_act_table_set("natural_log_exp_and_others")

            def evacuate(n, dst, src, ready, used, done, amount=1.0):
                if later(n, 1):
                    act.wait_ge(used, n)
                act.wait_ge(ready, n + 1)
                act.activation(dst, src, ACT.Copy, scale=amount).then_inc(done, 1)

            def two(t):
                return t.rearrange("p (k t) -> p k t", k=2)

            def f_columns(n, c, b):
                evacuate(n, f_xnt[:, :, :], two(tile["f_cols"][:, 0:D]), f_cols_mm, qk_mm, f_cols_ok)

            def x_columns(n, c, b):
                evacuate(n, x_xnt[:, :, :], two(tile["x_cols"][:, 0:D]), x_cols_mm, xq_mm, x_cols_ok)

            def r_columns(n, c, b):
                evacuate(n, r_xnt[:, :, :], two(tile["r_cols"][:, 0:D]), r_cols_mm, rlg_mm, r_cols_ok)

            def x_queries(n, c, b):
                evacuate(n, xq_t[:, :, :], two(tile["xq"][:, 0:D]), xq_mm, xs_mm, xq_ok, XSCALE)

            def o_columns(n, c, b):
                evacuate(n, o_t[:, :, :], two(tile["o_cols"][:, 0:D]), o_mm, y_mm, o_ok)

            def xo_columns(n, c, b):
                evacuate(n, xo_t[:, :, :], two(tile["xo_cols"][:, 0:D]), xot_mm, xy_mm, xot_ok)

            def ks_columns(n, c, b):
                if later(n, 1):
                    act.wait_ge(mix_mm, n)
                else:
                    act.wait_ge(halves_zeroed, 6)
                act.wait_ge(ks_mm, n + 1)
                for t, dst, done in ((0, k_z, kz_ok), (1, s_z, ks_ok)):
                    for i in range(2):
                        rows = slice(M * i, M * i + M)
                        last = act.activation(dst[rows, i::2, :], two(tile["ks_cols"][rows, t * D:(t + 1) * D]), ACT.Copy)
                    last.then_inc(done, 1)

            def e_columns(n, c, b):
                if later(n, 1):
                    act.wait_ge(av_mm, n)
                act.wait_ge(et_mm, n + 1)
                for k in range(2):
                    last = act.activation(e_t[:, 4 * k:4 * k + 4, :],
                                          tile[f"e_cols{k}"].rearrange("p (k t) -> p k t", k=4), ACT.Copy)
                last.then_inc(et_ok, 1)

            def p_columns(n, c, b):
                evacuate(n, p_t[:, :, :], two(tile["p_cols"][:, 0:D]), p_mm, read_mm, p_ok)

            def f_absolute(n, c, b):
                act.wait_ge(vf_mm, n + 1)
                act.activation(f_abs[:, :], tile["vf"][:, D:2 * D], ACT.Abs).then_inc(abs_ok, 1)
                if later(n, 2):
                    act.wait_ge(read_mm, n - 1)
                act.activation(v_s[:, c % 2, :], tile["vf"][:, 0:D], ACT.Copy).then_inc(v_ok, 1)
                act.wait_ge(abs_ok, n + 1)
                act.activation(f_e[:, :], f_abs[:, :], ACT.Exp, scale=-1.0).then_inc(fe_ok, 1)
                act.wait_ge(fe_ok, n + 1)
                if later(n, 1):
                    act.wait_ge(g_ok, n)
                act.activation(f_l[:, :], f_e[:, :], ACT.Ln, bias=1.0).then_inc(fl_ok, 1)

            def qk_sigmoid(n, c, b):
                act.wait_ge(qk_mm, n + 1)
                act.activation(qk_e[:, :], tile["qk"], ACT.Exp, scale=-1.0).then_inc(e_ok, 1)
                act.wait_ge(e_ok, n + 1)
                act.activation(qk_l[:, :], qk_e[:, :], ACT.Ln, bias=1.0).then_inc(l_ok, 1)
                act.wait_ge(l_ok, n + 1)
                if later(n, 1):
                    act.wait_ge(qk_ok, n)
                act.activation(qk_s[:, :], qk_l[:, :], ACT.Exp, scale=-1.0).then_inc(sig_ok, 1)

            def one_minus(n, c, b):
                act.wait_ge(g_ok, n + 1)
                if later(n, 1):
                    act.wait_ge(s_ok, n)
                act.activation(one_less[:, :], g_s[:, c % 2, :], ACT.Exp, scale=1 / GATE_NORM).then_inc(less_ok, 1)

            def gates(n, c, b):
                act.wait_ge(gates_mm, n + 1)
                if later(n, 1):
                    act.wait_ge(s_ok, n)
                    act.wait_ge(h_ok, n)
                grow = tile["gates"][:, 0:D]
                act.activation(down[:, :], grow, ACT.Exp, scale=-1 / GATE_NORM).then_inc(down_ok, 1)
                act.activation(decay[:, :], tile["gates"][:, D:2 * D], ACT.Exp, scale=1 / GATE_NORM)\
                   .then_inc(decay_ok, 1)
                if later(n, 2):
                    act.wait_ge(bp_ok, n - 1)
                act.activation(up[:, c % 2, :], grow, ACT.Exp, scale=1 / GATE_NORM).then_inc(gates_ok, 1)

            def softmax_exp(n, c, b):
                act.wait_ge(lgd_ok, n + 1)
                if later(n, 1):
                    act.wait_ge(bp_ok, n)
                    act.wait_ge(bsum_ok, n)
                act.activation(b_e[:, :, :], lg_d[:, :, :], ACT.Exp, scale=float(M) ** -0.5).then_inc(be_ok, 1)

            def squares(n, c, b):
                act.wait_ge(read_mm, n + 1)
                if later(n, 1):
                    act.wait_ge(rms_step, 3 * n)
                act.activation(b_sq[:, :, :], tile["read"][:, 0:D].rearrange("p (h m) -> p h m", h=H), ACT.Square)\
                    .then_inc(sq_ok, 1)

            def x_exp(n, c, b):
                act.wait_ge(scd_ok, n + 1)
                if later(n, 1):
                    act.wait_ge(et_mm, n)
                act.activation(ex[:, :, :], sc[:, :, :], ACT.Exp).then_inc(ex_ok, 1)

            def router_exp(n, c, b):
                act.wait_ge(gap_ok, n + 1)
                if later(n, 1):
                    act.wait_ge(slots_ok, n)
                act.activation(r_e[:, :], gap[:, :], ACT.Exp).then_inc(re_ok, 1)

            def step(run):
                run(0, f_columns)
                run(3, xo_columns)
                run(0, f_absolute)
                run(4, router_exp)
                run(0, qk_sigmoid)
                run(0, one_minus)
                run(0, gates)
                run(1, o_columns)
                run(2, x_exp)
                run(0, ks_columns)
                run(2, e_columns)
                run(1, x_columns)
                run(0, softmax_exp)
                run(3, r_columns)
                run(0, p_columns)
                run(1, x_queries)
                run(0, squares)

            over_chunks(act, step)

            def split_weights(e, par, piece):
                m, i = piece // 2, piece % 2
                act.wait_ge(raw_landed[m], e * 16 + 16)
                act.activation(w_s[par][m][0][:, i, :], raw[m][:, i, :], ACT.Copy).then_inc(w_hi_ok, 1)

            def columns(g, par):
                act.wait_ge(xet_mm, g + 1)
                if later(g, 2):
                    act.wait_ge(up_mm, (g - 1) * FT)
                act.activation(xe_t[0][:, par, :, :].rearrange("p k t -> p (k t)"), bank[0][:, :], ACT.Copy)\
                   .then_inc(xe_hi_ok, 1)

            def hidden_high(g, par, f):
                act.wait_ge(gated_ok, g * FT + f + 1)
                if f == 0 and later(g, 2):
                    act.wait_ge(dn_mm, g - 1)
                act.activation(h_t[0][:, par, f, :], h_f[:, f % 2, :], ACT.Copy).then_inc(h_hi_ok, 1)

            for piece in range(PIECES):
                split_weights(0, 0, piece)
            columns(0, 0)

            def group(d, j):
                g, par = d * GPL + j, j % 2
                for f in range(FT):
                    n = g * FT + f
                    act.wait_ge(up_mm, n + 1)
                    if later(n, 2):
                        act.wait_ge(gated_ok, n - 1)
                    act.activation(h_a[:, f % 2, :], bank[2 + f % 4][:, 0:GS], ACT.Silu).then_inc(silu_ok, 1)
                    if f:
                        hidden_high(g, par, f - 1)
                    if f == 1 and not is_last(g, NG - 1):
                        columns(g + 1, 1 - par)
                    if splits(d, j, f):
                        e, piece = splits(d, j, f)
                        if piece == 0 and later(g, GPE):
                            act.wait_ge(dn_mm, g - 1)
                        split_weights(e, 1 - j // GPE, piece)
                hidden_high(g, par, FT - 1)

            over_groups(act, group)

        @block.vector
        def _(dve):
            for t in (k_z, s_z, *hk, *hv):
                dve.memset(t[:, :, :], 0.0).then_inc(halves_zeroed, 1)
            dve.wait_ge(ctx_landed, 48)
            for k in range(KT):
                dve.tensor_copy(ctx2[:, k, :, :, :],
                                ctx_s[:, k, :].rearrange("p (b a k) -> p b a k", b=B, a=1).to_broadcast([P, B, 2, KL]))\
                   .then_inc(ctx_doubled, 1)
            dve.wait_ge(consts_step, CONSTS)
            dve.wait_ge(ctx_mm, 1)
            for k in range(KT):
                last = dve.tensor_copy(k_all[:, k, :], bank[k][:, :])
            last.then_inc(k_made, 1)
            for b in range(B):
                dve.wait_ge(ctx_mm, 2 + b)
                dve.tensor_tensor(
                    v_all[:, b, :, 0:2 * XD].rearrange("p j (i d) -> p j i d", i=2),
                    bank[2 + b % 6][:, 0:D].rearrange("p (j i d) -> p j i d", j=PAIRS, i=2),
                    pair_of[:, :].rearrange("p (a i b) -> p a i b", a=1, b=1).to_broadcast([P, PAIRS, 2, XD]),
                    ALU.mult).then_inc(v_made, 1)
                dve.tensor_copy(v_all[:, b, :, 2 * XD:VW],
                                pair_of[:, :].rearrange("p (a i) -> p a i", a=1).to_broadcast([P, PAIRS, 2]))\
                   .then_inc(v_made, 1)
            dve.wait_ge(w_landed, W_LOADS * 16)
            dve.tensor_copy(kp[:, :, :], kp_i[:, :].rearrange("p (b k) -> p b k", b=B)).then_inc(small_made, 1)
            dve.tensor_copy(qp[:, :], qp_i[:, :]).then_inc(small_made, 1)
            for k in range(KT):
                dve.tensor_scalar(wo_s[:, k, :], wo_raw[:, k, :], gn[:, 0:1], None, ALU.mult).then_inc(small_made, 1)

            def hold():
                dve.memset(idle_v[:, :], 0.0)

            def statistics(n, src, st, mv, var, step_s, vared_s, rstded_s):
                dve.bn_stats(st[:, :], src).then_inc(step_s, 1)
                dve.wait_ge(step_s, 2 * n + 1)
                hold()
                dve.bn_aggr(mv[:, :], st[:, :]).then_inc(step_s, 1)
                dve.wait_ge(step_s, 2 * n + 2)
                if later(n, 1):
                    dve.wait_ge(rstded_s, n)
                dve.tensor_scalar(var[:, :], mv[:, 1:2], EPS, None, ALU.add).then_inc(vared_s, 1)

            def norm(n, src, dst, mv, rstd, rstded_s, normed_s):
                dve.wait_ge(rstded_s, n + 1)
                dve.tensor_scalar(dst, src, mv[:, 0:1], rstd[:, 0:1], ALU.subtract, ALU.mult).then_inc(normed_s, 1)

            def wide(t, n):
                return t.rearrange("p (h a) -> p h a", a=1).to_broadcast([P, t.shape[1], n])

            def heads(t):
                return t.rearrange("p (h m) -> p h m", h=H)

            def two(t):
                return t.rearrange("p (k t) -> p k t", k=2)

            causal_h = causal[:, :].rearrange("p (a t) -> p a t", a=1).to_broadcast([P, H, P])

            def f_statistics(n, c, b):
                dve.wait_ge(x_landed[c], (n - c) * 4 + 16)
                statistics(n, xin[:, c, :], f_st, f_mv, f_var, f_stats, f_vared, f_rstded)

            def f_norm(n, c, b):
                if later(n, 1):
                    dve.wait_ge(f_cols_mm, n)
                norm(n, xin[:, c, :], f_xn[:, :], f_mv, f_rstd, f_rstded, f_normed)

            def log_gates(n, c, b):
                dve.wait_ge(fl_ok, n + 1)
                dve.wait_ge(v_ok, n + 1)
                if later(n, 1):
                    dve.wait_ge(gates_mm, n)
                if later(n, 2):
                    dve.wait_ge(less_ok, n - 1)
                dve.scalar_tensor_tensor(out=g_s[:, c % 2, :], in0=tile["vf"][:, D:2 * D], scalar=0.0, in1=f_l[:, :],
                                         op0=ALU.min, op1=ALU.subtract).then_inc(g_ok, 1)

            def queries_keys(n, c, b):
                dve.wait_ge(sig_ok, n + 1)
                if later(n, 2):
                    dve.wait_ge(logits_mm, n - 1)
                    dve.wait_ge(sums_mm, n - 1)
                dve.tensor_tensor(q_t[:, c % 2, :, :], two(tile["qk"][:, 0:D]), two(qk_s[:, 0:D]), ALU.mult)
                dve.tensor_tensor(k_s[:, c % 2, :], tile["qk"][:, D:2 * D], qk_s[:, D:2 * D], ALU.mult).then_inc(qk_ok, 1)

            def slot_values(n, c, b):
                dve.wait_ge(less_ok, n + 1)
                dve.wait_ge(down_ok, n + 1)
                if later(n, 2):
                    dve.wait_ge(sums_mm, n - 1)
                    dve.wait_ge(logits_mm, n - 1)
                dve.scalar_tensor_tensor(out=s_s[:, c % 2, :], in0=one_less[:, :], scalar=1.0, in1=down[:, :],
                                         op0=ALU.subtract, op1=ALU.mult, reverse0=True).then_inc(s_ok, 1)

            def start_states(n, c, b):
                if later(n, 1):
                    dve.wait_ge(z_ok, n)
                if later(n, 2):
                    dve.wait_ge(read_mm, n - 1)
                dve.wait_ge(decay_mm, n + 1)
                if c == 0:
                    dve.memset(hk[c % 2][:, :, :], 0.0)
                    dve.memset(hv[c % 2][:, :, :], 0.0).then_inc(h_ok, 1)
                else:
                    for i in range(2):
                        own = (slice(M * i, M * i + M), slice(0, 2), slice(M * i, M * i + M))
                        dve.tensor_tensor(hk[c % 2][own], zk[own], two(decay[:, :])[own], ALU.mult)
                        last = dve.tensor_tensor(
                            hv[c % 2][own], zv[own],
                            two(tile["decay_cols"][:, 0:D])[M * i:M * i + M, :, 0:1].to_broadcast([M, 2, M]), ALU.mult)
                    last.then_inc(h_ok, 1)

            def end_states(n, c, b):
                dve.wait_ge(sums_mm, n + 1)
                dve.wait_ge(h_ok, n + 1)
                dve.tensor_tensor(zk[:, :, :], two(tile["sums"][:, 0:D]), hk[c % 2][:, :, :], ALU.add)
                dve.tensor_tensor(zv[:, :, :], two(tile["sums"][:, D:2 * D]), hv[c % 2][:, :, :], ALU.add).then_inc(z_ok, 1)

            def causal_scores(n, c, b):
                if later(n, 1):
                    dve.wait_ge(logits_mm, n)
                dve.wait_ge(scores_mm, n + 1)
                dve.tensor_tensor(a_s[:, :, :], tile["scores"].rearrange("p (h t) -> p h t", h=H), causal_h, ALU.mult)\
                   .then_inc(a_ok, 1)

            def slot_logits(n, c, b):
                dve.wait_ge(logits_mm, n + 1)
                dve.wait_ge(gates_ok, n + 1)
                dve.tensor_tensor(lg[:, :, :], heads(tile["logits"][:, 0:D]), heads(up[:, c % 2, :]), ALU.mult).then_inc(lg_ok, 1)
                dve.wait_ge(lg_ok, n + 1)
                dve.tensor_reduce(lg_m[:, :], lg[:, :, :], AX.X, ALU.max).then_inc(lgm_ok, 1)
                dve.wait_ge(lgm_ok, n + 1)
                if later(n, 1):
                    dve.wait_ge(be_ok, n)
                dve.tensor_tensor(lg_d[:, :, :], lg[:, :, :], wide(lg_m[:, :], M), ALU.subtract).then_inc(lgd_ok, 1)

            def gate_probs(n, c, b):
                if later(n, 1):
                    dve.wait_ge(p_mm, n)
                dve.wait_ge(be_ok, n + 1)
                dve.tensor_tensor(b_p[:, :], b_e[:, :, :].rearrange("p h m -> p (h m)"), up[:, c % 2, :], ALU.mult)\
                    .then_inc(bp_ok, 1)

            def softmax_sum(n, c, b):
                dve.wait_ge(be_ok, n + 1)
                dve.tensor_reduce(b_sum[:, :], b_e[:, :, :], AX.X, ALU.add).then_inc(bsum_ok, 1)
                dve.wait_ge(bsum_ok, n + 1)
                dve.reciprocal(b_rec[:, :], b_sum[:, :]).then_inc(brec_ok, 1)

            def causal_mix(n, c, b):
                if later(n, 1):
                    dve.wait_ge(read_mm, n)
                dve.wait_ge(mix_mm, n + 1)
                dve.tensor_tensor(bt_s[:, :, :], tile["mix"].rearrange("p (h t) -> p h t", h=H), causal_h, ALU.mult)\
                   .then_inc(mix_ok, 1)

            def head_squares(n, c, b):
                dve.wait_ge(sq_ok, n + 1)
                dve.tensor_reduce(b_ss[:, :], b_sq[:, :, :], AX.X, ALU.add).then_inc(rms_step, 1)
                dve.wait_ge(rms_step, 3 * n + 1)
                dve.wait_ge(brec_ok, n + 1)
                dve.tensor_tensor(b_t1[:, :], b_ss[:, :], b_rec[:, :], ALU.mult).then_inc(rms_step, 1)

            def head_squares2(n, c, b):
                dve.wait_ge(rms_step, 3 * n + 2)
                dve.tensor_tensor(b_t2[:, :], b_t1[:, :], b_rec[:, :], ALU.mult).then_inc(rms_step, 1)
                dve.wait_ge(rms_step, 3 * n + 3)
                if later(n, 1):
                    dve.wait_ge(rms_ok, n)
                dve.tensor_scalar(b_ms[:, :], b_t2[:, :], 1.0 / M, EPS, ALU.mult, ALU.add).then_inc(ms_ok, 1)

            def head_weights(n, c, b):
                dve.wait_ge(rms_ok, n + 1)
                dve.tensor_tensor(b_w[:, :], b_rms[:, :], b_rec[:, :], ALU.mult).then_inc(bw_ok, 1)

            def head_outputs(n, c, b):
                dve.wait_ge(bw_ok, n + 1)
                if later(n, 1):
                    dve.wait_ge(o_mm, n)
                dve.tensor_tensor(b_o[:, :, :], heads(tile["read"][:, 0:D]), wide(b_w[:, :], M), ALU.mult)\
                   .then_inc(bo_ok, 1)

            def residual1(n, c, b):
                dve.wait_ge(y_mm, n + 1)
                dve.tensor_tensor(x1[:, c % 2, :], tile["y"][:, 0:D], xin[:, c, :], ALU.add).then_inc(x1_ok, 1)

            def x_statistics(n, c, b):
                dve.wait_ge(x1_ok, n + 1)
                statistics(n, x1[:, c % 2, :], x_st, x_mv, x_var, x_stats, x_vared, x_rstded)

            def x_norm(n, c, b):
                if later(n, 1):
                    dve.wait_ge(x_cols_mm, n)
                norm(n, x1[:, c % 2, :], x_xn[:, :], x_mv, x_rstd, x_rstded, x_normed)

            def hidden_keys(n, c, b):
                dve.wait_ge(mask_landed[c % 2], (n - c % 2) * 8 + 16)
                dve.tensor_scalar(hid[:, :], mask_i[:, c % 2, :], 0.0, -HIDDEN, ALU.is_equal, ALU.mult)\
                   .then_inc(hid_ok, 1)

            def distances(n, c, b):
                dve.wait_ge(hid_ok, n + 1)
                if later(n, 1):
                    dve.wait_ge(bias_ok, n)
                dve.scalar_tensor_tensor(
                    out=dist[:, :], in0=kp[:, bass.ds(b, 1), :].rearrange("p a k -> p (a k)"),
                    scalar=qp[:, bass.ds(n, 1)], in1=hid[:, :], op0=ALU.subtract, op1=ALU.add).then_inc(dist_ok, 1)

            def x_scores(n, c, b):
                dve.wait_ge(bias_ok, n + 1)
                dve.wait_ge(xs_mm, n + 1)
                if later(n, 1):
                    dve.wait_ge(ex_ok, n)
                for k in range(2):
                    last = dve.tensor_tensor(sc[:, 8 * k:8 * k + 8, :],
                                             tile[f"x_scores{k}"].rearrange("p (h k) -> p h k", h=HPT),
                                             bias[:, 8 * k:8 * k + 8, :], ALU.add)
                last.then_inc(sc_ok, 1)

            def x_maximum(n, c, b):
                dve.wait_ge(sc_ok, n + 1)
                if later(n, 1):
                    dve.wait_ge(scd_ok, n)
                dve.tensor_reduce(sc_m[:, :], sc[:, :, :], AX.X, ALU.max).then_inc(scm_ok, 1)

            def x_denominators(n, c, b):
                dve.wait_ge(av_mm, n + 1)
                dve.tensor_scalar(x_den[:, :].rearrange("p (j i) -> p j i", i=2),
                                  tile["values"][:, 0:PAIRS * VW].rearrange("p (j n) -> p j n", n=VW)[:, :, 2 * XD:VW],
                                  1.0, None, ALU.add).then_inc(xden_ok, 1)
                dve.wait_ge(xden_ok, n + 1)
                dve.reciprocal(x_rec[:, :], x_den[:, :]).then_inc(xrec_ok, 1)

            def x_outputs(n, c, b):
                dve.wait_ge(xrec_ok, n + 1)
                if later(n, 1):
                    dve.wait_ge(xot_mm, n)
                dve.tensor_tensor(
                    x_o[:, :, :].rearrange("p j (i d) -> p j i d", i=2),
                    tile["values"][:, 0:PAIRS * VW].rearrange("p (j n) -> p j n", n=VW)[:, :, 0:2 * XD]
                    .rearrange("p j (i d) -> p j i d", i=2),
                    x_rec[:, :].rearrange("p (j i a) -> p j i a", i=2, a=1).to_broadcast([P, PAIRS, 2, XD]),
                    ALU.mult).then_inc(xo_ok, 1)

            def residual2(n, c, b):
                dve.wait_ge(xy_mm, n + 1)
                if later(n, 2):
                    dve.wait_ge(x2_stored[c % 2], (n - c % 2) * 8)
                dve.tensor_tensor(x2[:, c % 2, :], tile["xy"][:, 0:D], x1[:, c % 2, :], ALU.add).then_inc(x2_ok, 1)

            def r_statistics(n, c, b):
                dve.wait_ge(x2_ok, n + 1)
                statistics(n, x2[:, c % 2, :], r_st, r_mv, r_var, r_stats, r_vared, r_rstded)

            def sent_before(n, c):
                if later(n, 2):
                    for k in range(2):
                        dve.wait_ge(sent[2 * (c % 2) + k], (n - c % 2) * 8)

            def r_norm(n, c, b):
                sent_before(n, c)
                if later(n, 2):
                    dve.wait_ge(r_cols_mm, n - 1)
                norm(n, x2[:, c % 2, :].rearrange("p (a d) -> p a d", a=1).to_broadcast([P, 2, D]),
                     r_xn[:, c % 2, :, 0:D], r_mv, r_rstd, r_rstded, r_normed)
                dve.tensor_copy(r_xn[:, c % 2, :, D:D + 1],
                                token_no[:, bass.ds(n, 1)].rearrange("p (a b) -> p a b", b=1).to_broadcast([P, 2, 1]))

            def top_two(n, c, b):
                dve.wait_ge(rlg_mm, n + 1)
                dve.tensor_scalar(r_lg[:, :], tile["r_logits"][:, 0:E], -CLAMP, CLAMP, ALU.max, ALU.min)\
                   .then_inc(rlg_ok, 1)
                dve.wait_ge(rlg_ok, n + 1)
                hold()
                dve.max(top[:, :], r_lg[:, :]).then_inc(route_step, 1)
                dve.wait_ge(route_step, n * ROUTE_STEPS + 1)
                if later(n, 1):
                    dve.wait_ge(re_ok, n)
                dve.tensor_scalar(gap[:, :], top[:, 1:2], top[:, 0:1], None, ALU.subtract).then_inc(gap_ok, 1)
                dve.max_index(top_i[:, :], top[:, :], r_lg[:, :]).then_inc(topi_ok, 1)
                dve.wait_ge(topi_ok, n + 1)
                dve.tensor_copy(top_f[:, :], top_i[:, 0:2]).then_inc(route_step, 1)
                dve.wait_ge(route_step, n * ROUTE_STEPS + 2)
                for k in range(2):
                    dve.tensor_scalar(hot[:, k, :], expert_no[:, :], top_f[:, k:k + 1], None, ALU.is_equal)\
                       .then_inc(route_step, 1)
                dve.wait_ge(route_step, n * ROUTE_STEPS + 4)
                if later(n, 1):
                    dve.wait_ge(cnt_mm, n)
                dve.tensor_tensor(both[:, :], hot[:, 0, :], hot[:, 1, :], ALU.add).then_inc(both_ok, 1)

            def places(n, c, b):
                dve.wait_ge(cnt_mm, n + 1)
                if later(n, 1):
                    dve.wait_ge(taken_ok, n)
                dve.tensor_tensor(place[:, :], tile["counts"][:, 0:E], taken[:, :], ALU.add).then_inc(place_ok, 1)
                dve.wait_ge(place_ok, n + 1)
                dve.tensor_tensor(taken[:, :], tile["counts"][:, E:2 * E], taken[:, :], ALU.add).then_inc(taken_ok, 1)
                dve.tensor_tensor(place_h[:, :, :], hot[:, :, :],
                                  place[:, :].rearrange("p (a e) -> p a e", a=1).to_broadcast([P, 2, E]),
                                  ALU.mult).then_inc(route_step, 1)
                dve.tensor_scalar(base[:, :], top_f[:, :], float(CAP), None, ALU.mult).then_inc(route_step, 1)
                dve.wait_ge(re_ok, n + 1)
                dve.tensor_scalar(r_den[:, :], r_e[:, :], 1.0, 1e-12, ALU.add, ALU.add).then_inc(route_step, 1)
                dve.wait_ge(route_step, n * ROUTE_STEPS + 5)
                dve.tensor_reduce(pos[:, :], place_h[:, :, :], AX.X, ALU.add).then_inc(route_step, 1)
                dve.wait_ge(route_step, n * ROUTE_STEPS + 7)
                dve.reciprocal(r_p[:, :], r_den[:, :]).then_inc(route_step, 1)
                dve.wait_ge(route_step, n * ROUTE_STEPS + 8)
                dve.tensor_scalar(off_f[:, :], pos[:, :], float(CAP), SKIPPED, ALU.is_ge, ALU.mult)\
                   .then_inc(route_step, 1)
                dve.tensor_tensor(slot_f[:, :], pos[:, :], base[:, :], ALU.add).then_inc(route_step, 1)
                dve.wait_ge(route_step, n * ROUTE_STEPS + 9)
                dve.tensor_copy(r_xn[:, c % 2, 0, D + 1:ROW], r_p[:, :])
                dve.tensor_tensor(r_xn[:, c % 2, 1, D + 1:ROW], r_p[:, :], r_e[:, :], ALU.mult)
                dve.wait_ge(route_step, n * ROUTE_STEPS + ROUTE_STEPS)
                dve.tensor_tensor(send[:, c % 2, :], slot_f[:, :], off_f[:, :], ALU.add).then_inc(slots_ok, 1)

            def step(run):
                run(0, f_statistics)
                run(0, f_norm)
                run(1, end_states)
                run(1, head_squares)
                run(1, head_squares2)
                run(2, x_scores)
                run(1, head_weights)
                run(1, head_outputs)
                run(2, x_maximum)
                run(4, top_two)
                run(0, log_gates)
                run(4, places)
                run(0, queries_keys)
                run(0, slot_values)
                run(3, residual2)
                run(0, start_states)
                run(3, r_statistics)
                run(1, residual1)
                run(1, hidden_keys)
                run(1, x_statistics)
                run(0, causal_scores)
                run(1, distances)
                run(1, x_norm)
                run(3, r_norm)
                run(0, slot_logits)
                run(0, gate_probs)
                run(0, softmax_sum)
                run(2, x_denominators)
                run(2, x_outputs)
                run(0, causal_mix)

            over_chunks(dve, step)

            def split_weights(e, par, piece):
                m, i = piece // 2, piece % 2
                dve.wait_ge(w_hi_ok, e * PIECES + piece + 1)
                hi, lo = w_s[par][m]
                dve.tensor_tensor(lo[:, i, :], raw[m][:, i, :], hi[:, i, :], ALU.subtract).then_inc(w_lo_ok, 1)

            def columns(g, par):
                dve.wait_ge(xe_hi_ok, g + 1)
                if later(g, 2):
                    dve.wait_ge(up_mm, (g - 1) * FT)
                hi, lo = (t[:, par, :, :].rearrange("p k t -> p (k t)") for t in xe_t)
                dve.tensor_tensor(lo, bank[0][:, :], hi, ALU.subtract).then_inc(xet_ok, 1)

            def gated(g, par, f):
                n = g * FT + f
                dve.wait_ge(silu_ok, n + 1)
                if later(n, 2):
                    dve.wait_ge(h_lo_ok, n - 1)
                dve.tensor_tensor(h_f[:, f % 2, :], bank[2 + f % 4][:, GS:2 * GS], h_a[:, f % 2, :], ALU.mult)\
                   .then_inc(gated_ok, 1)

            def hidden_low(g, par, f):
                dve.wait_ge(h_hi_ok, g * FT + f + 1)
                if f == 0 and later(g, 2):
                    dve.wait_ge(dn_mm, g - 1)
                dve.tensor_tensor(h_t[1][:, par, f, :], h_f[:, f % 2, :], h_t[0][:, par, f, :], ALU.subtract)\
                   .then_inc(h_lo_ok, 1)

            def results(g, par):
                dve.wait_ge(dn_mm, g + 1)
                if later(g, 2):
                    dve.wait_ge(added, (g - 1) * 32)
                dve.wait_ge(about_ok, g + 1)
                for a in range(2):
                    dve.tensor_copy(token[par][a][:, :], about[:, par, a, 0:1])
                for a in range(2):
                    last = dve.tensor_scalar(y_s[:, par, a, :], bank[6 + par][:, a * D:(a + 1) * D],
                                             about[:, par, a, 1:2], None, ALU.mult)
                last.then_inc(y_ok, 1)

            def read_about(g, par):
                if later(g, 2):
                    dve.wait_ge(y_ok, g - 1)
                dve.wait_ge(xe_landed[par], (g - par) * 8 + 16)
                dve.tensor_copy(about[:, par, :, :], xe[:, par, :, D:ROW]).then_inc(about_ok, 1)

            for piece in range(PIECES):
                split_weights(0, 0, piece)
            columns(0, 0)
            for g in range(2):
                read_about(g, g)

            def group(d, j):
                g, par = d * GPL + j, j % 2
                for f in range(FT):
                    gated(g, par, f)
                    if f:
                        hidden_low(g, par, f - 1)
                    if f == 2 and not is_last(g, NG - 1):
                        columns(g + 1, 1 - par)
                    if splits(d, j, f):
                        e, piece = splits(d, j, f)
                        split_weights(e, 1 - j // GPE, piece)
                hidden_low(g, par, FT - 1)
                if later(g, 1):
                    results(g - 1, 1 - par)
                    if not is_last(g, NG - 1):
                        read_about(g + 1, 1 - par)

            over_groups(dve, group)
            results(NG - 1, 1)

        @block.tensor
        def _(pe):
            def flip(dst, tiles, done):
                for i, t in enumerate(tiles):
                    last = pe.transpose(dst[:, i * P:(i + 1) * P], t, ident[:, :])
                last.then_inc(done, 1)

            def product(dst, pairs):
                for i, (lhs, rhs) in enumerate(pairs):
                    last = pe.matmul(dst, lhs, rhs, start=(i == 0), stop=(i == len(pairs) - 1))
                return last

            def halves(t):
                return [t[:, k * P:(k + 1) * P] for k in range(2)]

            pe.wait_ge(ctx_landed, 48)
            for m in range(KT):
                last = product(bank[m][:, :], [(xw[:, 1, k, m * P:(m + 1) * P], ctx_s[:, k, :]) for k in range(KT)])
            last.then_inc(ctx_mm, 1)
            pe.wait_ge(ctx_doubled, KT)
            for b in range(B):
                if b >= 6:
                    pe.wait_ge(v_made, 2 * (b - 5))
                product(bank[2 + b % 6][:, 0:D], [
                    (ctx2[:, k, b, :, :].rearrange("p a k -> p (a k)"), xw[:, 2, k, :]) for k in range(KT)]).then_inc(ctx_mm, 1)
            pe.wait_ge(consts_step, CONSTS)
            pe.wait_ge(w_landed, W_LOADS * 16)
            pe.wait_ge(small_made, 4)
            pe.wait_ge(k_made, 1)
            pe.wait_ge(v_made, 2 * B)

            def f_columns(n, c, b):
                pe.wait_ge(f_normed, n + 1)
                bank_left(pe, "f_cols", n)
                flip(tile["f_cols"], halves(f_xn), f_cols_mm)

            def project_vf(n, c, b):
                pe.wait_ge(f_cols_ok, n + 1)
                bank_left(pe, "vf", n)
                product(tile["vf"], [(f_xnt[:, k, :], w_in[:, k, 2 * D:4 * D]) for k in range(KT)]).then_inc(vf_mm, 1)

            def project_qk(n, c, b):
                bank_left(pe, "qk", n)
                for m in range(2):
                    product(tile["qk"][:, m * P:(m + 1) * P],
                            [(w_in[:, k, m * P:(m + 1) * P], f_xnt[:, k, :]) for k in range(KT)])
                product(tile["qk"][:, D:2 * D], [(f_xnt[:, k, :], w_in[:, k, D:2 * D]) for k in range(KT)])\
                    .then_inc(qk_mm, 1)

            def sum_gates(n, c, b):
                pe.wait_ge(g_ok, n + 1)
                bank_left(pe, "gates", n)
                product(tile["gates"][:, 0:D], [(tri_half[:, :], g_s[:, c % 2, :])])
                now_last = [c % 2] if c == 0 else [c % 2, 1 - c % 2]
                product(tile["gates"][:, D:2 * D], [(half[:, :], g_s[:, i, :]) for i in now_last]).then_inc(gates_mm, 1)

            def decay_columns(n, c, b):
                pe.wait_ge(decay_ok, n + 1)
                bank_left(pe, "decay_cols", n)
                flip(tile["decay_cols"], halves(decay), decay_mm)

            def ks_columns(n, c, b):
                pe.wait_ge(s_ok, n + 1)
                pe.wait_ge(qk_ok, n + 1)
                bank_left(pe, "ks_cols", n)
                flip(tile["ks_cols"], halves(k_s[:, c % 2, :]) + halves(s_s[:, c % 2, :]), ks_mm)

            def sum_states(n, c, b):
                pe.wait_ge(v_ok, n + 1)
                bank_left(pe, "sums", n)
                for m in range(2):
                    cols = slice(m * P, (m + 1) * P)
                    product(tile["sums"][:, cols], [(k_s[:, c % 2, cols], s_s[:, c % 2, cols])])
                    last = product(tile["sums"][:, D + m * P:D + (m + 1) * P], [(s_s[:, c % 2, cols], v_s[:, c % 2, cols])])
                last.then_inc(sums_mm, 1)

            def scores(n, c, b):
                pe.wait_ge(kz_ok, n + 1)
                bank_left(pe, "scores", n)
                for h in range(H):
                    last = product(tile["scores"][:, h * P:(h + 1) * P], [(k_z[:, h, :], q_t[:, c % 2, h // 2, :])])
                last.then_inc(scores_mm, 1)

            def with_states(dst, queries, states, weights, rows, weights_ok, n):
                for m in range(PAIRS1):
                    pe.matmul(dst[:, m * P:(m + 1) * P], queries[:, m, :], states[:, m, :], start=True, stop=False)
                    if m == 0:
                        pe.wait_ge(weights_ok, n + 1)
                    for h in (2 * m, 2 * m + 1):
                        cols = slice(h * M, (h + 1) * M)
                        last = pe.matmul(dst[:, cols], weights[:, h, :], rows[:, cols], start=False, stop=(h % 2 == 1))
                return last

            def logits(n, c, b):
                pe.wait_ge(h_ok, n + 1)
                bank_left(pe, "logits", n)
                last = with_states(tile["logits"], q_t[:, c % 2, :, :], hk[c % 2], a_s, s_s[:, c % 2, :], a_ok, n)
                last.then_inc(logits_mm, 1)

            def p_columns(n, c, b):
                pe.wait_ge(bp_ok, n + 1)
                bank_left(pe, "p_cols", n)
                flip(tile["p_cols"], halves(b_p), p_mm)

            def mix(n, c, b):
                pe.wait_ge(p_ok, n + 1)
                bank_left(pe, "mix", n)
                for h in range(H):
                    last = product(tile["mix"][:, h * P:(h + 1) * P], [(s_z[:, h, :], p_t[:, h // 2, :])])
                last.then_inc(mix_mm, 1)

            def read_out(n, c, b):
                pe.wait_ge(p_ok, n + 1)
                bank_left(pe, "read", n)
                last = with_states(tile["read"], p_t, hv[c % 2], bt_s, v_s[:, c % 2, :], mix_ok, n)
                last.then_inc(read_mm, 1)

            def o_columns(n, c, b):
                pe.wait_ge(bo_ok, n + 1)
                bank_left(pe, "o_cols", n)
                flip(tile["o_cols"], halves(b_o[:, :, :].rearrange("p h m -> p (h m)")), o_mm)

            def project_o(n, c, b):
                pe.wait_ge(o_ok, n + 1)
                bank_left(pe, "y", n)
                product(tile["y"][:, 0:D], [(o_t[:, k, :], wo_s[:, k, :]) for k in range(2)]).then_inc(y_mm, 1)

            def x_columns(n, c, b):
                pe.wait_ge(x_normed, n + 1)
                bank_left(pe, "x_cols", n)
                flip(tile["x_cols"], halves(x_xn), x_cols_mm)

            def x_queries(n, c, b):
                pe.wait_ge(x_cols_ok, n + 1)
                bank_left(pe, "xq", n)
                for m in range(2):
                    last = product(tile["xq"][:, m * P:(m + 1) * P],
                                   [(xw[:, 0, k, m * P:(m + 1) * P], x_xnt[:, k, :]) for k in range(KT)])
                last.then_inc(xq_mm, 1)

            def x_scores(n, c, b):
                pe.wait_ge(xq_ok, n + 1)
                pe.wait_ge(kbd_ok, b * KT + KT)
                for k in range(KT):
                    bank_left(pe, f"x_scores{k}", n)
                    last = product(tile[f"x_scores{k}"], [(xq_t[:, k, :], k_bd[:, k, :, :].rearrange("p h k -> p (h k)"))])
                last.then_inc(xs_mm, 1)

            def e_columns(n, c, b):
                pe.wait_ge(ex_ok, n + 1)
                for k in range(2):
                    bank_left(pe, f"e_cols{k}", n)
                    for j in range(4):
                        pair = ex[:, 8 * k + 2 * j:8 * k + 2 * j + 2, :].rearrange("p h k -> p (h k)")
                        last = pe.transpose(tile[f"e_cols{k}"][:, j * P:(j + 1) * P], pair, ident[:, :])
                last.then_inc(et_mm, 1)

            def values(n, c, b):
                pe.wait_ge(et_ok, n + 1)
                pe.wait_ge(vbd_ok, b + 1)
                bank_left(pe, "values", n)
                for j in range(PAIRS):
                    last = product(tile["values"][:, j * VW:(j + 1) * VW], [(e_t[:, j, :], v_bd[:, j, :])])
                last.then_inc(av_mm, 1)

            def xo_columns(n, c, b):
                pe.wait_ge(xo_ok, n + 1)
                bank_left(pe, "xo_cols", n)
                flip(tile["xo_cols"], halves(x_o[:, :, :].rearrange("p j n -> p (j n)")), xot_mm)

            def x_project_o(n, c, b):
                pe.wait_ge(xot_ok, n + 1)
                bank_left(pe, "xy", n)
                product(tile["xy"][:, 0:D], [(xo_t[:, k, :], xw[:, 3, k, :]) for k in range(KT)]).then_inc(xy_mm, 1)

            def r_columns(n, c, b):
                pe.wait_ge(r_normed, n + 1)
                bank_left(pe, "r_cols", n)
                flip(tile["r_cols"], halves(r_xn[:, c % 2, 0, :]), r_cols_mm)

            def r_logits(n, c, b):
                pe.wait_ge(r_cols_ok, n + 1)
                bank_left(pe, "r_logits", n)
                product(tile["r_logits"][:, 0:E], [(r_xnt[:, k, :], wr_s[:, k, :]) for k in range(KT)]).then_inc(rlg_mm, 1)

            def counts(n, c, b):
                pe.wait_ge(both_ok, n + 1)
                bank_left(pe, "counts", n)
                product(tile["counts"][:, 0:E], [(before[:, :], both[:, :])])
                product(tile["counts"][:, E:2 * E], [(all_b[:, :], both[:, :])]).then_inc(cnt_mm, 1)

            def step(run):
                run(2, x_scores)
                run(0, f_columns)
                run(4, r_logits)
                run(3, xo_columns)
                run(0, project_vf)
                run(0, project_qk)
                run(1, o_columns)
                run(4, counts)
                run(0, sum_gates)
                run(3, x_project_o)
                run(0, decay_columns)
                run(0, ks_columns)
                run(1, project_o)
                run(0, scores)
                run(2, e_columns)
                run(0, logits)
                run(1, x_columns)
                run(2, values)
                run(3, r_columns)
                run(0, p_columns)
                run(1, x_queries)
                run(0, mix)
                run(0, sum_states)
                run(0, read_out)

            over_chunks(pe, step)

            def columns(g, par):
                pe.wait_ge(xe_landed[par], (g - par) * 8 + 16)
                if later(g, 1):
                    pe.wait_ge(xet_ok, g)
                flip(bank[0], [xe[:, par, a, k * P:(k + 1) * P] for k in range(KT) for a in range(2)], xet_mm)

            def split_product(dst, pairs):
                return product(dst, [(lhs[i], rhs[k]) for lhs, rhs in pairs for i, k in ((0, 0), (0, 1), (1, 0))])

            def hidden(g, j):
                par, w = j % 2, w_s[j // GPE]
                pe.wait_ge(xet_ok, g + 1)
                for f in range(FT):
                    n = g * FT + f
                    if later(n, 4):
                        pe.wait_ge(gated_ok, n - 3)
                    to = bank[2 + f % 4]
                    for m in range(2):
                        last = split_product(to[:, m * GS:(m + 1) * GS], [
                            ([w[m][part][:, k, f * P:(f + 1) * P] for part in range(2)],
                             [xe_t[part][:, par, k, :] for part in range(2)]) for k in range(KT)])
                    last.then_inc(up_mm, 1)

            def results(d, j):
                g, par, w = d * GPL + j, j % 2, w_s[(j // GPE) % 2][2]
                pe.wait_ge(h_lo_ok, g * FT + FT)
                if j % GPE == 0:
                    pe.wait_ge(w_lo_ok, (2 * d + j // GPE + 1) * PIECES)
                if later(g, 2):
                    pe.wait_ge(y_ok, g - 1)
                for a in range(2):
                    last = split_product(bank[6 + par][:, a * D:(a + 1) * D], [
                        ([h_t[part][:, par, f, a * P:(a + 1) * P] for part in range(2)],
                         [w[part][:, f // 4, (f % 4) * D:(f % 4 + 1) * D] for part in range(2)]) for f in range(FT)])
                last.then_inc(dn_mm, 1)

            def group(d, j):
                g = d * GPL + j
                if not is_last(g, NG - 1):
                    columns(g + 1, 1 - j % 2)
                if j % GPE == 0:
                    pe.wait_ge(w_lo_ok, (2 * d + j // GPE) * PIECES + 4)
                hidden(g, j)
                if later(g, 1):
                    results(d, j - 1)

            columns(0, 0)
            over_groups(pe, group)
            results(E // 2 - 1, GPL - 1)


def kernel(x, ctx_1024, itok_BxS_8_8191, itok_BxS2_1_8191, mask_BxSxS2_if1, L0_attn_Wq, L0_attn_Wk, L0_attn_Wv,
           L0_attn_Wf, L0_attn_g_norm_w, L0_attn_Wo, L0_xattn_W_q, L0_xattn_W_k, L0_xattn_W_v, L0_xattn_W_o,
           L0_ffn_Wr, L0_ffn_W1, L0_ffn_W3, L0_ffn_W2):
    import concourse.bacc as bacc
    from concourse.bass_utils import run_bass_kernel_spmd

    laid_out = {
        "x": x, "qpos": itok_BxS_8_8191.reshape(NCH, P).T, "kpos": itok_BxS2_1_8191, "mask": mask_BxSxS2_if1,
        "ctx_t": ctx_1024.reshape(B * KL, D).T, "wq": L0_attn_Wq, "wk": L0_attn_Wk, "wv": L0_attn_Wv,
        "wf": L0_attn_Wf, "gnorm": L0_attn_g_norm_w, "wo": L0_attn_Wo, "xwq_t": L0_xattn_W_q.T,
        "xwk_t": L0_xattn_W_k.T, "xwv_t": L0_xattn_W_v.T, "xwo_t": L0_xattn_W_o.T, "wr": L0_ffn_Wr,
        "w1": L0_ffn_W1, "w3": L0_ffn_W3, "w2": L0_ffn_W2,
    }
    nc = bacc.Bacc("TRN2", target_bir_lowering=False, num_devices=1)
    arrays, args = {}, []
    for name, a in laid_out.items():
        a = np.ascontiguousarray(a)
        arrays[f"in_{name}"] = a
        args.append(nc.dram_tensor(f"in_{name}", a.shape, mybir.dt.from_np(a.dtype), kind="ExternalInput").ap())
    args.append(nc.dram_tensor("out_dram", (B * T + P, D), F32, kind="ExternalOutput").ap())
    decoder_layer(nc, *args)
    return run_bass_kernel_spmd(nc, [arrays], core_ids=[0]).results[0]["out_dram"][:B * T].reshape(B, T, D)
```
